# Optimizing a Trainium2 kernel written in Bass

```python
import numpy as np
import jax
import jax.numpy as jnp

def _softmax(x, axis=-1):
    return jax.nn.softmax(x, axis=axis)

def _gelu(x):
    return jax.nn.gelu(x, approximate=True)

def _silu(x):
    return jax.nn.silu(x)

def _sigmoid(x):
    return jax.nn.sigmoid(x)

def _layernorm(x, axis=-1, eps=1e-05):
    m = jnp.mean(x, axis=axis, keepdims=True)
    v = jnp.var(x, axis=axis, keepdims=True)
    return (x - m) / jnp.sqrt(v + eps)

def _scatter_add(tgt, idx, src, axis=0):
    return tgt.at[idx].add(src)

def _segment_sum(src, seg, n):
    return jax.ops.segment_sum(src, seg, n)
kernel_name = 'mk_gnn_resnorm_d4_gnn_r32_713761'

def setup_inputs(seed: int=0):
    np.random.seed(seed)
    _w = jnp.asarray

    def _rec_inputs():
        import jax
        import jax.numpy as jnp
        _gk = jax.random.key(seed)
        x = -0.0005121 + 1.001 * jax.random.normal(jax.random.fold_in(_gk, 1), (3125, 160), jnp.float32)
        _s = jax.random.randint(jax.random.fold_in(_gk, 2), (50000,), 0, 3125, jnp.int32)
        _d = jax.random.randint(jax.random.fold_in(_gk, 3), (50000,), 0, 3125, jnp.int32)
        _loop = jnp.arange(3125, dtype=jnp.int32)
        src = jnp.concatenate([_s, _d, _loop])
        dst = jnp.concatenate([_d, _s, _loop])
        _o = jnp.argsort(dst, stable=True)
        src = src[_o]
        dst = dst[_o]
        edge_attr_10 = jax.random.uniform(jax.random.fold_in(_gk, 12), (103125, 10), jnp.float32, 0.0, 1)
        edge_attr_16 = -0.000191324 + 0.999809 * jax.random.normal(jax.random.fold_in(_gk, 13), (103125, 16), jnp.float32)
        edge_attr_4 = 0.000126197 + 0.999763 * jax.random.normal(jax.random.fold_in(_gk, 14), (103125, 4), jnp.float32)
        edge_attr_8 = 0.000398945 + 1.00003 * jax.random.normal(jax.random.fold_in(_gk, 15), (103125, 8), jnp.float32)
        node_vec1 = jax.random.uniform(jax.random.fold_in(_gk, 17), (3125, 1), jnp.float32, 0.0, 1)
        return (x, src, dst, edge_attr_10, edge_attr_16, edge_attr_4, edge_attr_8, node_vec1)
    x, src, dst, edge_attr_10, edge_attr_16, edge_attr_4, edge_attr_8, node_vec1 = _rec_inputs()

    def _L0_gnn_setup():
        import jax, jax.numpy as jnp
        import numpy as np
        N = 625
        E = 10000
        MUL0 = 64
        MUL1 = 32
        FC_IN = 16
        FC_H = 64
        WNUM = 192
        key = jax.random.key(seed)
        ks = jax.random.split(key, 16)
        return {'x': jax.random.normal(ks[0], (N, MUL0 + 3 * MUL1), jnp.float32), 'node_attr': jnp.ones((N, 1), jnp.float32), 'edge_scalars': jax.random.normal(ks[1], (E, FC_IN), jnp.float32), 'edge_attr_sh': jax.random.normal(ks[2], (E, 4), jnp.float32), 'edge_src': jax.random.randint(ks[3], (E,), 0, N), 'edge_dst': jax.random.randint(ks[4], (E,), 0, N), 'Wfc1': jax.random.normal(ks[5], (FC_IN, FC_H), jnp.float32), 'Wfc2': jax.random.normal(ks[6], (FC_H, WNUM), jnp.float32), 'Wsc0': jax.random.normal(ks[7], (MUL0, MUL0), jnp.float32), 'Wsc1': jax.random.normal(ks[8], (MUL1, MUL1), jnp.float32), 'Wl1_0': jax.random.normal(ks[9], (MUL0, MUL0), jnp.float32), 'Wl1_1': jax.random.normal(ks[10], (MUL1, MUL1), jnp.float32), 'Wl2_s': jax.random.normal(ks[11], (MUL0 + MUL1, MUL0), jnp.float32), 'Wl2_v': jax.random.normal(ks[12], (MUL0 + MUL1, MUL1), jnp.float32), 'Wa': 0.1 * jax.random.normal(ks[13], (MUL0 + MUL1, 1), jnp.float32)}
    _L0_gnn_all = _L0_gnn_setup()
    _L0_gnn_in = {k: v for k, v in _L0_gnn_all.items() if k in ('Wfc1', 'Wfc2', 'Wsc0', 'Wsc1', 'Wl1_0', 'Wl1_1', 'Wl2_s', 'Wl2_v', 'Wa')}
    del _L0_gnn_all

    def _L1_gnn_setup():
        import jax, jax.numpy as jnp
        import numpy as np
        N = 625
        E = 20000
        INV_SQRT3 = 0.5773502691896258
        INV8 = 0.125
        INV_SQRT32 = 0.17677669529663687
        INV64 = 0.015625
        INV32 = 0.03125
        INV_SQRT2048 = 0.022097086912079608
        key = jax.random.key(seed)
        ks = jax.random.split(key, 16)
        f32 = jnp.float32
        return {'node_features': jax.random.normal(ks[0], (N, 160), f32), 'edge_index': jax.random.randint(ks[1], (2, E), 0, N), 'edge_attr_tensor': jax.random.normal(ks[2], (E, 4), f32), 'node_attr_scalar_raw': jax.random.normal(ks[3], (N, 1), f32), 'Wm_ss': jax.random.normal(ks[4], (64, 64), f32), 'Wm_vv': jax.random.normal(ks[5], (32, 64), f32), 'Wm_sv': jax.random.normal(ks[6], (64, 32), f32), 'Wm_vs': jax.random.normal(ks[7], (32, 32), f32), 'Lm_s': jax.random.normal(ks[8], (64, 64), f32), 'Lm_v': jax.random.normal(ks[9], (32, 32), f32), 'Wu_ss': jax.random.normal(ks[10], (64, 64, 64), f32), 'Wu_vv': jax.random.normal(ks[11], (32, 32, 64), f32), 'Wu_sv': jax.random.normal(ks[12], (64, 32, 32), f32), 'Wu_vs': jax.random.normal(ks[13], (32, 64, 32), f32), 'Lu_s': jax.random.normal(ks[14], (64, 64), f32), 'Lu_v': jax.random.normal(ks[15], (32, 32), f32)}
    _L1_gnn_all = _L1_gnn_setup()
    _L1_gnn_in = {k: v for k, v in _L1_gnn_all.items() if k in ('Wm_ss', 'Wm_vv', 'Wm_sv', 'Wm_vs', 'Lm_s', 'Lm_v', 'Wu_ss', 'Wu_vv', 'Wu_sv', 'Wu_vs', 'Lu_s', 'Lu_v')}
    del _L1_gnn_all

    def _L2_gnn_setup():
        import jax, jax.numpy as jnp
        import numpy as np
        INV3 = 1.0 / np.sqrt(3.0)

        def _fctp(x_s, x_v, attr, w0, w1):
            s = x_s @ w0 * (1.0 / np.sqrt(x_s.shape[-1])) * attr
            v = jnp.einsum('nud,uw->nwd', x_v, w1) * (1.0 / np.sqrt(x_v.shape[-2])) * attr[..., None]
            return (s, v)
        key = jax.random.key(seed)
        ks = jax.random.split(key, 16)
        N, E = (50000, 25000)
        inp = {'node_input': jax.random.normal(ks[0], (N, 160), jnp.float32), 'node_attr': jnp.ones((N, 1), jnp.float32), 'edge_attr': jax.random.normal(ks[1], (E, 4), jnp.float32), 'edge_scalars': jax.random.normal(ks[2], (E, 8), jnp.float32), 'sc_w0': jax.random.normal(ks[3], (64, 64), jnp.float32), 'sc_w1': jax.random.normal(ks[4], (32, 32), jnp.float32), 'lin1_w0': jax.random.normal(ks[5], (64, 64), jnp.float32), 'lin1_w1': jax.random.normal(ks[6], (32, 32), jnp.float32), 'fc_w1': jax.random.normal(ks[7], (8, 64), jnp.float32), 'fc_w2': jax.random.normal(ks[8], (64, 192), jnp.float32), 'lin2_w0': jax.random.normal(ks[9], (96, 64), jnp.float32), 'lin2_w1': jax.random.normal(ks[10], (96, 32), jnp.float32), 'lin3_w': jax.random.normal(ks[11], (96, 1), jnp.float32), 'edge_src': jax.random.randint(ks[12], (E,), 0, N), 'edge_dst': jax.random.randint(ks[13], (E,), 0, N), 'num_neighbors': 16}
        return inp
    _L2_gnn_all = _L2_gnn_setup()
    _L2_gnn_in = {k: v for k, v in _L2_gnn_all.items() if k in ('sc_w0', 'sc_w1', 'lin1_w0', 'lin1_w1', 'fc_w1', 'fc_w2', 'lin2_w0', 'lin2_w1', 'lin3_w')}
    del _L2_gnn_all

    def _L3_gnn_setup():
        import jax, jax.numpy as jnp
        import numpy as np
        N_NODES = 50000
        N_EDGES = 25000
        MUL0, MUL1 = (64, 32)
        N_BASIS, N_RADIAL = (10, 100)
        W_NUMEL = 192
        NUM_NEIGHBORS = 16.0
        INV_SQRT3 = np.float32(1.0 / np.sqrt(3.0))
        RELU_GAIN = np.float32(np.sqrt(2.0))
        FAN_L2 = np.float32(np.sqrt(MUL0 + MUL1))

        def _fctp_scalar_attr(x0, x1, a, W0, W1):
            o0 = x0 @ W0 * a * (1.0 / np.sqrt(W0.shape[0]))
            o1 = jnp.einsum('nud,uw->nwd', x1, W1) * a[..., None] * (1.0 / np.sqrt(W1.shape[0]))
            return (o0, o1)
        key = jax.random.key(seed)
        ks = jax.random.split(key, 16)
        return {'node_input': jax.random.normal(ks[0], (N_NODES, MUL0 + 3 * MUL1), jnp.float32), 'node_attr': jnp.ones((N_NODES, 1), jnp.float32), 'edge_attr': jax.random.normal(ks[1], (N_EDGES, 4), jnp.float32), 'edge_length_embedded': jax.random.uniform(ks[2], (N_EDGES, N_BASIS), dtype=jnp.float32), 'W_si0': jax.random.normal(ks[3], (MUL0, MUL0), jnp.float32), 'W_si1': jax.random.normal(ks[4], (MUL1, MUL1), jnp.float32), 'W_l1_0': jax.random.normal(ks[5], (MUL0, MUL0), jnp.float32), 'W_l1_1': jax.random.normal(ks[6], (MUL1, MUL1), jnp.float32), 'W_l2_00': jax.random.normal(ks[7], (MUL0, MUL0), jnp.float32), 'W_l2_10': jax.random.normal(ks[8], (MUL1, MUL0), jnp.float32), 'W_l2_01': jax.random.normal(ks[9], (MUL0, MUL1), jnp.float32), 'W_l2_11': jax.random.normal(ks[10], (MUL1, MUL1), jnp.float32), 'W_fc1': jax.random.normal(ks[11], (N_BASIS, N_RADIAL), jnp.float32), 'W_fc2': jax.random.normal(ks[12], (N_RADIAL, W_NUMEL), jnp.float32), 'edge_src': jax.random.randint(ks[13], (N_EDGES,), 0, N_NODES), 'edge_dst': jax.random.randint(ks[14], (N_EDGES,), 0, N_NODES)}
    _L3_gnn_all = _L3_gnn_setup()
    _L3_gnn_in = {k: v for k, v in _L3_gnn_all.items() if k in ('W_si0', 'W_si1', 'W_l1_0', 'W_l1_1', 'W_l2_00', 'W_l2_10', 'W_l2_01', 'W_l2_11', 'W_fc1', 'W_fc2')}
    del _L3_gnn_all
    return {'x': x, 'src': src, 'dst': dst, 'edge_attr_10': edge_attr_10, 'edge_attr_16': edge_attr_16, 'edge_attr_4': edge_attr_4, 'edge_attr_8': edge_attr_8, 'node_vec1': node_vec1, 'L0_gnn_Wfc1': _L0_gnn_in['Wfc1'], 'L0_gnn_Wfc2': _L0_gnn_in['Wfc2'], 'L0_gnn_Wsc0': _L0_gnn_in['Wsc0'], 'L0_gnn_Wsc1': _L0_gnn_in['Wsc1'], 'L0_gnn_Wl1_0': _L0_gnn_in['Wl1_0'], 'L0_gnn_Wl1_1': _L0_gnn_in['Wl1_1'], 'L0_gnn_Wl2_s': _L0_gnn_in['Wl2_s'], 'L0_gnn_Wl2_v': _L0_gnn_in['Wl2_v'], 'L0_gnn_Wa': _L0_gnn_in['Wa'], 'L1_gnn_Wm_ss': _L1_gnn_in['Wm_ss'], 'L1_gnn_Wm_vv': _L1_gnn_in['Wm_vv'], 'L1_gnn_Wm_sv': _L1_gnn_in['Wm_sv'], 'L1_gnn_Wm_vs': _L1_gnn_in['Wm_vs'], 'L1_gnn_Lm_s': _L1_gnn_in['Lm_s'], 'L1_gnn_Lm_v': _L1_gnn_in['Lm_v'], 'L1_gnn_Wu_ss': _L1_gnn_in['Wu_ss'], 'L1_gnn_Wu_vv': _L1_gnn_in['Wu_vv'], 'L1_gnn_Wu_sv': _L1_gnn_in['Wu_sv'], 'L1_gnn_Wu_vs': _L1_gnn_in['Wu_vs'], 'L1_gnn_Lu_s': _L1_gnn_in['Lu_s'], 'L1_gnn_Lu_v': _L1_gnn_in['Lu_v'], 'L2_gnn_sc_w0': _L2_gnn_in['sc_w0'], 'L2_gnn_sc_w1': _L2_gnn_in['sc_w1'], 'L2_gnn_lin1_w0': _L2_gnn_in['lin1_w0'], 'L2_gnn_lin1_w1': _L2_gnn_in['lin1_w1'], 'L2_gnn_fc_w1': _L2_gnn_in['fc_w1'], 'L2_gnn_fc_w2': _L2_gnn_in['fc_w2'], 'L2_gnn_lin2_w0': _L2_gnn_in['lin2_w0'], 'L2_gnn_lin2_w1': _L2_gnn_in['lin2_w1'], 'L2_gnn_lin3_w': _L2_gnn_in['lin3_w'], 'L3_gnn_W_si0': _L3_gnn_in['W_si0'], 'L3_gnn_W_si1': _L3_gnn_in['W_si1'], 'L3_gnn_W_l1_0': _L3_gnn_in['W_l1_0'], 'L3_gnn_W_l1_1': _L3_gnn_in['W_l1_1'], 'L3_gnn_W_l2_00': _L3_gnn_in['W_l2_00'], 'L3_gnn_W_l2_10': _L3_gnn_in['W_l2_10'], 'L3_gnn_W_l2_01': _L3_gnn_in['W_l2_01'], 'L3_gnn_W_l2_11': _L3_gnn_in['W_l2_11'], 'L3_gnn_W_fc1': _L3_gnn_in['W_fc1'], 'L3_gnn_W_fc2': _L3_gnn_in['W_fc2']}

def reference(x, src, dst, edge_attr_10, edge_attr_16, edge_attr_4, edge_attr_8, node_vec1, L0_gnn_Wfc1, L0_gnn_Wfc2, L0_gnn_Wsc0, L0_gnn_Wsc1, L0_gnn_Wl1_0, L0_gnn_Wl1_1, L0_gnn_Wl2_s, L0_gnn_Wl2_v, L0_gnn_Wa, L1_gnn_Wm_ss, L1_gnn_Wm_vv, L1_gnn_Wm_sv, L1_gnn_Wm_vs, L1_gnn_Lm_s, L1_gnn_Lm_v, L1_gnn_Wu_ss, L1_gnn_Wu_vv, L1_gnn_Wu_sv, L1_gnn_Wu_vs, L1_gnn_Lu_s, L1_gnn_Lu_v, L2_gnn_sc_w0, L2_gnn_sc_w1, L2_gnn_lin1_w0, L2_gnn_lin1_w1, L2_gnn_fc_w1, L2_gnn_fc_w2, L2_gnn_lin2_w0, L2_gnn_lin2_w1, L2_gnn_lin3_w, L3_gnn_W_si0, L3_gnn_W_si1, L3_gnn_W_l1_0, L3_gnn_W_l1_1, L3_gnn_W_l2_00, L3_gnn_W_l2_10, L3_gnn_W_l2_01, L3_gnn_W_l2_11, L3_gnn_W_fc1, L3_gnn_W_fc2):
    import jax
    import jax.numpy as jnp

    def _L0_gnn_ref(x, node_attr, edge_scalars, edge_attr_sh, edge_src, edge_dst, Wfc1, Wfc2, Wsc0, Wsc1, Wl1_0, Wl1_1, Wl2_s, Wl2_v, Wa):
        import jax, jax.numpy as jnp
        import numpy as np
        N = 625
        E = 10000
        MUL0 = 64
        MUL1 = 32
        FC_IN = 16
        FC_H = 64
        WNUM = 192
        n = x.shape[0]
        x0 = x[:, :MUL0]
        x1 = x[:, MUL0:].reshape(n, MUL1, 3)
        a = node_attr
        h = jax.nn.silu(edge_scalars @ (Wfc1 / jnp.sqrt(jnp.float32(FC_IN))))
        w = h @ (Wfc2 / jnp.sqrt(jnp.float32(FC_H)))
        w0 = w[:, :64]
        w1 = w[:, 64:128]
        w2 = w[:, 128:160]
        w3 = w[:, 160:192]
        inv8 = 1.0 / jnp.sqrt(jnp.float32(MUL0))
        inv32 = 1.0 / jnp.sqrt(jnp.float32(MUL1))
        sc = jnp.concatenate([x0 @ Wsc0 * a * inv8, (jnp.einsum('num,uv->nvm', x1, Wsc1) * a[..., None] * inv32).reshape(n, 3 * MUL1)], axis=1)
        f0 = x0 @ Wl1_0 * a * inv8
        f1 = jnp.einsum('num,uv->nvm', x1, Wl1_1) * a[..., None] * inv32
        e0 = f0[edge_src]
        e1 = f1[edge_src]
        sh0 = edge_attr_sh[:, :1]
        sh1 = edge_attr_sh[:, 1:4]
        mid0 = w0 * e0 * sh0
        mid1 = w3 * jnp.einsum('eum,em->eu', e1, sh1) / jnp.sqrt(3.0)
        mid2 = w1[:, :, None] * e0[:, :, None] * sh1[:, None, :]
        mid3 = w2[:, :, None] * e1 * sh0[:, :, None]
        cnt = jnp.clip(jax.ops.segment_sum(jnp.ones(edge_dst.shape, x.dtype), edge_dst, num_segments=n), 1.0)

        def smean(v):
            s = jax.ops.segment_sum(v, edge_dst, num_segments=n)
            return s / cnt.reshape((n,) + (1,) * (v.ndim - 1))
        n0, n1 = (smean(mid0), smean(mid1))
        n2, n3 = (smean(mid2), smean(mid3))
        scal = jnp.concatenate([n0, n1], axis=1)
        vec = jnp.concatenate([n2, n3], axis=1)
        inv96 = 1.0 / jnp.sqrt(jnp.float32(MUL0 + MUL1))
        alpha = scal @ Wa * a * inv96
        out_s = scal @ Wl2_s * a * inv96
        out_v = jnp.einsum('num,uv->nvm', vec, Wl2_v) * a[..., None] * inv96
        conv = jnp.concatenate([out_s, out_v.reshape(n, 3 * MUL1)], axis=1)
        return sc + alpha * conv

    def _L1_gnn_ref(node_features, edge_index, edge_attr_tensor, node_attr_scalar_raw, Wm_ss, Wm_vv, Wm_sv, Wm_vs, Lm_s, Lm_v, Wu_ss, Wu_vv, Wu_sv, Wu_vs, Lu_s, Lu_v):
        import jax, jax.numpy as jnp
        import numpy as np
        N = 625
        E = 20000
        INV_SQRT3 = 0.5773502691896258
        INV8 = 0.125
        INV_SQRT32 = 0.17677669529663687
        INV64 = 0.015625
        INV32 = 0.03125
        INV_SQRT2048 = 0.022097086912079608
        n = node_features.shape[0]
        e = edge_attr_tensor.shape[0]
        row, col = (edge_index[0], edge_index[1])
        r_vec = edge_attr_tensor[:, :3]
        dist = edge_attr_tensor[:, 3:4]
        xj = node_features[col]
        s = xj[:, :64]
        v = xj[:, 64:].reshape(e, 32, 3)
        m0 = s @ Wm_ss * dist * INV8 + jnp.einsum('eui,ei->eu', v, r_vec) @ Wm_vv * (INV_SQRT3 * INV_SQRT32)
        m1 = (s @ Wm_sv)[:, :, None] * r_vec[:, None, :] * INV8 + jnp.einsum('eui,uw->ewi', v, Wm_vs) * dist[:, :, None] * INV_SQRT32
        m0 = m0 + s @ Lm_s * INV8
        m1 = m1 + jnp.einsum('eui,uw->ewi', v, Lm_v) * INV_SQRT32
        msg = jnp.concatenate([m0, m1.reshape(e, 96)], axis=-1)
        agg = jax.ops.segment_sum(msg, row, num_segments=n)
        a0 = agg[:, :64]
        a1 = agg[:, 64:].reshape(n, 32, 3)
        xs = node_features[:, :64]
        xv = node_features[:, 64:].reshape(n, 32, 3)
        u0 = jnp.einsum('nu,nv,uvw->nw', xs, a0, Wu_ss) * INV64 + jnp.einsum('nui,nvi,uvw->nw', xv, a1, Wu_vv) * (INV_SQRT3 * INV32)
        u1 = jnp.einsum('nu,nvi,uvw->nwi', xs, a1, Wu_sv) * INV_SQRT2048 + jnp.einsum('nui,nv,uvw->nwi', xv, a0, Wu_vs) * INV_SQRT2048
        u0 = u0 + xs @ Lu_s * INV8
        u1 = u1 + jnp.einsum('nui,uw->nwi', xv, Lu_v) * INV_SQRT32
        upd = jnp.concatenate([u0, u1.reshape(n, 96)], axis=-1)
        return node_features + upd

    def _L2_gnn_ref(node_input, node_attr, edge_attr, edge_scalars, sc_w0, sc_w1, lin1_w0, lin1_w1, fc_w1, fc_w2, lin2_w0, lin2_w1, lin3_w, edge_src, edge_dst, num_neighbors):
        import jax, jax.numpy as jnp
        import numpy as np
        INV3 = 1.0 / np.sqrt(3.0)

        def _fctp(x_s, x_v, attr, w0, w1):
            s = x_s @ w0 * (1.0 / np.sqrt(x_s.shape[-1])) * attr
            v = jnp.einsum('nud,uw->nwd', x_v, w1) * (1.0 / np.sqrt(x_v.shape[-2])) * attr[..., None]
            return (s, v)
        N = node_input.shape[0]
        h = jax.nn.silu(edge_scalars @ fc_w1 * (1.0 / np.sqrt(8.0)))
        weight = h @ fc_w2 * (1.0 / np.sqrt(64.0))
        xs, xv = (node_input[:, :64], node_input[:, 64:].reshape(N, 32, 3))
        sc_s, sc_v = _fctp(xs, xv, node_attr, sc_w0, sc_w1)
        f_s, f_v = _fctp(xs, xv, node_attr, lin1_w0, lin1_w1)
        gs = f_s[edge_src]
        gv = f_v[edge_src]
        ys, yv = (edge_attr[:, :1], edge_attr[:, 1:])
        w1_, w2_ = (weight[:, :64], weight[:, 64:128])
        w3_, w4_ = (weight[:, 128:160], weight[:, 160:192])
        m0a = gs * ys * w1_
        m0b = jnp.sum(gv * yv[:, None, :], -1) * INV3 * w4_
        m1a = gs[..., None] * yv[:, None, :] * w2_[..., None]
        m1b = gv * ys[..., None] * w3_[..., None]
        E = m0a.shape[0]
        edge_feat = jnp.concatenate([m0a, m0b, m1a.reshape(E, 192), m1b.reshape(E, 96)], -1)
        mid = jax.ops.segment_sum(edge_feat, edge_dst, num_segments=N)
        mid = mid / np.sqrt(float(num_neighbors))
        mid_s, mid_v = (mid[:, :96], mid[:, 96:].reshape(N, 96, 3))
        c_s, c_v = _fctp(mid_s, mid_v, node_attr, lin2_w0, lin2_w1)
        conv = jnp.concatenate([c_s, c_v.reshape(N, -1)], -1)
        scfeat = jnp.concatenate([sc_s, sc_v.reshape(N, -1)], -1)
        angle = 0.1 * (mid_s @ lin3_w) * (1.0 / np.sqrt(96.0)) * node_attr
        return jnp.cos(angle) * scfeat + jnp.sin(angle) * conv

    def _L3_gnn_ref(node_input, node_attr, edge_src, edge_dst, edge_attr, edge_length_embedded, W_si0, W_si1, W_l1_0, W_l1_1, W_l2_00, W_l2_10, W_l2_01, W_l2_11, W_fc1, W_fc2):
        import jax, jax.numpy as jnp
        import numpy as np
        N_NODES = 50000
        N_EDGES = 25000
        MUL0, MUL1 = (64, 32)
        N_BASIS, N_RADIAL = (10, 100)
        W_NUMEL = 192
        NUM_NEIGHBORS = 16.0
        INV_SQRT3 = np.float32(1.0 / np.sqrt(3.0))
        RELU_GAIN = np.float32(np.sqrt(2.0))
        FAN_L2 = np.float32(np.sqrt(MUL0 + MUL1))

        def _fctp_scalar_attr(x0, x1, a, W0, W1):
            o0 = x0 @ W0 * a * (1.0 / np.sqrt(W0.shape[0]))
            o1 = jnp.einsum('nud,uw->nwd', x1, W1) * a[..., None] * (1.0 / np.sqrt(W1.shape[0]))
            return (o0, o1)
        N = node_input.shape[0]
        x0 = node_input[:, :MUL0]
        x1 = node_input[:, MUL0:].reshape(N, MUL1, 3)
        a = node_attr
        h = jax.nn.relu(edge_length_embedded @ W_fc1 * (1.0 / np.sqrt(N_BASIS))) * RELU_GAIN
        w = h @ W_fc2 * (1.0 / np.sqrt(N_RADIAL))
        w0, w1, w2, w3 = (w[:, :64], w[:, 64:128], w[:, 128:160], w[:, 160:192])
        si0, si1 = _fctp_scalar_attr(x0, x1, a, W_si0, W_si1)
        l0, l1 = _fctp_scalar_attr(x0, x1, a, W_l1_0, W_l1_1)
        y0 = l0[edge_src]
        y1 = l1[edge_src]
        e0 = edge_attr[:, :1]
        e1 = edge_attr[:, 1:4]
        m0 = w0 * y0 * e0
        m1 = (w1 * y0)[:, :, None] * e1[:, None, :]
        m2 = (w2 * e0)[:, :, None] * y1
        m3 = w3 * jnp.einsum('eud,ed->eu', y1, e1) * INV_SQRT3
        inv = np.float32(1.0 / np.sqrt(NUM_NEIGHBORS))
        s0 = jax.ops.segment_sum(m0, edge_dst, num_segments=N) * inv
        s1 = jax.ops.segment_sum(m1, edge_dst, num_segments=N) * inv
        s2 = jax.ops.segment_sum(m2, edge_dst, num_segments=N) * inv
        s3 = jax.ops.segment_sum(m3, edge_dst, num_segments=N) * inv
        o0 = (s0 @ W_l2_00 + s3 @ W_l2_10) * a / FAN_L2
        o1 = (jnp.einsum('nud,uw->nwd', s1, W_l2_01) + jnp.einsum('nud,uw->nwd', s2, W_l2_11)) * a[..., None] / FAN_L2
        out0 = si0 + 0.5 * o0
        out1 = si1 + 0.5 * o1
        return jnp.concatenate([out0, out1.reshape(N, 3 * MUL1)], axis=1)
    edge_index = jnp.stack([src, dst])
    x = _layernorm(x + _L0_gnn_ref(x, node_vec1, edge_attr_16, edge_attr_4, src, dst, L0_gnn_Wfc1, L0_gnn_Wfc2, L0_gnn_Wsc0, L0_gnn_Wsc1, L0_gnn_Wl1_0, L0_gnn_Wl1_1, L0_gnn_Wl2_s, L0_gnn_Wl2_v, L0_gnn_Wa), axis=-1)
    x = _layernorm(x + _L1_gnn_ref(x, edge_index, edge_attr_4, node_vec1, L1_gnn_Wm_ss, L1_gnn_Wm_vv, L1_gnn_Wm_sv, L1_gnn_Wm_vs, L1_gnn_Lm_s, L1_gnn_Lm_v, L1_gnn_Wu_ss, L1_gnn_Wu_vv, L1_gnn_Wu_sv, L1_gnn_Wu_vs, L1_gnn_Lu_s, L1_gnn_Lu_v), axis=-1)
    x = _layernorm(x + _L2_gnn_ref(x, node_vec1, edge_attr_4, edge_attr_8, L2_gnn_sc_w0, L2_gnn_sc_w1, L2_gnn_lin1_w0, L2_gnn_lin1_w1, L2_gnn_fc_w1, L2_gnn_fc_w2, L2_gnn_lin2_w0, L2_gnn_lin2_w1, L2_gnn_lin3_w, src, dst, 16), axis=-1)
    x = _layernorm(x + _L3_gnn_ref(x, node_vec1, src, dst, edge_attr_4, edge_attr_10, L3_gnn_W_si0, L3_gnn_W_si1, L3_gnn_W_l1_0, L3_gnn_W_l1_1, L3_gnn_W_l2_00, L3_gnn_W_l2_10, L3_gnn_W_l2_01, L3_gnn_W_l2_11, L3_gnn_W_fc1, L3_gnn_W_fc2), axis=-1)
    return x

_drawn_inputs = setup_inputs


def setup_inputs(seed=0):
    import zlib

    import numpy as np

    out = dict(_drawn_inputs(seed))
    spreads = {}
    factors = {'edge_attr_16': 8.0,
     'edge_attr_8': 7.512,
     'L0_gnn_Wfc1': 8.0,
     'L0_gnn_Wfc2': 8.0,
     'L0_gnn_Wl1_0': 8.0,
     'L0_gnn_Wl1_1': 8.0,
     'L0_gnn_Wl2_s': 8.0,
     'L0_gnn_Wl2_v': 8.0,
     'L0_gnn_Wa': 8.0,
     'L2_gnn_lin1_w0': 7.841,
     'L2_gnn_lin1_w1': 8.0,
     'L2_gnn_fc_w1': 7.306,
     'L2_gnn_fc_w2': 7.486,
     'L2_gnn_lin2_w0': 8.0,
     'L2_gnn_lin2_w1': 8.0,
     'L2_gnn_lin3_w': 8.0,
     'L2_gnn_sc_w0': 46.664,
     'L2_gnn_sc_w1': 39.6}
    for name, (base, spread) in spreads.items():
        noise = np.random.default_rng([zlib.crc32(name.encode()), seed]).standard_normal(out[name].shape)
        drawn = base * np.exp(spread * noise) if base else spread * noise
        out[name] = jnp.asarray(drawn.astype(out[name].dtype))
    for name, factor in factors.items():
        out[name] = (out[name] * factor).astype(out[name].dtype)
    return out
```

```python
from contextlib import ExitStack
import math

import concourse.bass as bass
from concourse import mybir

F32 = mybir.dt.float32
BF16 = mybir.dt.bfloat16
I32 = mybir.dt.int32
ALU = mybir.AluOpType
ACT = mybir.ActivationFunctionType
AX = mybir.AxisListType
ds = bass.ds

P = 128
N = 3125
NB = 25
E = 103125
T = 816
TA = 832
EA = TA * P
BT = 4
S, V, D = 64, 32, 160
EPS = 1e-5
PAD_DST = NB * P + P - 1
PAD_SRC = NB * P - 1
TWO_PI = (6.28125, 2029 / 2.0 ** 20, 2 * math.pi - 6.28125 - 2029 / 2.0 ** 20)
ROUND = 1.5 * 2.0 ** 23
U = 5
WX = 224
NREC = T * P + BT * P
AW = 608
CW = 162
LAST_LAYER = 3

R96, R32, R3 = 1 / math.sqrt(96.0), 1 / math.sqrt(32.0), 1 / math.sqrt(3.0)

FC = {
    0: dict(attr="a16T", k=16, h=64, c1=1 / 4.0, c2=1 / 8.0, act=ACT.Silu, cm=R96),
    2: dict(attr="a8T", k=8, h=64, c1=1 / math.sqrt(8.0), c2=1 / 8.0, act=ACT.Silu, cm=R96 / 4.0),
    3: dict(attr="a10T", k=10, h=100, c1=1 / math.sqrt(10.0), c2=math.sqrt(2.0) / 10.0, act=ACT.Relu,
            cm=R96 / 4.0 * 0.5),
}
W_FC = {0: ("L0_gnn_Wfc1", "L0_gnn_Wfc2"), 2: ("L2_gnn_fc_w1", "L2_gnn_fc_w2"), 3: ("L3_gnn_W_fc1", "L3_gnn_W_fc2")}
W_LIN = {0: ("L0_gnn_Wl1_0", "L0_gnn_Wl1_1"), 2: ("L2_gnn_lin1_w0", "L2_gnn_lin1_w1"),
         3: ("L3_gnn_W_l1_0", "L3_gnn_W_l1_1")}
W_SELF = {0: ("L0_gnn_Wsc0", "L0_gnn_Wsc1"), 1: ("L1_gnn_Lu_s", "L1_gnn_Lu_v"),
          2: ("L2_gnn_sc_w0", "L2_gnn_sc_w1"), 3: ("L3_gnn_W_si0", "L3_gnn_W_si1")}

PB = 160
PW = 448
CONV_ROWS = [("P2", 0, 0), ("P0", 0, 0), ("P2", 1, 0), ("P0", 1, 0), ("P2", 2, 0),
             ("P3", 0, 0), ("P1", 0, 0), ("P1", 1, 0),
             ("P1", 0, 1), ("P3", 1, 1), ("P1", 1, 1),
             ("P1", 0, 2), ("P1", 1, 2), ("P3", 2, 2)]
CNT_COL = 32 * len(CONV_ROWS)
TP_PARTS = [(0, D, 0, 0), (0, D, 1, 160), (32, 96, 2, 320), (0, 96, 3, 416), (128, 96, 4, 0)]


def msg_rows():
    order = [("v", 1), ("s", 0), ("s", 1), ("v", 0), ("v", 2)]
    rows = []
    for kind, m in order:
        rows.append(("Lm_s", m, 0, S, 1 / 8) if kind == "s" else ("Lm_v", 0, S + V * m, V, R32))
    for kind, m in order:
        rows.append(("Wm_ss", m, 0, S, 1 / 8) if kind == "s" else ("Wm_vs", 0, S + V * m, V, R32))
    for i, part in ((0, "ssv"), (1, "vss"), (2, "vss")):
        half = 0
        for kind in part:
            if kind == "s":
                rows.append(("Wm_sv", half, S + V * i, V, 1 / 8))
                half += 1
            else:
                rows.append(("Wm_vv", 0, 0, S, R3 * R32))
    return rows


def gnn_kernel(nc, A, out):
    ctx = ExitStack()
    with ctx:
        def sb(name, shape, dt=F32):
            return ctx.enter_context(nc.sbuf_tensor(name, shape, dt))

        def sem(name):
            return ctx.enter_context(nc.semaphore(name))

        def scratch(name, shape, dt=F32):
            return nc.dram_tensor(name, shape, dt, kind="Internal").ap()

        table = {l: scratch(f"table{l}", (NB * P, D)) for l in (0, 2, 3)}
        table[1] = scratch("table1", ((NB + 1) * P, WX))
        agg_dram = {l: scratch(f"agg{l}", (NB * P, AW)) for l in range(4)}
        rec_dram = scratch("records", (NREC, 8))
        xT_dram = scratch("xT", (NB * P, 2 * P))

        ident = sb("ident", [P, P])
        lower = sb("lower", [P, P])
        ones = sb("ones", [P, P])
        ones_bf = sb("ones_bf", [P, 1], BF16)
        zeros_bf = sb("zeros_bf", [P, 512], BF16)
        iota = sb("iota", [P, P])
        blk_id = sb("blk_id", [P, NB])
        tile_id = sb("tile_id", [P, 7])
        node_id = sb("node_id", [P, P])
        av = sb("av", [P, NB])
        meta = sb("meta", [P, TA, 5])
        srci = sb("srci", [P, TA], I32)
        x_all = sb("x_all", [P, NB, D])
        self_all = sb("self_all", [P, NB, D])
        conv_all = sb("conv_all", [P, NB, CW])
        ebuf = sb("ebuf", [P, BT * (WX + PW + 5 * P)])
        idx_slot = sb("idx_slot", [P, BT], I32)
        meta_slot = sb("meta_slot", [P, BT, 5])
        rec_slot = sb("rec_slot", [P, BT, 8])
        hot = sb("hot", [P, BT, P], BF16)
        attrT = sb("attrT", [16, BT * P])
        hidT = sb("hidT", [100, BT * P])
        agg_stage = sb("agg_stage", [P, AW])
        agg_in = sb("agg_in", [P, U, AW])
        aggT = sb("aggT", [P, U, 5 * P])
        xs = sb("xs", [P, U, D])
        xsT = sb("xsT", [P, U, 2 * P])
        row_out = sb("row_out", [P, U, WX])
        small = sb("small", [P, 16, NB])
        stats = sb("stats", [P, NB, 6])
        tab_i = {l: sb(f"tab_{l}", [1, 3, NB], I32) for l in ("dst", "src")}

        gathered = ebuf[:, 0:BT * WX].rearrange("p (j c) -> p j c", j=BT)
        prod = ebuf[:, BT * WX:BT * WX + BT * PW].rearrange("p (j c) -> p j c", j=BT)
        sel0 = BT * (WX + PW)
        sel = ebuf[:, sel0:sel0 + BT * 5 * P].rearrange("p (j k n) -> p j k n", j=BT, k=5)
        bil = ebuf[:, 0:5120]
        sort_v = ebuf[:, 0:5 * T].rearrange("p (c t) -> p c t", c=5)
        blk_i = ebuf[:, 5 * T:6 * T].bitcast(I32)

        w1 = {l: sb(f"w1_{l}", [f["k"], f["h"]]) for l, f in FC.items()}
        w2 = {l: sb(f"w2_{l}", [f["h"], 192]) for l, f in FC.items()}
        wconv = {l: sb(f"wconv_{l}", [P, 4, 161]) for l in FC}
        wmsg = sb("wmsg", [P, 5, D])
        wa = {l: sb(f"wa_{l}", [P, 2, P]) for l in range(4)}
        wb = {l: sb(f"wb_{l}", [V, 2, V]) for l in range(4)}
        wu_ss = sb("wu_ss", [S, S * S])
        wu_vv = sb("wu_vv", [P, V * S])
        wu_sv = sb("wu_sv", [S, V * V])
        wu_vs = sb("wu_vs", [S, V * V])
        upd = sb("upd", [P, 5, S])
        row_scale = {l: sb(f"row_scale{l}", [P, 5]) for l in range(4)}
        wa_scale = sb("wa_scale", [P, 1])
        blk128 = sb("blk128", [P, NB])
        tile_mm = sb("tile_mm", [P, 2, 7])
        tile_lim = sb("tile_lim", [P, 2, 7])
        hit = sb("hit", [P, 2, NB, 7])
        rng = sb("rng", [P, 2 * NB])
        rng_max = sb("rng_max", [2 * NB, 1])
        trow = sb("trow", [1, 4, NB])
        tri = sb("tri", [1, NB], I32)
        zrow = sb("zrow", [P, T])
        rec_idx = sb("rec_idx", [P, BT], I32)
        scat_rec = sb("scat_rec", [P, 2, 8, 8])
        scat_idx = sb("scat_idx", [P, 2, 8], I32)

        banks = [ctx.enter_context(nc.psum_tensor(f"bank{i}", [P, 512], F32)) for i in range(8)]
        ps_hid, ps_w, ps_agg, ps_agg2 = banks[0], banks[1:3], banks[3], banks[4]

        bar = sem("bar")
        w_zero, loads, wscaled = sem("w_zero"), sem("loads"), sem("wscaled")
        consts = sem("consts")
        held_act, held_dve = sem("held_act"), sem("held_dve")
        go = sem("go")
        vch = sem("vch")
        pch = sem("pch")
        out_done = sem("out_done")
        init_done = sem("init_done")

        bars = {}

        def barrier(eng, name):
            k = bars.get(name, 0) + 1
            bars[name] = k
            eng.drain().then_inc(bar, 1)
            eng.wait_ge(bar, 5 * k)

        chain = [0]

        def link(ins):
            chain[0] += 1
            ins.then_inc(vch, 1)
            nc.vector.wait_ge(vch, chain[0])

        def link2(ins, b, c):
            ins.then_inc(bil_link, 1)
            nc.vector.wait_ge(bil_link, b * 2 + c + 1)

        block = ctx.enter_context(nc.Block())

        w_loads = []
        for l, f in FC.items():
            w_loads += [(w1[l][:, :], A[W_FC[l][0]]), (w2[l][:, :], A[W_FC[l][1]])]
            w_loads += [(wa[l][0:S, 0, 0:S], A[W_LIN[l][0]]), (wb[l][:, 0, :], A[W_LIN[l][1]])]
            w_loads += [(wa[l][S + V * m:S + V * m + V, 0, S + V * m:S + V * m + V], A[W_LIN[l][1]]) for m in (0, 1)]
            for r, (what, h, i) in enumerate(CONV_ROWS):
                q, c = 32 * (r % 4), r // 4
                dst = wconv[l][q:q + 32, c, :]
                if l == 0:
                    ws, wv, wg = A["L0_gnn_Wl2_s"], A["L0_gnn_Wl2_v"], A["L0_gnn_Wa"]
                    ws, wv = [ws[0:32], ws[32:64], ws[64:96]], [wv[0:32], wv[32:64], wv[64:96]]
                elif l == 2:
                    ws, wv, wg = A["L2_gnn_lin2_w0"], A["L2_gnn_lin2_w1"], A["L2_gnn_lin3_w"]
                    ws, wv = [ws[0:32], ws[32:64], ws[64:96]], [wv[0:32], wv[32:64], wv[64:96]]
                else:
                    ws = [A["L3_gnn_W_l2_00"][0:32], A["L3_gnn_W_l2_00"][32:64], A["L3_gnn_W_l2_10"]]
                    wv = [A["L3_gnn_W_l2_01"][0:32], A["L3_gnn_W_l2_01"][32:64], A["L3_gnn_W_l2_11"]]
                    wg = None
                if what in ("P0", "P3"):
                    part = h if what == "P0" else 2
                    w_loads.append((dst[:, 0:S], ws[part]))
                    if wg is not None:
                        w_loads.append((dst[:, D:D + 1], wg[32 * part:32 * part + 32, :]))
                else:
                    part, m = (h, i) if what == "P1" else (2, h)
                    w_loads.append((dst[:, S + V * m:S + V * m + V], wv[part]))
        for l, (w0, w1n) in W_SELF.items():
            w_loads += [(wa[l][0:S, 1, 0:S], A[w0]), (wb[l][:, 1, :], A[w1n])]
            w_loads += [(wa[l][S + V * m:S + V * m + V, 1, S + V * m:S + V * m + V], A[w1n]) for m in (0, 1)]
        for r, (name, h, c0, cn, _) in enumerate(msg_rows()):
            w_loads.append((wmsg[32 * (r % 4):32 * (r % 4) + 32, r // 4, c0:c0 + cn],
                            A["L1_gnn_" + name][32 * h:32 * h + 32, :]))
        w_loads += [(wu_ss[:, :], A["wu_ss"]), (wu_sv[:, :], A["wu_sv"]), (wu_vs[:, :], A["wu_vs"])]
        w_loads += [(wu_vv[q:q + V, :], A["wu_vv"]) for q in (0, S, S + V)]
        half = len(w_loads) // 2

        both = ("prod_ready", "sel_done", "meta_ready", "idx_ready", "agg_closed", "agg_out", "agg_stored",
                "node_ids")
        sems = {}
        for l in range(4):
            names = both + (("rec_in",) if l == 1 else ("attr_in", "hid_ps", "hid_ready", "w_ready"))
            sems[l] = {n: sem(f"{n}_{l}") for n in names}
            sems[l]["got"] = [sem(f"got{j}_{l}") for j in range(BT)]
        nsem = {n: sem("n_" + n) for n in ("aT_ps", "aT", "conv_ps", "conv", "sqrt_in", "sqrt_out")}
        nsem["in"] = [sem(f"n_in{k}") for k in range(U)]
        psem = {n: sem("p_" + n) for n in ("xs", "xT_ps", "xT", "out_ps", "row", "back")}
        psem["stored"] = [sem(f"p_stored{k}") for k in range(U)]
        psem["tstored"] = [sem(f"p_tstored{k}") for k in range(U)]
        bsem = {n: sem("b_" + n) for n in ("xT_in", "a_slot", "aT_ps", "aT", "y_ps", "y_used", "done")}
        ssem = {n: sem("s_" + n) for n in ("cnt", "off", "trows", "tred", "t50", "tred2", "trow", "dstf")}
        srt, srt2, final = sem("srt"), sem("srt2"), sem("final")
        sc_slot = [sem(f"sc_slot{h}") for h in range(2)]
        sc_done = [[sem(f"sc_done{h}_{j}") for j in range(8)] for h in range(2)]
        stats_sem = sem("stats_sem")
        bil_own, bil_link = sem("bil_own"), sem("bil_link")
        sin_in, sin_out = sem("sin_in"), sem("sin_out")
        rec_fill = sem("rec_fill")

        def table_reg(eng, tab, row, b, hi):
            return eng.value_load(tab[0:1, row, ds(b, 1)], min_val=0, max_val=hi)

        def bounded(v, hi):
            return nc.s_assert_within(v, 0, hi, skip_runtime_bounds_check_because=
                                      "a body starts before its block's end, or at an empty block's start")

        def rounds(eng, n, body):
            body(0, True)
            with eng.Fori(1, n) as u:
                body(u, False)

        credits = []
        for l in range(4):
            q = sems[l]
            credits += [(q["prod_ready"], BT), (q["sel_done"], BT), (q["meta_ready"], 1), (q["idx_ready"], BT),
                        (q["agg_out"], 1)]
            if l != 1:
                credits += [(q["hid_ps"], 1), (q["hid_ready"], 1)]
        credits += [(nsem[n], U) for n in ("aT", "conv", "conv_ps")]
        credits += [(psem[n], U) for n in ("xT_ps", "xT", "out_ps", "row", "back")]
        credits += [(bsem["done"], 1), (bsem["y_used"], 6)]

        def pair_end(k):
            return min(k // 2 * 2 + 2, U)

        def conv_end(k, l):
            return 3 if k < 3 and l != 1 else U

        def table_of(l):
            return tab_i["src"] if l == 1 else tab_i["dst"]

        MAXB = NB * (TA // BT)

        def chunks(l):
            return [128, 128, 128, 128, 96] if l == 1 else [128, 128, 128, 64]

        @block.sync
        def _(sp):
            sp.dma_start(srci[:, :], A["src_t"]).then_inc(loads, 16)
            sp.dma_start(x_all[:, :, :], A["x_in"].rearrange("(b p) d -> p b d", p=P)).then_inc(loads, 16)
            sp.dma_start(av[:, :], A["a_t"]).then_inc(loads, 16)
            sp.dma_start(ebuf[:, 0:TA].bitcast(I32), A["dst_t"]).then_inc(loads, 16)
            sp.dma_start(ebuf[:, TA:5 * TA], A["attr4_t"]).then_inc(loads, 16)
            sp.wait_ge(w_zero, 1)
            for dst, src in w_loads[:half]:
                sp.dma_start(dst, src).then_inc(loads, 16)
            barrier(sp, "sp")
            barrier(sp, "sp")

            def publish(l):
                with sp.Fori(0, NB // U) as u:
                    for k in range(U):
                        sp.wait_ge(psem["row"], NB * l + u * U + k + 1 + U)
                        w = WX if l == 1 else D
                        sp.dma_start(table[l][ds((u * U + k) * P, P), :], row_out[:, k, 0:w])\
                            .then_inc(psem["stored"][k], 16)
                        if l == 1:
                            sp.wait_ge(psem["xT"], NB * l + u * U + k + 1 + U)
                            sp.dma_start(xT_dram[ds((u * U + k) * P, P), 0:P], xsT[:, k, 0:P])\
                                .then_inc(psem["tstored"][k], 16)
                            sp.dma_start(xT_dram[ds((u * U + k) * P, V), P:2 * P], xsT[0:V, k, P:2 * P])\
                                .then_inc(psem["tstored"][k], 16)
                for k in range(U):
                    sp.wait_ge(psem["stored"][k], 16 * (NB // U) * (l + 1))
                    if l == 1:
                        sp.wait_ge(psem["tstored"][k], 32 * (NB // U))

            publish(0)
            barrier(sp, "sp")
            for l in range(LAST_LAYER + 1):
                q = sems[l]
                tab = table_of(l)
                with sp.Fori(0, NB) as b:
                    n = table_reg(sp, tab, 0, b, MAXB)
                    base = table_reg(sp, tab, 1, b, MAXB)
                    start = table_reg(sp, tab, 2, b, NREC)
                    with sp.Fori(0, n) as i:
                        if l == 1:
                            sp.wait_ge(q["meta_ready"], base + i + 1)
                            src = rec_dram[ds(bounded(start + i * (BT * P), T * P), BT * P), :]
                            sp.dma_start(rec_slot[:, :, :], src.rearrange("(p j) c -> p j c", j=BT))\
                                .then_inc(q["rec_in"], 16)
                        else:
                            f = FC[l]
                            sp.wait_ge(q["hid_ps"], base + i + 1)
                            sp.dma_start(attrT[0:f["k"], :],
                                         A[f["attr"]][:, ds(bounded((start + i * BT) * P, (T - 1) * P), BT * P)])\
                                .then_inc(q["attr_in"], 16)
                if l != 1:
                    total = table_reg(sp, tab, 1, NB - 1, MAXB) + table_reg(sp, tab, 0, NB - 1, MAXB)
                    sp.wait_ge(q["hid_ps"], total + 1)
                    sp.dma_start(attrT[0:FC[l]["k"], :], A[FC[l]["attr"]][:, 0:BT * P]).then_inc(q["attr_in"], 16)
                barrier(sp, "sp")
                w = {0: CNT_COL + 1, 1: AW, 2: CNT_COL, 3: CNT_COL}[l]
                with sp.Fori(0, NB // U) as u:
                    for k in range(U):
                        sp.wait_ge(nsem["conv"], NB * l + u * U + k + 1)
                        sp.dma_start(agg_in[:, k, 0:w], agg_dram[l][ds((u * U + k) * P, P), 0:w])\
                            .then_inc(nsem["in"][k], 16)
                barrier(sp, "sp")
                if l == 1:
                    with sp.Fori(0, NB) as b:
                        sp.wait_ge(bsem["done"], b + 1)
                        sp.dma_start(xsT[:, 0, 0:P], xT_dram[ds(b * P, P), 0:P]).then_inc(bsem["xT_in"], 16)
                        sp.dma_start(xsT[0:V, 0, P:2 * P], xT_dram[ds(b * P, V), P:2 * P]).then_inc(bsem["xT_in"], 16)
                    barrier(sp, "sp")
                if l < LAST_LAYER:
                    publish(l + 1)
                    barrier(sp, "sp")
            sp.wait_ge(final, NB)
            sp.dma_start(out.rearrange("(b p) d -> p b d", p=P), x_all[:, :, :]).then_inc(out_done, 16)
            sp.wait_ge(out_done, 16)

        @block.gpsimd
        def _(pool):
            def held():
                pool.sem_inc(go, 1)

            pool.memset(ident[:, :], 0.0).then_inc(pch, 1)
            pool.memset(lower[:, :], 1.0).then_inc(pch, 1)
            pool.memset(ones[:, :], 1.0).then_inc(consts, 1)
            pool.memset(zeros_bf[:, :], 0.0).then_inc(consts, 1)
            pool.memset(ones_bf[:, :], 1.0).then_inc(consts, 1)
            pool.iota(iota[:, :], [[1, P]], base=0, channel_multiplier=0,
                      allow_small_or_imprecise_dtypes=True).then_inc(consts, 1)
            pool.iota(blk_id[:, :], [[1, NB]], base=0, channel_multiplier=0,
                      allow_small_or_imprecise_dtypes=True).then_inc(consts, 1)
            pool.iota(tile_id[:, :], [[P, 7]], base=0, channel_multiplier=1,
                      allow_small_or_imprecise_dtypes=True).then_inc(consts, 1)
            pool.wait_ge(pch, 2)
            pool.affine_select(out=ident[:, :], in_=ident[:, :], compare_op=ALU.not_equal, fill=1.0, base=0,
                               pattern=[[-1, P]], channel_multiplier=1).then_inc(consts, 1)
            pool.affine_select(out=lower[:, :], in_=lower[:, :], compare_op=ALU.is_gt, fill=0.0, base=0,
                               pattern=[[1, P]], channel_multiplier=-1).then_inc(consts, 1)
            pool.memset(agg_stage[:, :], 0.0).then_inc(pch, 1)
            pool.wait_ge(pch, 3)
            pool.memset(agg_stage[:, 0:8 * BT].rearrange("p (j c) -> p j c", c=8)[:, :, 1:2], -1.0).then_inc(pch, 1)
            pool.wait_ge(pch, 4)
            pool.dma_start(rec_dram[T * P:NREC, :].rearrange("(p j) c -> p (j c)", j=BT),
                           agg_stage[:, 0:8 * BT]).then_inc(rec_fill, 16)
            pool.dma_start(table[1][NB * P:(NB + 1) * P, :], agg_stage[:, 64:64 + WX]).then_inc(rec_fill, 16)
            pool.wait_ge(rec_fill, 32)
            barrier(pool, "pool")
            with pool.Fori(0, T // 16) as i:
                for h in range(2):
                    pool.wait_ge(sc_slot[h], i + 1)
                    held()
                    for j in range(8):
                        pool.indirect_dma_start(
                            rec_dram[:, :], bass.IndirectOffsetOnAxis(ap=scat_idx[:, h, j:j + 1], axis=0),
                            scat_rec[:, h, j, :], None).then_inc(sc_done[h][j], 16)
            for h in range(2):
                for j in range(8):
                    pool.wait_ge(sc_done[h][j], 16 * (T // 16))
            barrier(pool, "pool")
            barrier(pool, "pool")
            for l in range(LAST_LAYER + 1):
                q = sems[l]
                tab = table_of(l)
                w = WX if l == 1 else D
                with pool.Fori(0, NB) as b:
                    n = table_reg(pool, tab, 0, b, MAXB)
                    base = table_reg(pool, tab, 1, b, MAXB)
                    start = table_reg(pool, tab, 2, b, NREC)
                    with pool.Fori(0, n) as i:
                        for j in range(BT):
                            g = base + i
                            if l == 1:
                                if j == 0:
                                    pool.wait_ge(q["meta_ready"], g + 2)
                                pool.wait_ge(q["sel_done"], g * BT + j + 1)
                                held()
                                pool.tensor_copy(idx_slot[:, j:j + 1], rec_idx[:, j:j + 1]).then_inc(q["idx_ready"], 1)
                            else:
                                pool.wait_ge(q["prod_ready"], g * BT + j + 1)
                                held()
                                pool.tensor_copy(idx_slot[:, j:j + 1], srci[:, ds(bounded(start + i * BT, T - 1) + j, 1)])\
                                    .then_inc(q["idx_ready"], 1)
                            pool.wait_ge(q["idx_ready"], g * BT + j + 1 + BT)
                            held()
                            pool.indirect_dma_start(
                                gathered[:, j, 0:w], None, table[l][:, :],
                                bass.IndirectOffsetOnAxis(ap=idx_slot[:, j:j + 1], axis=0))\
                                .then_inc(q["got"][j], 16)
                barrier(pool, "pool")
                barrier(pool, "pool")
                if l == 1:
                    barrier(pool, "pool")
                if l < LAST_LAYER:
                    barrier(pool, "pool")

        @block.scalar
        def _(act):
            act.wait_ge(w_zero, 1)
            for dst, src in w_loads[half:]:
                act.dma_start(dst, src).then_inc(loads, 16)
            barrier(act, "act")
            barrier(act, "act")

            def publish(l):
                q = psem

                def body(u, first):
                    for k in range(U):
                        g = u * U + k
                        tp = banks[5 + k // 2][:, 256 * (k % 2):256 * (k % 2) + 256]
                        act.wait_ge(q["xT_ps"], NB * l + u * U + pair_end(k) + U)
                        act.wait_ge(q["out_ps"], NB * l + g + 1)
                        if l == 1 and not first:
                            act.wait_ge(q["tstored"][k], u * 32)
                        nc.scalar.activation(xsT[:, k, 0:P], tp[:, 0:P], ACT.Copy)
                        nc.scalar.activation(xsT[0:V, k, P:2 * P], tp[0:V, P:2 * P], ACT.Copy).then_inc(q["xT"], 1)
                    for k in range(U):
                        if l > 0:
                            nc.scalar.activation(x_all[:, ds(u * U + k, 1), :], xs[:, k:k + 1, :], ACT.Copy)\
                                .then_inc(q["back"], 1)

                rounds(act, NB // U, body)

            publish(0)
            barrier(act, "act")
            for l in range(LAST_LAYER + 1):
                q = sems[l]
                tab = table_of(l)

                def hidden(g):
                    act.wait_ge(q["hid_ps"], g + 2)
                    act.wait_ge(q["w_ready"], g * BT)
                    nc.scalar.activation(hidT[0:FC[l]["h"], :], ps_hid[0:FC[l]["h"], :], FC[l]["act"])\
                        .then_inc(q["hid_ready"], 1)

                if l != 1:
                    act.wait_ge(q["hid_ps"], 2)
                    nc.scalar.activation(hidT[0:FC[l]["h"], :], ps_hid[0:FC[l]["h"], :], FC[l]["act"])\
                        .then_inc(q["hid_ready"], 1)
                act.dma_start(agg_dram[l][0:P, 0:NB], av[:, :]).then_inc(q["agg_stored"], 16)
                with act.Fori(0, NB) as b:
                    n = table_reg(act, tab, 0, b, MAXB)
                    base = table_reg(act, tab, 1, b, MAXB)
                    if l != 1:
                        with act.Fori(0, n) as i:
                            hidden(base + i + 1)
                    act.wait_ge(q["agg_closed"], b + 1)
                    act.wait_ge(q["agg_stored"], b * 16 + 16)
                    if l == 1:
                        nc.scalar.activation(agg_stage[:, 0:512], ps_agg[:, 0:512], ACT.Copy)
                        nc.scalar.activation(agg_stage[:, 512:AW], ps_agg2[:, 0:96], ACT.Copy)\
                            .then_inc(q["agg_out"], 1)
                        w = AW
                    else:
                        w = CNT_COL + 1 if l == 0 else CNT_COL
                        nc.scalar.activation(agg_stage[:, 0:w], ps_agg[:, 0:w], ACT.Copy).then_inc(q["agg_out"], 1)
                    act.wait_ge(q["agg_out"], b + 2)
                    act.dma_start(agg_dram[l][ds(b * P, P), 0:w], agg_stage[:, 0:w]).then_inc(q["agg_stored"], 16)
                act.wait_ge(q["agg_stored"], 16 * NB + 16)
                barrier(act, "act")
                r = nsem
                with act.Fori(0, NB // U) as u:
                    for k in range(U):
                        act.wait_ge(r["aT_ps"], NB * l + u * U + (U if l == 1 else k + 1))
                        act.wait_ge(r["conv_ps"], NB * l + u * U + k + 1)
                        last = chunks(l)[3]
                        nc.scalar.activation(aggT[:, k, 0:384], banks[k][:, 0:384], ACT.Copy)
                        ins = nc.scalar.activation(aggT[0:last, k, 384:512], banks[k][0:last, 384:512], ACT.Copy)
                        if l == 1:
                            bk, c = (7, P * k) if k < 4 else (6, 352)
                            ins = nc.scalar.activation(aggT[0:96, k, 512:640], banks[bk][0:96, c:c + P], ACT.Copy)
                        ins.then_inc(r["aT"], 1)
                if l == 2:
                    act.wait_ge(sin_in, 1)
                    nc.scalar.activation(small[:, 8:10, :], small[:, 6:8, :], ACT.Sin).then_inc(sin_out, 1)
                barrier(act, "act")
                if l == 1:
                    with act.Fori(0, NB) as b:
                        act.wait_ge(bsem["done"], b + 1)
                        act.sem_inc(held_act, 1)
                        nc.scalar.activation(xs[:, 0:1, :], conv_all[:, ds(b, 1), 0:D], ACT.Copy)\
                            .then_inc(bsem["a_slot"], 1)
                        act.wait_ge(bsem["aT_ps"], b + 1)
                        nc.scalar.activation(xsT[0:S, 1, 0:P], banks[0][0:S, 0:P], ACT.Copy).then_inc(bsem["aT"], 1)
                    barrier(act, "act")
                act.wait_ge(r["sqrt_in"], l + 1)
                nc.scalar.activation(small[:, 12, :], small[:, 11, :], ACT.Sqrt).then_inc(r["sqrt_out"], 1)
                if l < LAST_LAYER:
                    publish(l + 1)
                    barrier(act, "act")

        @block.tensor
        def _(pe):
            mm, tr = nc.tensor.matmul, nc.tensor.transpose
            pe.wait_ge(consts, 8)
            pe.wait_ge(ssem["dstf"], 1)
            for c in range(7):
                w = min(P, T - P * c)
                last = tr(banks[1 + c // 4][0:w, P * (c % 4):P * (c % 4) + P], sort_v[:, 4, P * c:P * c + w], ident[:, :])
            last.then_inc(ssem["trows"], 1)
            pe.wait_ge(ssem["tred"], 1)
            tr(banks[3][0:2 * NB, 0:P], rng[:, :], ident[:, :]).then_inc(ssem["t50"], 1)
            pe.wait_ge(ssem["tred2"], 1)
            tr(banks[4][0:1, 0:2 * NB], rng_max[:, 0:1], ident[0:2 * NB, 0:2 * NB]).then_inc(ssem["trow"], 1)
            pe.wait_ge(ssem["cnt"], 1)
            mm(banks[0][:, 0:NB], lower[:, :], small[:, 0, :], start=True, stop=True)
            mm(banks[0][:, NB:2 * NB], ones[:, :], small[:, 0, :], start=True, stop=True).then_inc(ssem["off"], 1)
            barrier(pe, "pe")
            barrier(pe, "pe")

            def publish(l):
                q = psem
                with pe.Fori(0, NB // U) as u:
                    for k in range(U):
                        g = u * U + k
                        tp = banks[5 + k // 2][:, 256 * (k % 2):256 * (k % 2) + 256]
                        pe.wait_ge(q["xs"], NB * l + g + 1)
                        pe.wait_ge(q["xT"], NB * l + u * U + pair_end(k))
                        tr(tp[:, 0:P], xs[:, k, 0:P], ident[:, :])
                        tr(tp[0:V, P:2 * P], xs[:, k, P:D], ident[:, :]).then_inc(q["xT_ps"], 1)
                    for k in range(U):
                        g = u * U + k
                        pe.wait_ge(q["xT"], NB * l + g + 1 + U)
                        pe.wait_ge(q["row"], NB * l + g + 1)
                        o = banks[k][:, 0:2 * D].rearrange("p (j c) -> p j c", j=2)
                        j0 = 1 if l == 1 else 0
                        mm(o[:, j0:2, 0:P], xsT[:, k, 0:P], wa[l][:, j0:2, :], start=True, stop=True)
                        mm(o[:, j0:2, P:D], xsT[0:V, k, P:2 * P], wb[l][:, j0:2, :], start=True, stop=True)\
                            .then_inc(q["out_ps"], 1)

            publish(0)
            barrier(pe, "pe")
            for l in range(LAST_LAYER + 1):
                q = sems[l]
                tab = table_of(l)
                wagg = 512 if l == 1 else (CNT_COL + 1 if l == 0 else CNT_COL)

                def hidden(g):
                    f = FC[l]
                    pe.wait_ge(q["attr_in"], g * 16 + 16)
                    pe.wait_ge(q["hid_ready"], g + 1)
                    mm(ps_hid[0:f["h"], :], w1[l][:, :], attrT[0:f["k"], :], start=True, stop=True)\
                        .then_inc(q["hid_ps"], 1)

                if l != 1:
                    pe.wait_ge(q["attr_in"], 16)
                    mm(ps_hid[0:FC[l]["h"], :], w1[l][:, :], attrT[0:FC[l]["k"], :], start=True, stop=True)\
                        .then_inc(q["hid_ps"], 1)
                with pe.Fori(0, NB) as b:
                    n = table_reg(pe, tab, 0, b, MAXB)
                    base = table_reg(pe, tab, 1, b, MAXB)
                    pe.wait_ge(q["agg_out"], b + 1)
                    mm(ps_agg[:, 0:wagg], zeros_bf[:, 0:P], zeros_bf[:, 0:wagg], start=True, stop=False)
                    if l == 1:
                        mm(ps_agg2[:, 0:96], zeros_bf[:, 0:P], zeros_bf[:, 0:96], start=True, stop=False)
                    with pe.Fori(0, n) as i:
                        g = base + i
                        if l != 1:
                            f = FC[l]
                            pe.wait_ge(q["hid_ready"], g + 2)
                            for j in range(BT):
                                if j % 2 == 0:
                                    pe.wait_ge(q["prod_ready"], g * BT + j + 2)
                                mm(ps_w[j // 2][:, 192 * (j % 2):192 * (j % 2) + 192],
                                   hidT[0:f["h"], P * j:P * j + P], w2[l][:, :], start=True, stop=True)\
                                    .then_inc(q["w_ready"], 1)
                            hidden(g + 1)
                            for j in range(BT):
                                pe.wait_ge(q["prod_ready"], g * BT + j + 1 + BT)
                                pr = prod[:, j, :]
                                mm(ps_agg[:, 0:D], sel[:, j, 0, :], pr[:, 0:D], start=False, stop=False)
                                for m, (c0, step) in enumerate(((0, 64), (64, 32), (64, 64))):
                                    rhs = pr[:, PB + c0:PB + c0 + 3 * step].rearrange("p (a c) -> p a c", c=step)[:, :, 0:32]
                                    last = mm(ps_agg[:, D + 96 * m:D + 96 * m + 96], sel[:, j, 1 + m, :], rhs,
                                              start=False, stop=False)
                                if l == 0:
                                    last = mm(ps_agg[:, CNT_COL:CNT_COL + 1], hot[:, j, :], ones_bf[:, :],
                                              start=False, stop=False)
                                last.then_inc(q["sel_done"], 1)
                        else:
                            for j in range(BT):
                                pe.wait_ge(q["prod_ready"], g * BT + j + 1 + BT)
                                pe.wait_ge(q["got"][j], g * 16 + 16)
                                for s0, w, k, c0 in TP_PARTS:
                                    dst = ps_agg2 if k == 4 else ps_agg
                                    last = mm(dst[:, c0:c0 + w], sel[:, j, k, :], gathered[:, j, s0:s0 + w],
                                              start=False, stop=False)
                                last.then_inc(q["sel_done"], 1)
                    if l == 1:
                        mm(ps_agg2[:, 0:96], zeros_bf[:, 0:P], zeros_bf[:, 0:96], start=False, stop=True)
                    mm(ps_agg[:, 0:wagg], zeros_bf[:, 0:P], zeros_bf[:, 0:wagg], start=False, stop=True)\
                        .then_inc(q["agg_closed"], 1)
                barrier(pe, "pe")
                r = nsem
                ch = chunks(l)
                with pe.Fori(0, NB // U) as u:
                    for k in range(U):
                        g = u * U + k
                        pe.wait_ge(r["in"][k], 16 * (NB // U) * l + u * 16 + 16)
                        pe.wait_ge(r["aT"], NB * l + u * U + (U if l == 1 else k + 1))
                        if l == 1:
                            pe.wait_ge(r["conv"], NB * l + u * U + U)
                        for c, rows in enumerate(ch):
                            bk, c0 = (k, P * c) if c < 4 else ((7, P * k) if k < 4 else (6, 352))
                            last = tr(banks[bk][0:rows, c0:c0 + P], agg_in[:, k, P * c:P * c + rows], ident[:, :])
                        last.then_inc(r["aT_ps"], 1)
                    for k in range(U):
                        g = u * U + k
                        w = D if l == 1 else 161
                        wt = wmsg if l == 1 else wconv[l]
                        pe.wait_ge(r["aT"], NB * l + u * U + (U if l == 1 else k + 1) + U)
                        pe.wait_ge(r["conv"], NB * l + u * U + conv_end(k, l))
                        o = banks[5 + k // 3][:, 161 * (k % 3):161 * (k % 3) + w] if k < 3 else \
                            banks[6][:, 161 * (k - 3):161 * (k - 3) + w]
                        for c, rows in enumerate(ch):
                            last = mm(o, aggT[0:rows, k, P * c:P * c + P], wt[0:rows, c, 0:w],
                                      start=(c == 0), stop=(c == len(ch) - 1))
                        last.then_inc(r["conv_ps"], 1)
                barrier(pe, "pe")
                if l == 1:
                    ring = [banks[i] for i in (1, 2, 3, 4, 5, 6)]
                    with pe.Fori(0, NB) as b:
                        pe.wait_ge(bsem["a_slot"], b + 1)
                        tr(banks[0][:, 0:P], xs[:, 0, 0:P], ident[:, :]).then_inc(bsem["aT_ps"], 1)
                        pe.wait_ge(bsem["xT_in"], b * 32 + 32)
                        for c in range(24):
                            if c < 8:
                                lhs, rhs = xsT[0:S, 0, 0:P], wu_ss[:, 512 * c:512 * c + 512]
                            elif c < 20:
                                i, cc = (c - 8) // 4, (c - 8) % 4
                                if i < 2:
                                    r0 = S + V * i
                                    lhs, rhs = xsT[r0:r0 + V, 0, 0:P], wu_vv[r0:r0 + V, 512 * cc:512 * cc + 512]
                                else:
                                    lhs, rhs = xsT[0:V, 0, P:2 * P], wu_vv[0:V, 512 * cc:512 * cc + 512]
                            elif c < 22:
                                lhs, rhs = xsT[0:S, 0, 0:P], wu_sv[:, 512 * (c - 20):512 * (c - 20) + 512]
                            else:
                                if c == 22:
                                    pe.wait_ge(bsem["aT"], b + 1)
                                lhs, rhs = xsT[0:S, 1, 0:P], wu_vs[:, 512 * (c - 22):512 * (c - 22) + 512]
                            pe.wait_ge(bsem["y_used"], b * 24 + c + 1)
                            mm(ring[c % 6][:, :], lhs, rhs, start=True, stop=True).then_inc(bsem["y_ps"], 1)
                    barrier(pe, "pe")
                if l < LAST_LAYER:
                    publish(l + 1)
                    barrier(pe, "pe")

        @block.vector
        def _(dve):
            v = nc.vector
            for l in FC:
                v.memset(wconv[l][:, :, :], 0.0)
            for l in range(4):
                v.memset(wa[l][:, :, :], 0.0)
            v.memset(wmsg[:, :, :], 0.0).then_inc(w_zero, 1)
            for l in FC:
                for r, (what, _, _) in enumerate(CONV_ROWS):
                    q0 = 32 * (r % 4)
                    v.memset(row_scale[l][q0:q0 + 32, r // 4:r // 4 + 1], FC[l]["cm"] * (R3 if what == "P3" else 1.0))
                v.memset(row_scale[l][64:P, 3:4], 0.0)
            for r, (_, _, _, _, s) in enumerate(msg_rows()):
                q0 = 32 * (r % 4)
                last = v.memset(row_scale[1][q0:q0 + 32, r // 4:r // 4 + 1], s)
            v.memset(row_scale[1][96:P, 4:5], 0.0)
            v.memset(wa_scale[0:S, :], 1 / 8)
            link(v.memset(wa_scale[S:P, :], R32))
            dve.wait_ge(loads, 16 * (5 + len(w_loads)))
            dve.wait_ge(consts, 8)
            v.tensor_scalar(blk128[:, :], blk_id[:, :], float(P), None, ALU.mult)
            for l, f in FC.items():
                v.tensor_scalar(w1[l][:, :], w1[l][:, :], f["c1"], None, ALU.mult)
                v.tensor_scalar(w2[l][:, :], w2[l][:, :], f["c2"], None, ALU.mult)
                for c in range(4):
                    v.tensor_scalar(wconv[l][:, c, :], wconv[l][:, c, :], row_scale[l][:, c:c + 1], None, ALU.mult)
            for c in range(5):
                v.tensor_scalar(wmsg[:, c, :], wmsg[:, c, :], row_scale[1][:, c:c + 1], None, ALU.mult)
            for l in range(4):
                v.tensor_scalar(wa[l][:, :, :], wa[l][:, :, :], wa_scale[:, 0:1], None, ALU.mult)
                v.tensor_scalar(wb[l][:, 0 if l != 1 else 1:2, :], wb[l][:, 0 if l != 1 else 1:2, :], R32, None, ALU.mult)
            v.tensor_scalar(wu_ss[:, :], wu_ss[:, :], 1 / 64, None, ALU.mult)
            for q0, n in ((0, V), (S, V), (S + V, V)):
                v.tensor_scalar(wu_vv[q0:q0 + n, :], wu_vv[q0:q0 + n, :], R3 / 32, None, ALU.mult)
            v.tensor_scalar(wu_sv[:, :], wu_sv[:, :], 1 / math.sqrt(2048.0), None, ALU.mult)
            v.tensor_scalar(wu_vs[:, :], wu_vs[:, :], 1 / math.sqrt(2048.0), None, ALU.mult)
            link(v.memset(zrow[:, :], 0.0))
            for c, n in credits:
                dve.sem_inc(c, n)
            raw_dst = ebuf[:, 0:TA].bitcast(I32)
            link(v.tensor_copy(meta[:, :, 0:4], ebuf[:, TA:5 * TA].rearrange("p (t c) -> p t c", c=4)))
            link(v.tensor_copy(meta[:, :, 4:5], raw_dst.rearrange("p (t c) -> p t c", c=1)))
            link(v.tensor_scalar(blk_i[:, :], raw_dst[:, 0:T], 7, None, ALU.logical_shift_right))
            v.tensor_copy(sort_v[:, 4, :], blk_i[:, :]).then_inc(ssem["dstf"], 1)
            dve.wait_ge(ssem["dstf"], 1)
            link(v.tensor_scalar(blk_i[:, :], srci[:, 0:T], 7, None, ALU.logical_shift_right))
            blk, eq, cum, pos = (sort_v[:, c, :] for c in (0, 1, 2, 3))
            link(v.tensor_copy(blk, blk_i[:, :]))
            dve.wait_ge(ssem["trows"], 1)
            link(v.memset(tile_mm[:, :, :], 30.0))
            link(v.memset(tile_mm[:, 1, :], -1.0))
            for c in range(7):
                w = min(P, T - P * c)
                src = banks[1 + c // 4][0:w, P * (c % 4):P * (c % 4) + P]
                v.tensor_reduce(tile_mm[0:w, 0, c:c + 1], src, AX.X, ALU.min)
                link(v.tensor_reduce(tile_mm[0:w, 1, c:c + 1], src, AX.X, ALU.max))
            bb = blk_id[:, :].unsqueeze(2).broadcast_to([P, NB, 7])
            for r in range(2):
                src = tile_mm[:, r:r + 1, :].broadcast_to([P, NB, 7])
                link(v.tensor_tensor(hit[:, r, :, :], src, bb, (ALU.is_le, ALU.is_ge)[r]))
            link(v.tensor_tensor(hit[:, 0, :, :], hit[:, 0, :, :], hit[:, 1, :, :], ALU.mult))
            v.tensor_scalar(tile_lim[:, 0, :], tile_id[:, :], -1.0, float(T), ALU.mult, ALU.add)
            link(v.tensor_scalar(tile_lim[:, 1, :], tile_id[:, :], 1.0, None, ALU.add))
            for r in (1, 0):
                src = tile_lim[:, r:r + 1, :].broadcast_to([P, NB, 7])
                link(v.tensor_tensor(hit[:, 1, :, :], hit[:, 0, :, :], src, ALU.mult))
                link(v.tensor_reduce(rng[:, NB * r:NB * r + NB], hit[:, 1, :, :], AX.X, ALU.max))
            v.tensor_copy(rng[:, 0:1], rng[:, 0:1]).then_inc(ssem["tred"], 1)
            dve.wait_ge(ssem["t50"], 1)
            v.tensor_reduce(rng_max[:, 0:1], banks[3][0:2 * NB, 0:P], AX.X, ALU.max).then_inc(ssem["tred2"], 1)
            dve.wait_ge(ssem["trow"], 1)
            link(v.tensor_copy(trow[0:1, 0:2, :], banks[4][0:1, 0:2 * NB].rearrange("p (r b) -> p r b", r=2)))
            link(v.tensor_scalar(trow[0:1, 2, :], trow[0:1, 0, :], -1.0, float(T), ALU.mult, ALU.add))
            link(v.tensor_scalar(trow[0:1, 2, :], trow[0:1, 2, :], float(T - BT), None, ALU.min))
            link(v.tensor_tensor(trow[0:1, 3, :], trow[0:1, 1, :], trow[0:1, 2, :], ALU.subtract))

            def finish_table(tab, shift):
                link(v.tensor_scalar(trow[0:1, 3, :], trow[0:1, 3, :], float(2 ** shift - 1), 1.0 * 2 ** shift,
                                     ALU.add, ALU.max))
                link(v.tensor_copy(tri[0:1, :], trow[0:1, 3, :]))
                link(v.tensor_scalar(tab[0:1, 0, :], tri[0:1, :], shift, None, ALU.logical_shift_right))
                link(v.tensor_copy(trow[0:1, 3, :], tab[0:1, 0, :]))
                link(v.tensor_tensor_scan(trow[0:1, 1, :], trow[0:1, 3, :], zrow[0:1, 0:NB], 0.0, ALU.add, ALU.add))
                link(v.tensor_tensor(trow[0:1, 1, :], trow[0:1, 1, :], trow[0:1, 3, :], ALU.subtract))
                link(v.tensor_copy(tab[0:1, 1, :], trow[0:1, 1, :]))
                link(v.tensor_copy(tab[0:1, 2, :], trow[0:1, 2, :]))

            finish_table(tab_i["dst"], 2)
            link(v.memset(pos, 0.0))
            with dve.Fori(0, NB) as b:
                c0 = small[:, 0, ds(b, 1)]
                v.tensor_scalar(eq, blk, blk_id[:, ds(b, 1)], None, ALU.is_equal).then_inc(srt, 1)
                dve.wait_ge(srt, b * 5 + 1)
                v.tensor_tensor_scan(cum, eq, zrow[:, :], 0.0, ALU.add, ALU.add).then_inc(srt, 1)
                dve.wait_ge(srt, b * 5 + 2)
                v.tensor_scalar(c0, cum[:, T - 1:T], 1.0, None, ALU.mult).then_inc(srt, 1)
                dve.wait_ge(srt, b * 5 + 3)
                v.tensor_tensor(cum, cum, eq, ALU.mult).then_inc(srt, 1)
                dve.wait_ge(srt, b * 5 + 4)
                v.tensor_tensor(pos, pos, cum, ALU.add).then_inc(srt, 1)
                dve.wait_ge(srt, b * 5 + 5)
            v.tensor_copy(small[:, 1, :], small[:, 0, :]).then_inc(ssem["cnt"], 1)
            dve.wait_ge(ssem["off"], 1)
            link(v.tensor_copy(small[:, 2, :], banks[0][:, NB:2 * NB]))
            link(v.tensor_tensor_scan(small[:, 3, :], small[:, 2, :], zrow[:, 0:NB], 0.0, ALU.add, ALU.add))
            link(v.tensor_tensor(small[:, 3, :], small[:, 3, :], small[:, 2, :], ALU.subtract))
            link(v.tensor_tensor(small[:, 4, :], small[:, 3, :], banks[0][:, 0:NB], ALU.add))
            link(v.tensor_scalar(small[:, 4, :], small[:, 4, :], -1.0, None, ALU.add))
            link(v.tensor_copy(trow[0:1, 2, :], small[0:1, 3, :]))
            link(v.tensor_copy(trow[0:1, 3, :], small[0:1, 2, :]))
            finish_table(tab_i["src"], 9)
            with dve.Fori(0, NB) as b:
                v.tensor_scalar(eq, blk, blk_id[:, ds(b, 1)], small[:, 4, ds(b, 1)], ALU.is_equal, ALU.mult)\
                    .then_inc(srt2, 1)
                dve.wait_ge(srt2, b * 2 + 1)
                v.tensor_tensor(pos, pos, eq, ALU.add).then_inc(srt2, 1)
                dve.wait_ge(srt2, b * 2 + 2)
            barrier(dve, "dve")
            link(v.memset(scat_rec[:, :, :, :], 0.0))

            def fill(i, first):
                for h in range(2):
                    if not first:
                        for j in range(8):
                            dve.wait_ge(sc_done[h][j], i * 16)
                    t0 = i * 16 + 8 * h
                    v.tensor_scalar(scat_rec[:, h, :, 2:6], meta[:, ds(t0, 8), 0:4], 1.0, None, ALU.mult)
                    v.tensor_scalar(scat_rec[:, h, :, 0:1].bitcast(I32), meta[:, ds(t0, 8), 4:5], 1.0, None, ALU.mult)
                    v.tensor_scalar(scat_rec[:, h, :, 1], srci[:, ds(t0, 8)], 1.0, None, ALU.mult)
                    v.tensor_scalar(scat_idx[:, h, :], pos[:, ds(t0, 8)], 1.0, None, ALU.mult).then_inc(sc_slot[h], 1)

            rounds(dve, T // 16, fill)
            barrier(dve, "dve")

            def publish(l):
                q = psem

                def body(u, first):
                    for k in range(U):
                        g = u * U + k
                        dve.wait_ge(q["xT_ps"], NB * l + g + 1)
                        if l == 0:
                            ins = v.tensor_scalar(xs[:, k:k + 1, :], x_all[:, ds(g, 1), :], 1.0, None, ALU.mult)
                        else:
                            dve.wait_ge(q["back"], NB * (l - 1) + g + 1)
                            if l == 1:
                                dve.wait_ge(q["row"], NB * l + g + 1)
                            ins = v.tensor_scalar(xs[:, k:k + 1, :], x_all[:, ds(g, 1), :], small[:, 14, ds(g, 1)],
                                                  small[:, 13, ds(g, 1)], ALU.subtract, ALU.mult)
                        ins.then_inc(q["xs"], 1)
                    for k in range(U):
                        g = u * U + k
                        dve.wait_ge(q["out_ps"], NB * l + g + 1 + U)
                        if not first:
                            dve.wait_ge(q["stored"][k], 16 * (NB // U) * l + u * 16)
                        if l == 1:
                            dve.wait_ge(q["xs"], NB * l + g + 1)
                            row = row_out[:, k, :]
                            v.tensor_scalar(row[:, 32:96], xs[:, k, 0:S], 1.0, None, ALU.mult)
                            v.tensor_scalar(row[:, 160:224], xs[:, k, 0:S], 1.0, None, ALU.mult)
                            v.tensor_scalar(row[:, 0:32], xs[:, k, S + V:S + 2 * V], 1.0, None, ALU.mult)
                            v.tensor_scalar(row[:, 96:128], xs[:, k, S:S + V], 1.0, None, ALU.mult)
                            v.tensor_scalar(row[:, 128:160], xs[:, k, S + 2 * V:D], 1.0, None, ALU.mult)
                        else:
                            v.tensor_scalar(row_out[:, k, 0:D], banks[k][:, 0:D], av[:, ds(g, 1)], None, ALU.mult)
                        v.tensor_scalar(self_all[:, ds(g, 1), :], banks[k][:, D:2 * D].unsqueeze(1), 1.0, None,
                                        ALU.mult).then_inc(q["row"], 1)

                rounds(dve, NB // U, body)

            def select(l, j, g):
                dve.wait_ge(sems[l]["sel_done"], g * BT + j + 1)
                node = meta_slot[:, j, 4:5]
                ks = [(1, 3), (2, 0), (3, 1), (4, 2)] if l == 1 else [(0, 0), (1, 1), (2, 2), (3, 3)]
                if l == 1:
                    last = v.tensor_scalar(sel[:, j, 0, :], node_id[:, :], node, None, ALU.is_equal)
                if l == 0:
                    v.tensor_scalar(hot[:, j, :], node_id[:, :], node, None, ALU.is_equal)
                for k, c in ks:
                    last = v.tensor_scalar(sel[:, j, k, :], node_id[:, :], node, meta_slot[:, j, c:c + 1],
                                           ALU.is_equal, ALU.mult)
                return last

            def bilinear():
                tt = bil
                b2 = bsem

                def summed(dst, src):
                    return v.tensor_reduce(dst, src, AX.X, ALU.add)

                with dve.Fori(0, NB) as b:
                    n0 = b * 24
                    a = xs[:, 0, :]
                    x = xs[:, 1, :]
                    dve.wait_ge(b2["done"], b + 1)
                    v.tensor_scalar(xs[:, 1:2, :], x_all[:, ds(b, 1), :], 1.0, None, ALU.mult).then_inc(bil_own, 1)
                    dve.wait_ge(b2["a_slot"], b + 1)
                    for c in range(20):
                        cc = c % 10
                        dve.wait_ge(b2["y_ps"], n0 + c + 1)
                        ins = v.tensor_tensor(
                            tt[:, 512 * cc:512 * cc + 512].rearrange("p (r w) -> p r w", w=S),
                            banks[1 + c % 6][:, :].rearrange("p (r w) -> p r w", w=S),
                            a[:, 8 * c:8 * c + 8].unsqueeze(2).broadcast_to([P, 8, S]), ALU.mult)
                        ins.then_inc(b2["y_used"], 1)
                        if cc == 9:
                            dve.wait_ge(b2["y_used"], n0 + c + 7)
                            summed(upd[:, c // 10, 0:S], tt[:, :].rearrange("p (r w) -> p w r", w=S))\
                                .then_inc(bil_own, 1)
                            dve.wait_ge(bil_own, b * 9 + 2 + c // 10)
                    for c in range(4):
                        dve.wait_ge(b2["y_ps"], n0 + 21 + c)
                    for i in range(3):
                        for c in range(4):
                            mul = a[:, S + V * i + 16 * c:S + V * i + 16 * c + 16] if c < 2 else \
                                x[:, S + V * i + 16 * (c - 2):S + V * i + 16 * (c - 2) + 16]
                            last = v.tensor_tensor(
                                tt[:, 512 * c:512 * c + 512].rearrange("p (r w) -> p r w", w=V),
                                banks[1 + (20 + c) % 6][:, :].rearrange("p (r w) -> p r w", w=V),
                                mul.unsqueeze(2).broadcast_to([P, 16, V]), ALU.mult)
                        last.then_inc(bil_own, 1)
                        dve.wait_ge(bil_own, b * 9 + 4 + 2 * i)
                        summed(upd[:, 2 + i, 0:V], tt[:, 0:2048].rearrange("p (r w) -> p w r", w=V))\
                            .then_inc(bil_own, 1)
                        dve.wait_ge(bil_own, b * 9 + 5 + 2 * i)
                    for c in range(4):
                        dve.sem_inc(b2["y_used"], 1)
                    link2(v.tensor_tensor(upd[:, 0, 0:S], upd[:, 0, 0:S], upd[:, 1, 0:S], ALU.add), b, 0)
                    v.scalar_tensor_tensor(x[:, 0:S], x[:, 0:S], 2.0, upd[:, 0, 0:S], ALU.mult, ALU.add)
                    link2(v.scalar_tensor_tensor(x[:, S:D].rearrange("p (i c) -> p i c", i=3),
                                                 x[:, S:D].rearrange("p (i c) -> p i c", i=3), 2.0,
                                                 upd[:, 2:5, 0:V], ALU.mult, ALU.add), b, 1)
                    v.tensor_tensor(x_all[:, ds(b, 1), :], xs[:, 1:2, :], self_all[:, ds(b, 1), :], ALU.add)\
                        .then_inc(b2["done"], 1)

            publish(0)
            barrier(dve, "dve")
            for l in range(LAST_LAYER + 1):
                q = sems[l]
                tab = table_of(l)
                with dve.Fori(0, NB) as b:
                    n = table_reg(dve, tab, 0, b, MAXB)
                    base = table_reg(dve, tab, 1, b, MAXB)
                    start = table_reg(dve, tab, 2, b, NREC)
                    dve.wait_ge(q["prod_ready"], base * BT + BT)
                    v.tensor_scalar(node_id[:, :], iota[:, :], blk128[:, ds(b, 1)], None, ALU.add)\
                        .then_inc(q["node_ids"], 1)
                    dve.wait_ge(q["node_ids"], b + 1)
                    dve.sem_inc(held_dve, 1)
                    with dve.Fori(0, n) as i:
                        g = base + i
                        if l == 1:
                            dve.wait_ge(q["rec_in"], g * 16 + 16)
                            dve.wait_ge(q["idx_ready"], g * BT + BT)
                            dve.wait_ge(q["prod_ready"], g * BT + BT)
                            v.tensor_copy(rec_idx[:, :], rec_slot[:, :, 0].bitcast(I32))
                            v.tensor_copy(meta_slot[:, :, 4], rec_slot[:, :, 1])
                            v.tensor_copy(meta_slot[:, :, 0:4], rec_slot[:, :, 2:6]).then_inc(q["meta_ready"], 1)
                            dve.wait_ge(q["meta_ready"], g + 2)
                            for j in range(BT):
                                select(l, j, g).then_inc(q["prod_ready"], 1)
                        else:
                            dve.wait_ge(q["prod_ready"], g * BT + BT)
                            v.tensor_scalar(meta_slot[:, :, :], meta[:, ds(bounded(start + i * BT, T - 1), BT), :], 1.0, None,
                                            ALU.mult).then_inc(q["meta_ready"], 1)
                            dve.wait_ge(q["meta_ready"], g + 2)
                            for j in range(BT):
                                select(l, j, g)
                                dve.wait_ge(q["got"][j], g * 16 + 16)
                                dve.wait_ge(q["w_ready"], g * BT + j // 2 * 2 + 2)
                                w = ps_w[j // 2][:, 192 * (j % 2):192 * (j % 2) + 192]
                                e = gathered[:, j, :]
                                vec = e[:, S:D].rearrange("p (m c) -> p m c", c=V)

                                def over_m(c):
                                    return w[:, c:c + V].unsqueeze(1).broadcast_to([P, 3, V])

                                v.tensor_tensor(
                                    prod[:, j, 0:384].rearrange("p (a c) -> p a c", a=2)[:, :, 32:160]
                                    .rearrange("p a (h c) -> p a h c", h=2)[:, :, :, 0:32],
                                    w[:, 0:128].rearrange("p (a h c) -> p a h c", a=2, h=2),
                                    e[:, 0:S].rearrange("p (h c) -> p h c", h=2).unsqueeze(1)
                                    .broadcast_to([P, 2, 2, 32]), ALU.mult)
                                v.tensor_tensor(
                                    prod[:, j, 0:192].rearrange("p (m c) -> p m c", m=3)[:, :, 0:32],
                                    over_m(128), vec, ALU.mult)
                                v.tensor_tensor(
                                    prod[:, j, PB:PB + 288].rearrange("p (m c) -> p m c", m=3)[:, :, 0:32],
                                    over_m(160), vec, ALU.mult).then_inc(q["prod_ready"], 1)
                barrier(dve, "dve")
                r = nsem
                w = D if l == 1 else 161
                with dve.Fori(0, NB // U) as u:
                    for k in range(U):
                        g = u * U + k
                        dve.wait_ge(r["conv_ps"], NB * l + u * U + conv_end(k, l) + U)
                        o = banks[5][:, 161 * k:161 * k + w] if k < 3 else banks[6][:, 161 * (k - 3):161 * (k - 3) + w]
                        if l == 0:
                            v.tensor_scalar(conv_all[:, ds(g, 1), 161:162],
                                            agg_in[:, k:k + 1, CNT_COL:CNT_COL + 1], 1.0, None, ALU.mult)
                        v.tensor_scalar(conv_all[:, ds(g, 1), 0:w], o.unsqueeze(1), 1.0, None, ALU.mult)\
                            .then_inc(r["conv"], 1)
                sm = lambda c: small[:, c, :]
                if l != 1:
                    dve.wait_ge(r["conv"], NB * (l + 1) + U)
                    gate = conv_all[:, :, 160]
                    if l == 0:
                        link(v.tensor_scalar(sm(2), conv_all[:, :, 161], 1.0, None, ALU.max))
                        link(v.reciprocal(sm(3), sm(2)))
                        link(v.tensor_tensor(sm(3), sm(3), av[:, :], ALU.mult))
                        link(v.tensor_tensor(sm(4), sm(3), sm(3), ALU.mult))
                        link(v.tensor_tensor(sm(1), sm(4), gate, ALU.mult))
                        link(v.tensor_copy(sm(0), av[:, :]))
                    elif l == 2:
                        link(v.scalar_tensor_tensor(sm(2), gate, 0.1, av[:, :], ALU.mult, ALU.mult))
                        link(v.tensor_scalar(sm(3), sm(2), 1 / (2 * math.pi), ROUND, ALU.mult, ALU.add))
                        link(v.tensor_scalar(sm(3), sm(3), -ROUND, None, ALU.add))
                        for part in TWO_PI:
                            link(v.scalar_tensor_tensor(sm(2), sm(3), -part, sm(2), ALU.mult, ALU.add))
                        link(v.tensor_scalar(sm(6), sm(2), 3.1415925, -3.1415925, ALU.min, ALU.max))
                        v.tensor_scalar(sm(7), sm(6), 0.5, None, ALU.mult).then_inc(sin_in, 1)
                        dve.wait_ge(sin_out, 1)
                        link(v.tensor_tensor(sm(1), sm(8), av[:, :], ALU.mult))
                        link(v.tensor_tensor(sm(3), sm(9), sm(9), ALU.mult))
                        link(v.tensor_scalar(sm(3), sm(3), -2.0, 1.0, ALU.mult, ALU.add))
                        link(v.tensor_tensor(sm(0), sm(3), av[:, :], ALU.mult))
                    else:
                        v.tensor_copy(sm(1), av[:, :])
                        link(v.tensor_copy(sm(0), av[:, :]))
                    v.tensor_tensor(self_all[:, :, :], self_all[:, :, :],
                                    sm(0).unsqueeze(2).broadcast_to([P, NB, D]), ALU.mult)
                    link(v.tensor_tensor(conv_all[:, :, 0:D], conv_all[:, :, 0:D],
                                         sm(1).unsqueeze(2).broadcast_to([P, NB, D]), ALU.mult))
                    link(v.tensor_tensor(x_all[:, :, :], x_all[:, :, :], self_all[:, :, :], ALU.add))
                    link(v.tensor_tensor(x_all[:, :, :], x_all[:, :, :], conv_all[:, :, 0:D], ALU.add))
                barrier(dve, "dve")
                if l == 1:
                    bilinear()
                    barrier(dve, "dve")
                with dve.Fori(0, NB // U) as u:
                    for k in range(U):
                        v.bn_stats(stats[:, ds(u * U + k, 1), :], x_all[:, ds(u * U + k, 1), :])\
                            .then_inc(stats_sem, 1)
                dve.wait_ge(stats_sem, NB * (l + 1))
                me, qe, mo, qo = (stats[:, :, c] for c in (1, 2, 4, 5))
                link(v.tensor_tensor(sm(14), me, mo, ALU.add))
                link(v.tensor_scalar(sm(14), sm(14), 0.5, None, ALU.mult))
                link(v.tensor_tensor(sm(10), me, mo, ALU.subtract))
                link(v.scalar_tensor_tensor(sm(10), sm(10), 0.25, sm(10), ALU.mult, ALU.mult))
                link(v.tensor_tensor(sm(11), qe, qo, ALU.add))
                link(v.scalar_tensor_tensor(sm(11), sm(11), 1 / D, sm(10), ALU.mult, ALU.add))
                v.tensor_scalar(sm(11), sm(11), EPS, None, ALU.add).then_inc(r["sqrt_in"], 1)
                dve.wait_ge(r["sqrt_out"], l + 1)
                link(v.reciprocal(sm(13), sm(12)))
                if l < LAST_LAYER:
                    publish(l + 1)
                    barrier(dve, "dve")
            with dve.Fori(0, NB // U) as u:
                for k in range(U):
                    g = u * U + k
                    v.tensor_scalar(x_all[:, ds(g, 1), :], x_all[:, ds(g, 1), :], small[:, 14, ds(g, 1)],
                                    small[:, 13, ds(g, 1)], ALU.subtract, ALU.mult).then_inc(final, 1)



def _component_major(x):
    import numpy as np
    n = x.shape[0]
    return np.concatenate([x[:, :S], x[:, S:].reshape(n, V, 3).transpose(0, 2, 1).reshape(n, 3 * V)], axis=1)


def _layout(inputs):
    import numpy as np
    i = {k: np.asarray(a) for k, a in inputs.items()}
    f = np.float32

    def tiles(a, fill):
        a = a.reshape(E, -1)
        p = np.full((EA, a.shape[1]), fill, a.dtype)
        p[:E] = a
        return p.reshape(TA, P, -1).transpose(1, 0, 2).reshape(P, -1)

    def wide(a):
        p = np.zeros((a.shape[1], EA), f)
        p[:, :E] = a.T
        return p

    x = np.zeros((NB * P, D), f)
    x[:N] = _component_major(i["x"])
    a = np.zeros((NB * P,), f)
    a[:N] = i["node_vec1"][:, 0]
    o = {
        "x_in": x, "a_t": a.reshape(NB, P).T,
        "src_t": tiles(i["src"], PAD_SRC), "dst_t": tiles(i["dst"], PAD_DST),
        "attr4_t": tiles(i["edge_attr_4"], 0),
        "a16T": wide(i["edge_attr_16"]), "a8T": wide(i["edge_attr_8"]), "a10T": wide(i["edge_attr_10"]),
        "wu_ss": i["L1_gnn_Wu_ss"].reshape(S, S * S), "wu_vv": i["L1_gnn_Wu_vv"].reshape(V, V * S),
        "wu_sv": i["L1_gnn_Wu_sv"].reshape(S, V * V),
        "wu_vs": i["L1_gnn_Wu_vs"].transpose(1, 0, 2).reshape(S, V * V),
    }
    for k, w in i.items():
        if k.startswith("L") and "Wu_" not in k:
            o[k] = w
    return {k: np.ascontiguousarray(w) for k, w in o.items()}


def kernel(**inputs):
    import numpy as _np
    import concourse.bacc as _bacc
    from concourse import mybir as _mybir
    from concourse.bass_utils import run_bass_kernel_spmd as _run

    nc = _bacc.Bacc("TRN2", target_bir_lowering=False, num_devices=1)
    arrays, args = {}, {}
    for name, a in _layout(inputs).items():
        arrays[f"in_{name}"] = a
        args[name] = nc.dram_tensor(f"in_{name}", a.shape, _mybir.dt.from_np(a.dtype), kind="ExternalInput").ap()
    out = nc.dram_tensor("out_x", (NB * P, D), _mybir.dt.float32, kind="ExternalOutput").ap()
    gnn_kernel(nc, args, out)
    y = _run(nc, [arrays], core_ids=[0]).results[0]["out_x"][:N]
    vec = y[:, S:].reshape(N, 3, V).transpose(0, 2, 1).reshape(N, 3 * V)
    return _np.concatenate([y[:, :S], vec], axis=1)
```

```python
from contextlib import ExitStack
import math

import concourse.bass as bass
from concourse import mybir

F32 = mybir.dt.float32
BF16 = mybir.dt.bfloat16
I32 = mybir.dt.int32
ALU = mybir.AluOpType
ACT = mybir.ActivationFunctionType
AX = mybir.AxisListType
ds = bass.ds

P = 128
N = 3125
NB = 25
E = 103125
T = 816
TA = 832
EA = TA * P
BT = 4
S, V, D = 64, 32, 160
EPS = 1e-5
PAD_DST = NB * P + P - 1
PAD_SRC = NB * P - 1
TWO_PI = (6.28125, 2029 / 2.0 ** 20, 2 * math.pi - 6.28125 - 2029 / 2.0 ** 20)
ROUND = 1.5 * 2.0 ** 23
U = 5
WX = 224
NREC = T * P + BT * P
AW = 608
CW = 162
GSS, GVV = 8, 6
NG = GSS + GVV
LAST_LAYER = 3

R96, R32, R3 = 1 / math.sqrt(96.0), 1 / math.sqrt(32.0), 1 / math.sqrt(3.0)

FC = {
    0: dict(attr="a16T", k=16, h=64, c1=1 / 4.0, c2=1 / 8.0, act=ACT.Silu, cm=R96),
    2: dict(attr="a8T", k=8, h=64, c1=1 / math.sqrt(8.0), c2=1 / 8.0, act=ACT.Silu, cm=R96 / 4.0),
    3: dict(attr="a10T", k=10, h=100, c1=1 / math.sqrt(10.0), c2=math.sqrt(2.0) / 10.0, act=ACT.Relu,
            cm=R96 / 4.0 * 0.5),
}
W_FC = {0: ("L0_gnn_Wfc1", "L0_gnn_Wfc2"), 2: ("L2_gnn_fc_w1", "L2_gnn_fc_w2"), 3: ("L3_gnn_W_fc1", "L3_gnn_W_fc2")}
W_LIN = {0: ("L0_gnn_Wl1_0", "L0_gnn_Wl1_1"), 2: ("L2_gnn_lin1_w0", "L2_gnn_lin1_w1"),
         3: ("L3_gnn_W_l1_0", "L3_gnn_W_l1_1")}
W_SELF = {0: ("L0_gnn_Wsc0", "L0_gnn_Wsc1"), 1: ("L1_gnn_Lu_s", "L1_gnn_Lu_v"),
          2: ("L2_gnn_sc_w0", "L2_gnn_sc_w1"), 3: ("L3_gnn_W_si0", "L3_gnn_W_si1")}

CONV_ROWS = [("P0", h, 0) for h in range(2)] + [("P1", h, i) for i in range(3) for h in range(2)] \
    + [("P2", m, 0) for m in range(3)] + [("P3", m, 0) for m in range(3)]
CNT_COL = 32 * len(CONV_ROWS)
MW = CNT_COL + 4
WW = S + V
TP_PARTS = [(0, D, 0, 0), (0, D, 1, 160), (32, 96, 2, 320), (0, 96, 3, 416), (128, 96, 4, 0)]


def msg_rows():
    order = [("v", 1), ("s", 0), ("s", 1), ("v", 0), ("v", 2)]
    rows = []
    for kind, m in order:
        rows.append(("Lm_s", m, 0, S, 1 / 8) if kind == "s" else ("Lm_v", 0, S + V * m, V, R32))
    for kind, m in order:
        rows.append(("Wm_ss", m, 0, S, 1 / 8) if kind == "s" else ("Wm_vs", 0, S + V * m, V, R32))
    for i, part in ((0, "ssv"), (1, "vss"), (2, "vss")):
        half = 0
        for kind in part:
            if kind == "s":
                rows.append(("Wm_sv", half, S + V * i, V, 1 / 8))
                half += 1
            else:
                rows.append(("Wm_vv", 0, 0, S, R3 * R32))
    return rows


def gnn_kernel(nc, A, out):
    ctx = ExitStack()
    with ctx:
        def sb(name, shape, dt=F32):
            return ctx.enter_context(nc.sbuf_tensor(name, shape, dt))

        def sem(name):
            return ctx.enter_context(nc.semaphore(name))

        def scratch(name, shape, dt=F32):
            return nc.dram_tensor(name, shape, dt, kind="Internal").ap()

        table = {l: scratch(f"table{l}", (NB * P, D)) for l in (0, 2, 3)}
        table[1] = scratch("table1", ((NB + 1) * P, WX))
        agg_dram = {l: scratch(f"agg{l}", (NB * P, AW)) for l in range(4)}
        rec_dram = scratch("records", (NREC, 8))

        ident = sb("ident", [P, P])
        lower = sb("lower", [P, P])
        ones = sb("ones", [P, P])
        zeros_bf = sb("zeros_bf", [P, 512], BF16)
        iota = sb("iota", [P, P])
        blk_id = sb("blk_id", [P, NB])
        tile_id = sb("tile_id", [P, 7])
        node_id = sb("node_id", [P, P])
        av = sb("av", [P, NB])
        meta = sb("meta", [P, TA, 5])
        srci = sb("srci", [P, TA], I32)
        x_all = sb("x_all", [P, NB, D])
        self_all = sb("self_all", [P, NB, D])
        conv_all = sb("conv_all", [P, NB, CW])
        ebuf = sb("ebuf", [P, 5248])
        agg_in = sb("agg_in", [P, U, AW])
        aggT = sb("aggT", [P, U, 5 * P])
        idx_slot = sb("idx_slot", [P, BT], I32)
        meta_slot = sb("meta_slot", [P, BT, 5])
        dst_slot = sb("dst_slot", [P, BT])
        sh_slot = sb("sh_slot", [P, BT, 4])
        rec_slot = sb("rec_slot", [P, BT, 8])
        attrT = sb("attrT", [P, BT * P])
        hidT = sb("hidT", [P, BT * P])
        agg_stage = sb("agg_stage", [P, AW])
        xs = sb("xs", [P, U, D])
        xsT = sb("xsT", [P, U, 2 * P])
        row_out = sb("row_out", [P, U, WX])
        small = sb("small", [P, 16, NB])
        stats = sb("stats", [P, NB, 6])
        tab_i = {l: sb(f"tab_{l}", [1, 3, NB], I32) for l in ("dst", "src")}

        gathered = ebuf[:, 0:BT * WX].rearrange("p (j c) -> p j c", j=BT)
        o0 = BT * WX
        sel = ebuf[:, o0:o0 + BT * 5 * P].rearrange("p (j k n) -> p j k n", j=BT, k=5)
        msg = ebuf[:, o0:o0 + BT * MW].rearrange("p (j c) -> p j c", j=BT)
        o1 = o0 + BT * MW
        wsh = ebuf[:, o1:o1 + BT * 4 * WW].rearrange("p (j k c) -> p j k c", j=BT, k=4)
        o2 = o1 + BT * 4 * WW
        hot = ebuf[:, o2:o2 + BT * P].rearrange("p (j n) -> p j n", j=BT)
        zs = ebuf[:, 0:4 * 1024].rearrange("p (k c) -> p k c", k=4)
        zT = ebuf[:, 4 * 1024:5 * 1024].rearrange("p (h c) -> p h c", h=2)
        zv = aggT[:, :, :].rearrange("p k c -> p (k c)")[:, 0:3 * 1024].rearrange("p (i c) -> p i c", i=3)
        tt = agg_in[:, :, :].rearrange("p k c -> p (k c)")[:, 0:2048]
        sort_v = ebuf[:, 0:5 * T].rearrange("p (c t) -> p c t", c=5)
        blk_i = ebuf[:, 5 * T:6 * T].bitcast(I32)

        w1 = {l: sb(f"w1_{l}", [P, f["h"]]) for l, f in FC.items()}
        w2 = {l: sb(f"w2_{l}", [P, 2 * WW]) for l, f in FC.items()}
        wconv = {l: sb(f"wconv_{l}", [P, 4, 161]) for l in FC}
        wmsg = sb("wmsg", [P, 5, D])
        wa = {l: sb(f"wa_{l}", [P, 2, P]) for l in range(4)}
        wb = {l: sb(f"wb_{l}", [V, 2, V]) for l in range(4)}
        wu_ss = sb("wu_ss", [P, GSS * 4, S])
        wu_vv = sb("wu_vv", [P, 8, S])
        wu_sv = sb("wu_sv", [S, V * V])
        wu_vs = sb("wu_vs", [S, V * V])
        upd = sb("upd", [P, 2, D])
        row_scale = {l: sb(f"row_scale{l}", [P, 5]) for l in range(4)}
        wa_scale = sb("wa_scale", [P, 1])
        blk128 = sb("blk128", [P, NB])
        tile_mm = sb("tile_mm", [P, 2, 7])
        tile_lim = sb("tile_lim", [P, 2, 7])
        hit = sb("hit", [P, 2, NB, 7])
        rng = sb("rng", [P, 2 * NB])
        rng_max = sb("rng_max", [2 * NB, 1])
        trow = sb("trow", [1, 4, NB])
        tri = sb("tri", [1, NB], I32)
        zrow = sb("zrow", [P, T])
        rec_idx = sb("rec_idx", [P, BT], I32)
        scat_rec = sb("scat_rec", [P, 2, 8, 8])
        scat_idx = sb("scat_idx", [P, 2, 8], I32)

        banks = [ctx.enter_context(nc.psum_tensor(f"bank{i}", [P, 512], F32)) for i in range(8)]
        ps_hid, ps_w, ps_agg, ps_agg2 = banks[0], banks[1:3], banks[3], banks[4]

        bar = sem("bar")
        w_zero, loads, wscaled = sem("w_zero"), sem("loads"), sem("wscaled")
        consts = sem("consts")
        held_act, held_dve = sem("held_act"), sem("held_dve")
        go = sem("go")
        vch = sem("vch")
        pch = sem("pch")
        out_done = sem("out_done")
        init_done = sem("init_done")

        bars = {}

        def barrier(eng, name):
            k = bars.get(name, 0) + 1
            bars[name] = k
            eng.drain().then_inc(bar, 1)
            eng.wait_ge(bar, 5 * k)

        chain = [0]

        def link(ins):
            chain[0] += 1
            ins.then_inc(vch, 1)
            nc.vector.wait_ge(vch, chain[0])

        block = ctx.enter_context(nc.Block())

        w_loads = []
        for l, f in FC.items():
            w_loads += [(w1[l][0:f["k"], :], A[W_FC[l][0]])]
            for c0, src0, n in ((0, 0, S), (S, 2 * S, V), (WW, S, S), (WW + S, 2 * S + V, V)):
                w_loads.append((w2[l][0:f["h"], c0:c0 + n], A[W_FC[l][1]][:, src0:src0 + n]))
            w_loads += [(wa[l][0:S, 0, 0:S], A[W_LIN[l][0]]), (wb[l][:, 0, :], A[W_LIN[l][1]])]
            w_loads += [(wa[l][S + V * m:S + V * m + V, 0, S + V * m:S + V * m + V], A[W_LIN[l][1]]) for m in (0, 1)]
            for r, (what, h, i) in enumerate(CONV_ROWS):
                q, c = 32 * (r % 4), r // 4
                dst = wconv[l][q:q + 32, c, :]
                if l == 0:
                    ws, wv, wg = A["L0_gnn_Wl2_s"], A["L0_gnn_Wl2_v"], A["L0_gnn_Wa"]
                    ws, wv = [ws[0:32], ws[32:64], ws[64:96]], [wv[0:32], wv[32:64], wv[64:96]]
                elif l == 2:
                    ws, wv, wg = A["L2_gnn_lin2_w0"], A["L2_gnn_lin2_w1"], A["L2_gnn_lin3_w"]
                    ws, wv = [ws[0:32], ws[32:64], ws[64:96]], [wv[0:32], wv[32:64], wv[64:96]]
                else:
                    ws = [A["L3_gnn_W_l2_00"][0:32], A["L3_gnn_W_l2_00"][32:64], A["L3_gnn_W_l2_10"]]
                    wv = [A["L3_gnn_W_l2_01"][0:32], A["L3_gnn_W_l2_01"][32:64], A["L3_gnn_W_l2_11"]]
                    wg = None
                if what in ("P0", "P3"):
                    part = h if what == "P0" else 2
                    w_loads.append((dst[:, 0:S], ws[part]))
                    if wg is not None:
                        w_loads.append((dst[:, D:D + 1], wg[32 * part:32 * part + 32, :]))
                else:
                    part, m = (h, i) if what == "P1" else (2, h)
                    w_loads.append((dst[:, S + V * m:S + V * m + V], wv[part]))
        for l, (w0, w1n) in W_SELF.items():
            w_loads += [(wa[l][0:S, 1, 0:S], A[w0]), (wb[l][:, 1, :], A[w1n])]
            w_loads += [(wa[l][S + V * m:S + V * m + V, 1, S + V * m:S + V * m + V], A[w1n]) for m in (0, 1)]
        for r, (name, h, c0, cn, _) in enumerate(msg_rows()):
            w_loads.append((wmsg[32 * (r % 4):32 * (r % 4) + 32, r // 4, c0:c0 + cn],
                            A["L1_gnn_" + name][32 * h:32 * h + 32, :]))
        w_loads += [(wu_ss[:, :, :], A["wu_ss"].rearrange("(c p) w -> p c w", p=P)),
                    (wu_vv[:, :, :], A["wu_vv"].rearrange("(c p) w -> p c w", p=P)), (wu_sv[:, :], A["wu_sv"]), (wu_vs[:, :], A["wu_vs"])]
        half = len(w_loads) // 2

        both = ("prod_ready", "sel_done", "meta_ready", "idx_ready", "agg_closed", "agg_out", "agg_stored",
                "node_ids")
        sems = {}
        for l in range(4):
            names = both + (("rec_in", "rec_idx", "hot_ready", "act_sel") if l == 1 else ("attr_in", "hid_ps", "hid_ready", "w_ready", "wsh_ready", "sh_ready"))
            sems[l] = {n: sem(f"{n}_{l}") for n in names}
            sems[l]["got"] = [sem(f"got{j}_{l}") for j in range(BT)]
        nsem = {n: sem("n_" + n) for n in ("aT_ps", "aT", "conv_ps", "conv", "sqrt_in", "sqrt_out")}
        nsem["in"] = [sem(f"n_in{k}") for k in range(U)]
        psem = {n: sem("p_" + n) for n in ("xs", "xT_ps", "xT", "out_ps", "row", "back")}
        psem["stored"] = [sem(f"p_stored{k}") for k in range(U)]
        bsem = {n: sem("b_" + n) for n in ("ax", "axT_ps", "axT", "y_ps", "y_used", "z_s", "z_v", "zT_ps", "zT",
                                           "z_mm", "done")}
        ssem = {n: sem("s_" + n) for n in ("cnt", "off", "trows", "tred", "t50", "tred2", "trow", "dstf")}
        srt, srt2, final = sem("srt"), sem("srt2"), sem("final")
        sc_slot = [sem(f"sc_slot{h}") for h in range(2)]
        sc_done = [[sem(f"sc_done{h}_{j}") for j in range(8)] for h in range(2)]
        stats_sem = sem("stats_sem")
        bil_own = sem("bil_own")
        sin_in, sin_out = sem("sin_in"), sem("sin_out")
        rec_fill = sem("rec_fill")

        def table_reg(eng, tab, row, b, hi):
            return eng.value_load(tab[0:1, row, ds(b, 1)], min_val=0, max_val=hi)

        def bounded(v, hi):
            return nc.s_assert_within(v, 0, hi, skip_runtime_bounds_check_because=
                                      "a body starts before its block's end, or at an empty block's start")

        def rounds(eng, n, body):
            body(0, True)
            with eng.Fori(1, n) as u:
                body(u, False)

        credits = []
        for l in range(4):
            q = sems[l]
            credits += [(q["prod_ready"], BT), (q["sel_done"], BT), (q["meta_ready"], 1), (q["idx_ready"], BT),
                        (q["agg_out"], 1)]
            if l != 1:
                credits += [(q["hid_ps"], 1), (q["hid_ready"], 1), (q["wsh_ready"], BT)]
            else:
                credits += [(q["rec_idx"], 1), (q["act_sel"], BT)]
        credits += [(nsem[n], U) for n in ("aT", "conv", "conv_ps")]
        credits += [(psem[n], U) for n in ("xT_ps", "xT", "out_ps", "row", "back")]
        credits += [(bsem[n], 1) for n in ("done", "y_used", "axT_ps", "y_ps")]
        credits += [(bsem["zT_ps"], NG), (bsem["zT"], 2), (bsem["z_mm"], 2)]

        def pair_end(k):
            return min(k // 2 * 2 + 2, U)

        def conv_end(k, l):
            return 3 if k < 3 and l != 1 else U

        def table_of(l):
            return tab_i["src"] if l == 1 else tab_i["dst"]

        MAXB = NB * (TA // BT)

        def chunks(l):
            return [128, 128, 128, 128, 96] if l == 1 else [128, 128, 128, 64]

        @block.sync
        def _(sp):
            sp.dma_start(srci[:, :], A["src_t"]).then_inc(loads, 16)
            sp.dma_start(x_all[:, :, :], A["x_in"].rearrange("(b p) d -> p b d", p=P)).then_inc(loads, 16)
            sp.dma_start(av[:, :], A["a_t"]).then_inc(loads, 16)
            sp.dma_start(ebuf[:, 0:TA].bitcast(I32), A["dst_t"]).then_inc(loads, 16)
            sp.dma_start(ebuf[:, TA:5 * TA], A["attr4_t"]).then_inc(loads, 16)
            sp.wait_ge(w_zero, 1)
            for dst, src in w_loads[:half]:
                sp.dma_start(dst, src).then_inc(loads, 16)
            barrier(sp, "sp")
            barrier(sp, "sp")

            def publish(l):
                with sp.Fori(0, NB // U) as u:
                    for k in range(U):
                        sp.wait_ge(psem["row"], NB * l + u * U + k + 1 + U)
                        w = WX if l == 1 else D
                        sp.dma_start(table[l][ds((u * U + k) * P, P), :], row_out[:, k, 0:w])\
                            .then_inc(psem["stored"][k], 16)
                for k in range(U):
                    sp.wait_ge(psem["stored"][k], 16 * (NB // U) * (l + 1))

            publish(0)
            barrier(sp, "sp")
            for l in range(LAST_LAYER + 1):
                q = sems[l]
                tab = table_of(l)
                with sp.Fori(0, NB) as b:
                    n = table_reg(sp, tab, 0, b, MAXB)
                    base = table_reg(sp, tab, 1, b, MAXB)
                    start = table_reg(sp, tab, 2, b, NREC)
                    with sp.Fori(0, n) as i:
                        if l == 1:
                            sp.wait_ge(q["meta_ready"], base + i + 1)
                            sp.wait_ge(q["rec_idx"], base + i + 1)
                            src = rec_dram[ds(bounded(start + i * (BT * P), T * P), BT * P), :]
                            sp.dma_start(rec_slot[:, :, :], src.rearrange("(p j) c -> p j c", j=BT))\
                                .then_inc(q["rec_in"], 16)
                        else:
                            f = FC[l]
                            sp.wait_ge(q["hid_ps"], base + i + 1)
                            sp.dma_start(attrT[0:f["k"], :],
                                         A[f["attr"]][:, ds(bounded((start + i * BT) * P, (T - 1) * P), BT * P)])\
                                .then_inc(q["attr_in"], 16)
                total = table_reg(sp, tab, 1, NB - 1, MAXB) + table_reg(sp, tab, 0, NB - 1, MAXB)
                if l == 1:
                    sp.wait_ge(q["meta_ready"], total + 1)
                    sp.wait_ge(q["rec_idx"], total + 1)
                    sp.dma_start(rec_slot[:, :, :], rec_dram[0:BT * P, :].rearrange("(p j) c -> p j c", j=BT))\
                        .then_inc(q["rec_in"], 16)
                else:
                    sp.wait_ge(q["hid_ps"], total + 1)
                    sp.dma_start(attrT[0:FC[l]["k"], :], A[FC[l]["attr"]][:, 0:BT * P]).then_inc(q["attr_in"], 16)
                barrier(sp, "sp")
                w = {0: CNT_COL + 1, 1: AW, 2: CNT_COL, 3: CNT_COL}[l]
                with sp.Fori(0, NB // U) as u:
                    for k in range(U):
                        sp.wait_ge(nsem["conv"], NB * l + u * U + k + 1)
                        sp.dma_start(agg_in[:, k, 0:w], agg_dram[l][ds((u * U + k) * P, P), 0:w])\
                            .then_inc(nsem["in"][k], 16)
                barrier(sp, "sp")
                if l == 1:
                    barrier(sp, "sp")
                if l < LAST_LAYER:
                    publish(l + 1)
                    barrier(sp, "sp")
            sp.wait_ge(final, NB)
            sp.dma_start(out.rearrange("(b p) d -> p b d", p=P), x_all[:, :, :]).then_inc(out_done, 16)
            sp.wait_ge(out_done, 16)

        @block.gpsimd
        def _(pool):
            def held():
                pool.sem_inc(go, 1)

            pool.memset(ident[:, :], 0.0).then_inc(pch, 1)
            pool.memset(lower[:, :], 1.0).then_inc(pch, 1)
            pool.memset(ones[:, :], 1.0).then_inc(consts, 1)
            pool.memset(zeros_bf[:, :], 0.0).then_inc(consts, 1)
            pool.iota(iota[:, :], [[1, P]], base=0, channel_multiplier=0,
                      allow_small_or_imprecise_dtypes=True).then_inc(consts, 1)
            pool.iota(blk_id[:, :], [[1, NB]], base=0, channel_multiplier=0,
                      allow_small_or_imprecise_dtypes=True).then_inc(consts, 1)
            pool.iota(tile_id[:, :], [[P, 7]], base=0, channel_multiplier=1,
                      allow_small_or_imprecise_dtypes=True).then_inc(consts, 1)
            pool.wait_ge(pch, 2)
            pool.affine_select(out=ident[:, :], in_=ident[:, :], compare_op=ALU.not_equal, fill=1.0, base=0,
                               pattern=[[-1, P]], channel_multiplier=1).then_inc(consts, 1)
            pool.affine_select(out=lower[:, :], in_=lower[:, :], compare_op=ALU.is_gt, fill=0.0, base=0,
                               pattern=[[1, P]], channel_multiplier=-1).then_inc(consts, 1)
            pool.memset(agg_stage[:, :], 0.0).then_inc(pch, 1)
            pool.wait_ge(pch, 3)
            pool.memset(agg_stage[:, 0:8 * BT].rearrange("p (j c) -> p j c", c=8)[:, :, 1:2], -1.0).then_inc(pch, 1)
            pool.wait_ge(pch, 4)
            pool.dma_start(rec_dram[T * P:NREC, :].rearrange("(p j) c -> p (j c)", j=BT),
                           agg_stage[:, 0:8 * BT]).then_inc(rec_fill, 16)
            pool.dma_start(table[1][NB * P:(NB + 1) * P, :], agg_stage[:, 64:64 + WX]).then_inc(rec_fill, 16)
            pool.wait_ge(rec_fill, 32)
            barrier(pool, "pool")
            with pool.Fori(0, T // 16) as i:
                for h in range(2):
                    pool.wait_ge(sc_slot[h], i + 1)
                    held()
                    for j in range(8):
                        pool.indirect_dma_start(
                            rec_dram[:, :], bass.IndirectOffsetOnAxis(ap=scat_idx[:, h, j:j + 1], axis=0),
                            scat_rec[:, h, j, :], None).then_inc(sc_done[h][j], 16)
            for h in range(2):
                for j in range(8):
                    pool.wait_ge(sc_done[h][j], 16 * (T // 16))
            barrier(pool, "pool")
            barrier(pool, "pool")
            for l in range(LAST_LAYER + 1):
                q = sems[l]
                tab = table_of(l)
                w = WX if l == 1 else D
                with pool.Fori(0, NB) as b:
                    n = table_reg(pool, tab, 0, b, MAXB)
                    base = table_reg(pool, tab, 1, b, MAXB)
                    start = table_reg(pool, tab, 2, b, NREC)
                    with pool.Fori(0, n) as i:
                        for j in range(BT):
                            g = base + i
                            if l == 1:
                                if j == 0:
                                    pool.wait_ge(q["rec_idx"], g + 2)
                                pool.wait_ge(q["sel_done"], g * BT + j + 1)
                                held()
                                pool.tensor_copy(idx_slot[:, j:j + 1], rec_idx[:, j:j + 1]).then_inc(q["idx_ready"], 1)
                            else:
                                pool.wait_ge(q["prod_ready"], g * BT + j + 1)
                                held()
                                pool.tensor_copy(idx_slot[:, j:j + 1], srci[:, ds(bounded(start + i * BT, T - 1) + j, 1)])\
                                    .then_inc(q["idx_ready"], 1)
                            pool.wait_ge(q["idx_ready"], g * BT + j + 1 + BT)
                            held()
                            pool.indirect_dma_start(
                                gathered[:, j, 0:w], None, table[l][:, :],
                                bass.IndirectOffsetOnAxis(ap=idx_slot[:, j:j + 1], axis=0))\
                                .then_inc(q["got"][j], 16)
                barrier(pool, "pool")
                barrier(pool, "pool")
                if l == 1:
                    z = bsem
                    with pool.Fori(0, NB) as b:
                        for i in range(3):
                            pool.wait_ge(z["zT_ps"], b * NG + GSS + 2 * i + 2)
                            held()
                            xv = x_all[:, ds(b, 1), S + V * i:S + V * i + V].rearrange("p o u -> p (o u)")
                            mv = conv_all[:, ds(b, 1), S + V * i:S + V * i + V].rearrange("p o u -> p (o u)")
                            pool.tensor_tensor(zv[:, i, :].rearrange("p (u v) -> p u v", v=V),
                                               xv.unsqueeze(2).broadcast_to([P, V, V]),
                                               mv.unsqueeze(1).broadcast_to([P, V, V]), ALU.mult)\
                                .then_inc(z["z_v"], 1)
                    barrier(pool, "pool")
                if l < LAST_LAYER:
                    barrier(pool, "pool")

        @block.scalar
        def _(act):
            act.wait_ge(w_zero, 1)
            for dst, src in w_loads[half:]:
                act.dma_start(dst, src).then_inc(loads, 16)
            barrier(act, "act")
            barrier(act, "act")

            def publish(l):
                q = psem

                def body(u, first):
                    for k in range(U):
                        g = u * U + k
                        tp = banks[5 + k // 2][:, 256 * (k % 2):256 * (k % 2) + 256]
                        act.wait_ge(q["xT_ps"], NB * l + u * U + pair_end(k) + U)
                        act.wait_ge(q["out_ps"], NB * l + g + 1)
                        nc.scalar.activation(xsT[:, k, 0:P], tp[:, 0:P], ACT.Copy)
                        nc.scalar.activation(xsT[0:V, k, P:2 * P], tp[0:V, P:2 * P], ACT.Copy).then_inc(q["xT"], 1)
                    for k in range(U):
                        if l > 0:
                            nc.scalar.activation(x_all[:, ds(u * U + k, 1), :], xs[:, k:k + 1, :], ACT.Copy)\
                                .then_inc(q["back"], 1)

                rounds(act, NB // U, body)

            publish(0)
            barrier(act, "act")
            for l in range(LAST_LAYER + 1):
                q = sems[l]
                tab = table_of(l)

                def hidden(g):
                    act.wait_ge(q["hid_ps"], g + 2)
                    act.wait_ge(q["w_ready"], g * BT)
                    nc.scalar.activation(hidT[0:FC[l]["h"], :], ps_hid[0:FC[l]["h"], :], FC[l]["act"])\
                        .then_inc(q["hid_ready"], 1)

                def indices(g):
                    act.wait_ge(q["rec_in"], g * 16 + 16)
                    act.wait_ge(q["idx_ready"], g * BT + BT)
                    nc.scalar.activation(rec_idx[:, :], rec_slot[:, :, 0].bitcast(I32), ACT.Copy)\
                        .then_inc(q["rec_idx"], 1)

                if l == 1:
                    indices(0)
                else:
                    act.wait_ge(q["hid_ps"], 2)
                    nc.scalar.activation(hidT[0:FC[l]["h"], :], ps_hid[0:FC[l]["h"], :], FC[l]["act"])\
                        .then_inc(q["hid_ready"], 1)
                act.dma_start(agg_dram[l][0:P, 0:NB], av[:, :]).then_inc(q["agg_stored"], 16)
                with act.Fori(0, NB) as b:
                    n = table_reg(act, tab, 0, b, MAXB)
                    base = table_reg(act, tab, 1, b, MAXB)
                    if l == 1:
                        with act.Fori(0, n) as i:
                            g = base + i
                            for j in range(BT):
                                act.wait_ge(q["hot_ready"], g * BT + j + 1)
                                for k, c in ((3, 1), (4, 2)):
                                    last = nc.scalar.activation(sel[:, j, k, :], sel[:, j, 0, :], ACT.Copy,
                                                                scale=meta_slot[:, j, c:c + 1])
                                last.then_inc(q["act_sel"], 1)
                                if j == 1:
                                    indices(g + 1)
                    else:
                        start = table_reg(act, tab, 2, b, NREC)
                        with act.Fori(0, n) as i:
                            g = base + i
                            act.wait_ge(q["wsh_ready"], g * BT + BT)
                            act.sem_inc(held_act, 1)
                            nc.scalar.activation(sh_slot[:, :, :], meta[:, ds(bounded(start + i * BT, T - 1), BT), 0:4],
                                                 ACT.Copy).then_inc(q["sh_ready"], 1)
                            act.wait_ge(q["sh_ready"], g + 1)
                            for j in range(BT):
                                if j % 2 == 0:
                                    act.wait_ge(q["w_ready"], g * BT + j + 2)
                                act.wait_ge(q["prod_ready"], g * BT + j + 1)
                                w = ps_w[j // 2][:, 2 * WW * (j % 2):2 * WW * (j % 2) + 2 * WW]
                                for k in range(4):
                                    c0 = WW if k else 0
                                    last = nc.scalar.activation(wsh[:, j, k, :], w[:, c0:c0 + WW], ACT.Copy,
                                                                scale=sh_slot[:, j, k:k + 1])
                                last.then_inc(q["wsh_ready"], 1)
                            hidden(g + 1)
                    act.wait_ge(q["agg_closed"], b + 1)
                    act.wait_ge(q["agg_stored"], b * 16 + 16)
                    if l == 1:
                        nc.scalar.activation(agg_stage[:, 0:512], ps_agg[:, 0:512], ACT.Copy)
                        nc.scalar.activation(agg_stage[:, 512:AW], ps_agg2[:, 0:96], ACT.Copy)\
                            .then_inc(q["agg_out"], 1)
                        w = AW
                    else:
                        w = CNT_COL + 1 if l == 0 else CNT_COL
                        nc.scalar.activation(agg_stage[:, 0:w], ps_agg[:, 0:w], ACT.Copy).then_inc(q["agg_out"], 1)
                    act.wait_ge(q["agg_out"], b + 2)
                    act.dma_start(agg_dram[l][ds(b * P, P), 0:w], agg_stage[:, 0:w]).then_inc(q["agg_stored"], 16)
                act.wait_ge(q["agg_stored"], 16 * NB + 16)
                barrier(act, "act")
                r = nsem
                with act.Fori(0, NB // U) as u:
                    for k in range(U):
                        act.wait_ge(r["aT_ps"], NB * l + u * U + (U if l == 1 else k + 1))
                        act.wait_ge(r["conv_ps"], NB * l + u * U + k + 1)
                        last = chunks(l)[3]
                        nc.scalar.activation(aggT[:, k, 0:384], banks[k][:, 0:384], ACT.Copy)
                        ins = nc.scalar.activation(aggT[0:last, k, 384:512], banks[k][0:last, 384:512], ACT.Copy)
                        if l == 1:
                            bk, c = (7, P * k) if k < 4 else (6, 352)
                            ins = nc.scalar.activation(aggT[0:96, k, 512:640], banks[bk][0:96, c:c + P], ACT.Copy)
                        ins.then_inc(r["aT"], 1)
                if l == 2:
                    act.wait_ge(sin_in, 1)
                    nc.scalar.activation(small[:, 8:10, :], small[:, 6:8, :], ACT.Sin).then_inc(sin_out, 1)
                barrier(act, "act")
                if l == 1:
                    z = bsem
                    with act.Fori(0, NB) as b:
                        act.wait_ge(z["axT_ps"], b + 1)
                        act.sem_inc(held_act, 1)
                        nc.scalar.activation(xs[:, 0:1, 0:P], conv_all[:, ds(b, 1), 0:P], ACT.Copy)
                        nc.scalar.activation(xs[:, 1:2, 0:P], x_all[:, ds(b, 1), 0:P], ACT.Copy).then_inc(z["ax"], 1)
                        act.wait_ge(z["axT_ps"], b + 2)
                        act.wait_ge(z["y_ps"], b + 1)
                        nc.scalar.activation(xsT[0:S, 0, :], banks[0][0:S, 0:2 * P], ACT.Copy).then_inc(z["axT"], 1)
                        for q in range(NG):
                            n = b * NG + q
                            act.wait_ge(z["zT_ps"], n + 1 + NG)
                            act.wait_ge(z["z_mm"], n + 1)
                            nc.scalar.activation(zT[:, q % 2, :], banks[1 + q % 2][:, :], ACT.Copy)\
                                .then_inc(z["zT"], 1)
                    barrier(act, "act")
                act.wait_ge(r["sqrt_in"], l + 1)
                nc.scalar.activation(small[:, 12, :], small[:, 11, :], ACT.Sqrt).then_inc(r["sqrt_out"], 1)
                if l < LAST_LAYER:
                    publish(l + 1)
                    barrier(act, "act")

        @block.tensor
        def _(pe):
            mm, tr = nc.tensor.matmul, nc.tensor.transpose
            pe.wait_ge(consts, 7)
            pe.wait_ge(ssem["dstf"], 1)
            for c in range(7):
                w = min(P, T - P * c)
                last = tr(banks[1 + c // 4][0:w, P * (c % 4):P * (c % 4) + P], sort_v[:, 4, P * c:P * c + w], ident[:, :])
            last.then_inc(ssem["trows"], 1)
            pe.wait_ge(ssem["tred"], 1)
            tr(banks[3][0:2 * NB, 0:P], rng[:, :], ident[:, :]).then_inc(ssem["t50"], 1)
            pe.wait_ge(ssem["tred2"], 1)
            tr(banks[4][0:1, 0:2 * NB], rng_max[:, 0:1], ident[0:2 * NB, 0:2 * NB]).then_inc(ssem["trow"], 1)
            pe.wait_ge(ssem["cnt"], 1)
            mm(banks[0][:, 0:NB], lower[:, :], small[:, 0, :], start=True, stop=True)
            mm(banks[0][:, NB:2 * NB], ones[:, :], small[:, 0, :], start=True, stop=True).then_inc(ssem["off"], 1)
            barrier(pe, "pe")
            barrier(pe, "pe")

            def publish(l):
                q = psem
                with pe.Fori(0, NB // U) as u:
                    for k in range(U):
                        g = u * U + k
                        tp = banks[5 + k // 2][:, 256 * (k % 2):256 * (k % 2) + 256]
                        pe.wait_ge(q["xs"], NB * l + g + 1)
                        pe.wait_ge(q["xT"], NB * l + u * U + pair_end(k))
                        tr(tp[:, 0:P], xs[:, k, 0:P], ident[:, :])
                        tr(tp[0:V, P:2 * P], xs[:, k, P:D], ident[:, :]).then_inc(q["xT_ps"], 1)
                    for k in range(U):
                        g = u * U + k
                        pe.wait_ge(q["xT"], NB * l + g + 1 + U)
                        pe.wait_ge(q["row"], NB * l + g + 1)
                        o = banks[k][:, 0:2 * D].rearrange("p (j c) -> p j c", j=2)
                        j0 = 1 if l == 1 else 0
                        mm(o[:, j0:2, 0:P], xsT[:, k, 0:P], wa[l][:, j0:2, :], start=True, stop=True)
                        mm(o[:, j0:2, P:D], xsT[0:V, k, P:2 * P], wb[l][:, j0:2, :], start=True, stop=True)\
                            .then_inc(q["out_ps"], 1)

            publish(0)
            barrier(pe, "pe")
            for l in range(LAST_LAYER + 1):
                q = sems[l]
                tab = table_of(l)
                wagg = 512 if l == 1 else (CNT_COL + 1 if l == 0 else CNT_COL)

                def hidden(g):
                    f = FC[l]
                    pe.wait_ge(q["attr_in"], g * 16 + 16)
                    pe.wait_ge(q["hid_ready"], g + 1)
                    mm(ps_hid[0:f["h"], :], w1[l][:, :], attrT[:, :], start=True, stop=True)\
                        .then_inc(q["hid_ps"], 1)

                def weights(g, j0):
                    pe.wait_ge(q["hid_ready"], g + 2)
                    pe.wait_ge(q["wsh_ready"], g * BT + j0 + 2)
                    for j in (j0, j0 + 1):
                        mm(ps_w[j0 // 2][:, 2 * WW * (j % 2):2 * WW * (j % 2) + 2 * WW],
                           hidT[:, P * j:P * j + P], w2[l][:, :], start=True, stop=True).then_inc(q["w_ready"], 1)

                def aggregate(g, j0):
                    for j in (j0, j0 + 1):
                        pe.wait_ge(q["prod_ready"], g * BT + j + 1 + BT)
                        mm(ps_agg[:, 0:wagg], hot[:, j, :], msg[:, j, 0:wagg], start=False, stop=False)\
                            .then_inc(q["sel_done"], 1)

                if l != 1:
                    pe.wait_ge(q["attr_in"], 16)
                    mm(ps_hid[0:FC[l]["h"], :], w1[l][:, :], attrT[:, :], start=True, stop=True)\
                        .then_inc(q["hid_ps"], 1)
                    weights(0, 0)
                with pe.Fori(0, NB) as b:
                    n = table_reg(pe, tab, 0, b, MAXB)
                    base = table_reg(pe, tab, 1, b, MAXB)
                    pe.wait_ge(q["agg_out"], b + 1)
                    mm(ps_agg[:, 0:wagg], zeros_bf[:, 0:P], zeros_bf[:, 0:wagg], start=True, stop=False)
                    if l == 1:
                        mm(ps_agg2[:, 0:96], zeros_bf[:, 0:P], zeros_bf[:, 0:96], start=True, stop=False)
                    with pe.Fori(0, n) as i:
                        g = base + i
                        if l != 1:
                            weights(g, 2)
                            hidden(g + 1)
                            aggregate(g, 0)
                            weights(g + 1, 0)
                            aggregate(g, 2)
                        else:
                            for j in range(BT):
                                pe.wait_ge(q["prod_ready"], g * BT + j + 1 + BT)
                                pe.wait_ge(q["act_sel"], g * BT + j + 1 + BT)
                                pe.wait_ge(q["got"][j], g * 16 + 16)
                                for s0, w, k, c0 in TP_PARTS:
                                    dst = ps_agg2 if k == 4 else ps_agg
                                    last = mm(dst[:, c0:c0 + w], sel[:, j, k, :], gathered[:, j, s0:s0 + w],
                                              start=False, stop=False)
                                last.then_inc(q["sel_done"], 1)
                    if l == 1:
                        mm(ps_agg2[:, 0:96], zeros_bf[:, 0:P], zeros_bf[:, 0:96], start=False, stop=True)
                    mm(ps_agg[:, 0:wagg], zeros_bf[:, 0:P], zeros_bf[:, 0:wagg], start=False, stop=True)\
                        .then_inc(q["agg_closed"], 1)
                barrier(pe, "pe")
                r = nsem
                ch = chunks(l)
                with pe.Fori(0, NB // U) as u:
                    for k in range(U):
                        g = u * U + k
                        pe.wait_ge(r["in"][k], 16 * (NB // U) * l + u * 16 + 16)
                        pe.wait_ge(r["aT"], NB * l + u * U + (U if l == 1 else k + 1))
                        if l == 1:
                            pe.wait_ge(r["conv"], NB * l + u * U + U)
                        for c, rows in enumerate(ch):
                            bk, c0 = (k, P * c) if c < 4 else ((7, P * k) if k < 4 else (6, 352))
                            last = tr(banks[bk][0:rows, c0:c0 + P], agg_in[:, k, P * c:P * c + rows], ident[:, :])
                        last.then_inc(r["aT_ps"], 1)
                    for k in range(U):
                        g = u * U + k
                        w = D if l == 1 else 161
                        wt = wmsg if l == 1 else wconv[l]
                        pe.wait_ge(r["aT"], NB * l + u * U + (U if l == 1 else k + 1) + U)
                        pe.wait_ge(r["conv"], NB * l + u * U + conv_end(k, l))
                        o = banks[5 + k // 3][:, 161 * (k % 3):161 * (k % 3) + w] if k < 3 else \
                            banks[6][:, 161 * (k - 3):161 * (k - 3) + w]
                        for c, rows in enumerate(ch):
                            last = mm(o, aggT[0:rows, k, P * c:P * c + P], wt[0:rows, c, 0:w],
                                      start=(c == 0), stop=(c == len(ch) - 1))
                        last.then_inc(r["conv_ps"], 1)
                barrier(pe, "pe")
                if l == 1:
                    z = bsem

                    def transposed(b, q):
                        if q < GSS:
                            src = zs[:, q // 2, :]
                            if q % 2 == 0:
                                pe.wait_ge(z["z_s"], b * 4 + q // 2 + 1)
                        else:
                            src = zv[:, (q - GSS) // 2, :]
                            if q % 2 == 0:
                                pe.wait_ge(z["z_v"], b * 3 + (q - GSS) // 2 + 1)
                        pe.wait_ge(z["zT"], b * NG + q + 1)
                        for c in range(4):
                            c0 = 512 * (q % 2) + P * c
                            last = tr(banks[1 + q % 2][:, P * c:P * c + P], src[:, c0:c0 + P], ident[:, :])
                        last.then_inc(z["zT_ps"], 1)

                    with pe.Fori(0, NB) as b:
                        pe.wait_ge(z["ax"], b + 1)
                        for h in range(2):
                            last = tr(banks[0][:, P * h:P * h + P], xs[:, h, 0:P], ident[:, :])
                        last.then_inc(z["axT_ps"], 1)
                        pe.wait_ge(z["axT"], b + 1)
                        pe.wait_ge(z["y_used"], b + 1)
                        for c in range(4):
                            h, wt = (1, wu_sv) if c < 2 else (0, wu_vs)
                            last = mm(banks[4 + c][:, :], xsT[0:S, 0, P * h:P * h + P],
                                      wt[:, 512 * (c % 2):512 * (c % 2) + 512], start=True, stop=True)
                        last.then_inc(z["y_ps"], 1)
                        transposed(b, 0)
                        for q in range(NG):
                            if q + 1 < NG:
                                transposed(b, q + 1)
                            pe.wait_ge(z["zT"], b * NG + q + 1 + 2)
                            if q == 0:
                                pe.wait_ge(z["done"], b + 1)
                            for c in range(4):
                                wt = wu_ss[:, 4 * q + c, :] if q < GSS else wu_vv[:, 4 * (q % 2) + c, :]
                                last = mm(banks[3][:, 0:S], zT[:, q % 2, P * c:P * c + P], wt,
                                          start=(q == 0 and c == 0), stop=(q == NG - 1 and c == 3))
                            last.then_inc(z["z_mm"], 1)
                    barrier(pe, "pe")
                if l < LAST_LAYER:
                    publish(l + 1)
                    barrier(pe, "pe")

        @block.vector
        def _(dve):
            v = nc.vector
            for l in FC:
                v.memset(wconv[l][:, :, :], 0.0)
                v.memset(w1[l][:, :], 0.0)
                v.memset(w2[l][:, :], 0.0)
            v.memset(attrT[:, :], 0.0)
            v.memset(hidT[:, :], 0.0)
            for l in range(4):
                v.memset(wa[l][:, :, :], 0.0)
            v.memset(wmsg[:, :, :], 0.0).then_inc(w_zero, 1)
            for l in FC:
                for r, (what, _, _) in enumerate(CONV_ROWS):
                    q0 = 32 * (r % 4)
                    v.memset(row_scale[l][q0:q0 + 32, r // 4:r // 4 + 1], FC[l]["cm"] * (R3 if what == "P3" else 1.0))
                v.memset(row_scale[l][64:P, 3:4], 0.0)
            for r, (_, _, _, _, s) in enumerate(msg_rows()):
                q0 = 32 * (r % 4)
                last = v.memset(row_scale[1][q0:q0 + 32, r // 4:r // 4 + 1], s)
            v.memset(row_scale[1][96:P, 4:5], 0.0)
            v.memset(wa_scale[0:S, :], 1 / 8)
            link(v.memset(wa_scale[S:P, :], R32))
            dve.wait_ge(loads, 16 * (5 + len(w_loads)))
            dve.wait_ge(consts, 7)
            v.tensor_scalar(blk128[:, :], blk_id[:, :], float(P), None, ALU.mult)
            for l, f in FC.items():
                v.tensor_scalar(w1[l][:, :], w1[l][:, :], f["c1"], None, ALU.mult)
                v.tensor_scalar(w2[l][:, :], w2[l][:, :], f["c2"], None, ALU.mult)
                for c in range(4):
                    v.tensor_scalar(wconv[l][:, c, :], wconv[l][:, c, :], row_scale[l][:, c:c + 1], None, ALU.mult)
            for c in range(5):
                v.tensor_scalar(wmsg[:, c, :], wmsg[:, c, :], row_scale[1][:, c:c + 1], None, ALU.mult)
            for l in range(4):
                v.tensor_scalar(wa[l][:, :, :], wa[l][:, :, :], wa_scale[:, 0:1], None, ALU.mult)
                v.tensor_scalar(wb[l][:, 0 if l != 1 else 1:2, :], wb[l][:, 0 if l != 1 else 1:2, :], R32, None, ALU.mult)
            v.tensor_scalar(wu_ss[:, :, :], wu_ss[:, :, :], 1 / 64, None, ALU.mult)
            v.tensor_scalar(wu_vv[:, :, :], wu_vv[:, :, :], R3 / 32, None, ALU.mult)
            v.tensor_scalar(wu_sv[:, :], wu_sv[:, :], 1 / math.sqrt(2048.0), None, ALU.mult)
            v.tensor_scalar(wu_vs[:, :], wu_vs[:, :], 1 / math.sqrt(2048.0), None, ALU.mult)
            link(v.memset(zrow[:, :], 0.0))
            for c, n in credits:
                dve.sem_inc(c, n)
            raw_dst = ebuf[:, 0:TA].bitcast(I32)
            link(v.tensor_copy(meta[:, :, 0:4], ebuf[:, TA:5 * TA].rearrange("p (t c) -> p t c", c=4)))
            link(v.tensor_copy(meta[:, :, 4:5], raw_dst.rearrange("p (t c) -> p t c", c=1)))
            link(v.tensor_scalar(blk_i[:, :], raw_dst[:, 0:T], 7, None, ALU.logical_shift_right))
            v.tensor_copy(sort_v[:, 4, :], blk_i[:, :]).then_inc(ssem["dstf"], 1)
            dve.wait_ge(ssem["dstf"], 1)
            link(v.tensor_scalar(blk_i[:, :], srci[:, 0:T], 7, None, ALU.logical_shift_right))
            blk, eq, cum, pos = (sort_v[:, c, :] for c in (0, 1, 2, 3))
            link(v.tensor_copy(blk, blk_i[:, :]))
            dve.wait_ge(ssem["trows"], 1)
            link(v.memset(tile_mm[:, :, :], 30.0))
            link(v.memset(tile_mm[:, 1, :], -1.0))
            for c in range(7):
                w = min(P, T - P * c)
                src = banks[1 + c // 4][0:w, P * (c % 4):P * (c % 4) + P]
                v.tensor_reduce(tile_mm[0:w, 0, c:c + 1], src, AX.X, ALU.min)
                link(v.tensor_reduce(tile_mm[0:w, 1, c:c + 1], src, AX.X, ALU.max))
            bb = blk_id[:, :].unsqueeze(2).broadcast_to([P, NB, 7])
            for r in range(2):
                src = tile_mm[:, r:r + 1, :].broadcast_to([P, NB, 7])
                link(v.tensor_tensor(hit[:, r, :, :], src, bb, (ALU.is_le, ALU.is_ge)[r]))
            link(v.tensor_tensor(hit[:, 0, :, :], hit[:, 0, :, :], hit[:, 1, :, :], ALU.mult))
            v.tensor_scalar(tile_lim[:, 0, :], tile_id[:, :], -1.0, float(T), ALU.mult, ALU.add)
            link(v.tensor_scalar(tile_lim[:, 1, :], tile_id[:, :], 1.0, None, ALU.add))
            for r in (1, 0):
                src = tile_lim[:, r:r + 1, :].broadcast_to([P, NB, 7])
                link(v.tensor_tensor(hit[:, 1, :, :], hit[:, 0, :, :], src, ALU.mult))
                link(v.tensor_reduce(rng[:, NB * r:NB * r + NB], hit[:, 1, :, :], AX.X, ALU.max))
            v.tensor_copy(rng[:, 0:1], rng[:, 0:1]).then_inc(ssem["tred"], 1)
            dve.wait_ge(ssem["t50"], 1)
            v.tensor_reduce(rng_max[:, 0:1], banks[3][0:2 * NB, 0:P], AX.X, ALU.max).then_inc(ssem["tred2"], 1)
            dve.wait_ge(ssem["trow"], 1)
            link(v.tensor_copy(trow[0:1, 0:2, :], banks[4][0:1, 0:2 * NB].rearrange("p (r b) -> p r b", r=2)))
            link(v.tensor_scalar(trow[0:1, 2, :], trow[0:1, 0, :], -1.0, float(T), ALU.mult, ALU.add))
            link(v.tensor_scalar(trow[0:1, 2, :], trow[0:1, 2, :], float(T - BT), None, ALU.min))
            link(v.tensor_tensor(trow[0:1, 3, :], trow[0:1, 1, :], trow[0:1, 2, :], ALU.subtract))

            def finish_table(tab, shift):
                link(v.tensor_scalar(trow[0:1, 3, :], trow[0:1, 3, :], float(2 ** shift - 1), 1.0 * 2 ** shift,
                                     ALU.add, ALU.max))
                link(v.tensor_copy(tri[0:1, :], trow[0:1, 3, :]))
                link(v.tensor_scalar(tab[0:1, 0, :], tri[0:1, :], shift, None, ALU.logical_shift_right))
                link(v.tensor_copy(trow[0:1, 3, :], tab[0:1, 0, :]))
                link(v.tensor_tensor_scan(trow[0:1, 1, :], trow[0:1, 3, :], zrow[0:1, 0:NB], 0.0, ALU.add, ALU.add))
                link(v.tensor_tensor(trow[0:1, 1, :], trow[0:1, 1, :], trow[0:1, 3, :], ALU.subtract))
                link(v.tensor_copy(tab[0:1, 1, :], trow[0:1, 1, :]))
                link(v.tensor_copy(tab[0:1, 2, :], trow[0:1, 2, :]))

            finish_table(tab_i["dst"], 2)
            link(v.memset(pos, 0.0))
            with dve.Fori(0, NB) as b:
                c0 = small[:, 0, ds(b, 1)]
                v.tensor_scalar(eq, blk, blk_id[:, ds(b, 1)], None, ALU.is_equal).then_inc(srt, 1)
                dve.wait_ge(srt, b * 5 + 1)
                v.tensor_tensor_scan(cum, eq, zrow[:, :], 0.0, ALU.add, ALU.add).then_inc(srt, 1)
                dve.wait_ge(srt, b * 5 + 2)
                v.tensor_scalar(c0, cum[:, T - 1:T], 1.0, None, ALU.mult).then_inc(srt, 1)
                dve.wait_ge(srt, b * 5 + 3)
                v.tensor_tensor(cum, cum, eq, ALU.mult).then_inc(srt, 1)
                dve.wait_ge(srt, b * 5 + 4)
                v.tensor_tensor(pos, pos, cum, ALU.add).then_inc(srt, 1)
                dve.wait_ge(srt, b * 5 + 5)
            v.tensor_copy(small[:, 1, :], small[:, 0, :]).then_inc(ssem["cnt"], 1)
            dve.wait_ge(ssem["off"], 1)
            link(v.tensor_copy(small[:, 2, :], banks[0][:, NB:2 * NB]))
            link(v.tensor_tensor_scan(small[:, 3, :], small[:, 2, :], zrow[:, 0:NB], 0.0, ALU.add, ALU.add))
            link(v.tensor_tensor(small[:, 3, :], small[:, 3, :], small[:, 2, :], ALU.subtract))
            link(v.tensor_tensor(small[:, 4, :], small[:, 3, :], banks[0][:, 0:NB], ALU.add))
            link(v.tensor_scalar(small[:, 4, :], small[:, 4, :], -1.0, None, ALU.add))
            link(v.tensor_copy(trow[0:1, 2, :], small[0:1, 3, :]))
            link(v.tensor_copy(trow[0:1, 3, :], small[0:1, 2, :]))
            finish_table(tab_i["src"], 9)
            with dve.Fori(0, NB) as b:
                v.tensor_scalar(eq, blk, blk_id[:, ds(b, 1)], small[:, 4, ds(b, 1)], ALU.is_equal, ALU.mult)\
                    .then_inc(srt2, 1)
                dve.wait_ge(srt2, b * 2 + 1)
                v.tensor_tensor(pos, pos, eq, ALU.add).then_inc(srt2, 1)
                dve.wait_ge(srt2, b * 2 + 2)
            barrier(dve, "dve")
            link(v.memset(scat_rec[:, :, :, :], 0.0))

            def fill(i, first):
                for h in range(2):
                    if not first:
                        for j in range(8):
                            dve.wait_ge(sc_done[h][j], i * 16)
                    t0 = i * 16 + 8 * h
                    v.tensor_scalar(scat_rec[:, h, :, 2:6], meta[:, ds(t0, 8), 0:4], 1.0, None, ALU.mult)
                    v.tensor_scalar(scat_rec[:, h, :, 0:1].bitcast(I32), meta[:, ds(t0, 8), 4:5], 1.0, None, ALU.mult)
                    v.tensor_scalar(scat_rec[:, h, :, 1], srci[:, ds(t0, 8)], 1.0, None, ALU.mult)
                    v.tensor_scalar(scat_idx[:, h, :], pos[:, ds(t0, 8)], 1.0, None, ALU.mult).then_inc(sc_slot[h], 1)

            rounds(dve, T // 16, fill)
            barrier(dve, "dve")

            def publish(l):
                q = psem

                def body(u, first):
                    for k in range(U):
                        g = u * U + k
                        dve.wait_ge(q["xT_ps"], NB * l + g + 1)
                        if l == 0:
                            ins = v.tensor_scalar(xs[:, k:k + 1, :], x_all[:, ds(g, 1), :], 1.0, None, ALU.mult)
                        else:
                            dve.wait_ge(q["back"], NB * (l - 1) + g + 1)
                            if l == 1:
                                dve.wait_ge(q["row"], NB * l + g + 1)
                            ins = v.tensor_scalar(xs[:, k:k + 1, :], x_all[:, ds(g, 1), :], small[:, 14, ds(g, 1)],
                                                  small[:, 13, ds(g, 1)], ALU.subtract, ALU.mult)
                        ins.then_inc(q["xs"], 1)
                    for k in range(U):
                        g = u * U + k
                        dve.wait_ge(q["out_ps"], NB * l + g + 1 + U)
                        if not first:
                            dve.wait_ge(q["stored"][k], 16 * (NB // U) * l + u * 16)
                        if l == 1:
                            dve.wait_ge(q["xs"], NB * l + g + 1)
                            row = row_out[:, k, :]
                            v.tensor_scalar(row[:, 32:96], xs[:, k, 0:S], 1.0, None, ALU.mult)
                            v.tensor_scalar(row[:, 160:224], xs[:, k, 0:S], 1.0, None, ALU.mult)
                            v.tensor_scalar(row[:, 0:32], xs[:, k, S + V:S + 2 * V], 1.0, None, ALU.mult)
                            v.tensor_scalar(row[:, 96:128], xs[:, k, S:S + V], 1.0, None, ALU.mult)
                            v.tensor_scalar(row[:, 128:160], xs[:, k, S + 2 * V:D], 1.0, None, ALU.mult)
                        else:
                            v.tensor_scalar(row_out[:, k, 0:D], banks[k][:, 0:D], av[:, ds(g, 1)], None, ALU.mult)
                        v.tensor_scalar(self_all[:, ds(g, 1), :], banks[k][:, D:2 * D].unsqueeze(1), 1.0, None,
                                        ALU.mult).then_inc(q["row"], 1)

                rounds(dve, NB // U, body)

            def select(l, j, g):
                dve.wait_ge(sems[l]["sel_done"], g * BT + j + 1)
                node = meta_slot[:, j, 4:5]
                v.tensor_scalar(sel[:, j, 0, :], node_id[:, :], node, None, ALU.is_equal)\
                    .then_inc(sems[l]["hot_ready"], 1)
                for k, c in ((1, 3), (2, 0)):
                    last = v.tensor_scalar(sel[:, j, k, :], node_id[:, :], node, meta_slot[:, j, c:c + 1],
                                           ALU.is_equal, ALU.mult)
                return last

            def bilinear():
                z = bsem
                with dve.Fori(0, NB) as b:
                    def cols(t, c0, n):
                        return t[:, ds(b, 1), c0:c0 + n].rearrange("p o c -> p (o c)")

                    for p in range(4):
                        dve.wait_ge(z["zT_ps"], b * NG + 2 * p + 2)
                        v.tensor_tensor(zs[:, p, :].rearrange("p (u v) -> p u v", v=S),
                                        cols(x_all, 16 * p, 16).unsqueeze(2).broadcast_to([P, 16, S]),
                                        cols(conv_all, 0, S).unsqueeze(1).broadcast_to([P, 16, S]), ALU.mult)\
                            .then_inc(z["z_s"], 1)
                    dve.wait_ge(z["y_ps"], b + 2)
                    for i in range(3):
                        for c in range(4):
                            mul = cols(conv_all if c < 2 else x_all, S + V * i + 16 * (c % 2), 16)
                            last = v.tensor_tensor(
                                tt[:, 512 * c:512 * c + 512].rearrange("p (r w) -> p r w", w=V),
                                banks[4 + c][:, :].rearrange("p (r w) -> p r w", w=V),
                                mul.unsqueeze(2).broadcast_to([P, 16, V]), ALU.mult)
                        last.then_inc(z["y_used"] if i == 2 else bil_own, 1)
                        if i == 2:
                            dve.wait_ge(z["y_used"], b + 2)
                        else:
                            dve.wait_ge(bil_own, b * 7 + 2 * i + 1)
                        v.tensor_reduce(upd[:, 1, S + V * i:S + V * i + V],
                                        tt[:, :].rearrange("p (r w) -> p w r", w=V), AX.X, ALU.add)\
                            .then_inc(bil_own, 1)
                        dve.wait_ge(bil_own, b * 7 + (5 if i == 2 else 2 * i + 2))
                    v.scalar_tensor_tensor(upd[:, 0, :], cols(x_all, 0, D), 2.0, cols(self_all, 0, D), ALU.mult,
                                           ALU.add).then_inc(bil_own, 1)
                    dve.wait_ge(bil_own, b * 7 + 6)
                    dve.wait_ge(z["z_mm"], b * NG + NG + 2)
                    v.tensor_tensor(cols(x_all, S, 3 * V), upd[:, 0, S:D], upd[:, 1, S:D], ALU.add)\
                        .then_inc(bil_own, 1)
                    v.tensor_tensor(cols(x_all, 0, S), upd[:, 0, 0:S], banks[3][:, 0:S], ALU.add)\
                        .then_inc(z["done"], 1)
                    dve.wait_ge(z["done"], b + 2)

            publish(0)
            barrier(dve, "dve")
            for l in range(LAST_LAYER + 1):
                q = sems[l]
                tab = table_of(l)
                if l == 0:
                    link(v.memset(msg[:, :, CNT_COL:MW], 1.0))
                with dve.Fori(0, NB) as b:
                    n = table_reg(dve, tab, 0, b, MAXB)
                    base = table_reg(dve, tab, 1, b, MAXB)
                    start = table_reg(dve, tab, 2, b, NREC)
                    dve.wait_ge(q["prod_ready"], base * BT + BT)
                    v.tensor_scalar(node_id[:, :], iota[:, :], blk128[:, ds(b, 1)], None, ALU.add)\
                        .then_inc(q["node_ids"], 1)
                    dve.wait_ge(q["node_ids"], b + 1)
                    dve.sem_inc(held_dve, 1)
                    with dve.Fori(0, n) as i:
                        g = base + i
                        if l == 1:
                            dve.wait_ge(q["rec_in"], g * 16 + 16)
                            dve.wait_ge(q["act_sel"], g * BT + BT)
                            dve.wait_ge(q["prod_ready"], g * BT + BT)
                            v.tensor_copy(meta_slot[:, :, 4], rec_slot[:, :, 1])
                            v.tensor_copy(meta_slot[:, :, 0:4], rec_slot[:, :, 2:6]).then_inc(q["meta_ready"], 1)
                            dve.wait_ge(q["meta_ready"], g + 2)
                            for j in range(BT):
                                select(l, j, g).then_inc(q["prod_ready"], 1)
                        else:
                            dve.wait_ge(q["prod_ready"], g * BT + BT)
                            v.tensor_scalar(dst_slot[:, :].unsqueeze(2), meta[:, ds(bounded(start + i * BT, T - 1), BT), 4:5],
                                            1.0, None, ALU.mult).then_inc(q["meta_ready"], 1)
                            dve.wait_ge(q["meta_ready"], g + 2)
                            for j in range(BT):
                                dve.wait_ge(q["sel_done"], g * BT + j + 1)
                                v.tensor_scalar(hot[:, j, :], node_id[:, :], dst_slot[:, j:j + 1], None, ALU.is_equal)
                                dve.wait_ge(q["got"][j], g * 16 + 16)
                                dve.wait_ge(q["wsh_ready"], g * BT + j + 1 + BT)
                                e0 = gathered[:, j, 0:S].unsqueeze(1).broadcast_to([P, 4, S])
                                e1 = gathered[:, j, S:D].rearrange("p (m c) -> p m c", c=V)
                                out = msg[:, j, 0:CNT_COL]
                                v.tensor_tensor(out[:, 0:4 * S].rearrange("p (k c) -> p k c", c=S),
                                                wsh[:, j, :, 0:S], e0, ALU.mult)
                                v.tensor_tensor(out[:, 4 * S:4 * S + 96].rearrange("p (m c) -> p m c", c=V),
                                                wsh[:, j, 0:1, S:WW].broadcast_to([P, 3, V]), e1, ALU.mult)
                                v.tensor_tensor(out[:, 4 * S + 96:CNT_COL].rearrange("p (m c) -> p m c", c=V),
                                                wsh[:, j, 1:4, S:WW], e1, ALU.mult).then_inc(q["prod_ready"], 1)
                barrier(dve, "dve")
                r = nsem
                w = D if l == 1 else 161
                with dve.Fori(0, NB // U) as u:
                    for k in range(U):
                        g = u * U + k
                        dve.wait_ge(r["conv_ps"], NB * l + u * U + conv_end(k, l) + U)
                        o = banks[5][:, 161 * k:161 * k + w] if k < 3 else banks[6][:, 161 * (k - 3):161 * (k - 3) + w]
                        if l == 0:
                            v.tensor_scalar(conv_all[:, ds(g, 1), 161:162],
                                            agg_in[:, k:k + 1, CNT_COL:CNT_COL + 1], 1.0, None, ALU.mult)
                        v.tensor_scalar(conv_all[:, ds(g, 1), 0:w], o.unsqueeze(1), 1.0, None, ALU.mult)\
                            .then_inc(r["conv"], 1)
                sm = lambda c: small[:, c, :]
                if l != 1:
                    dve.wait_ge(r["conv"], NB * (l + 1) + U)
                    gate = conv_all[:, :, 160]
                    if l == 0:
                        link(v.tensor_scalar(sm(2), conv_all[:, :, 161], 1.0, None, ALU.max))
                        link(v.reciprocal(sm(3), sm(2)))
                        link(v.tensor_tensor(sm(3), sm(3), av[:, :], ALU.mult))
                        link(v.tensor_tensor(sm(4), sm(3), sm(3), ALU.mult))
                        link(v.tensor_tensor(sm(1), sm(4), gate, ALU.mult))
                        link(v.tensor_copy(sm(0), av[:, :]))
                    elif l == 2:
                        link(v.scalar_tensor_tensor(sm(2), gate, 0.1, av[:, :], ALU.mult, ALU.mult))
                        link(v.tensor_scalar(sm(3), sm(2), 1 / (2 * math.pi), ROUND, ALU.mult, ALU.add))
                        link(v.tensor_scalar(sm(3), sm(3), -ROUND, None, ALU.add))
                        for part in TWO_PI:
                            link(v.scalar_tensor_tensor(sm(2), sm(3), -part, sm(2), ALU.mult, ALU.add))
                        link(v.tensor_scalar(sm(6), sm(2), 3.1415925, -3.1415925, ALU.min, ALU.max))
                        v.tensor_scalar(sm(7), sm(6), 0.5, None, ALU.mult).then_inc(sin_in, 1)
                        dve.wait_ge(sin_out, 1)
                        link(v.tensor_tensor(sm(1), sm(8), av[:, :], ALU.mult))
                        link(v.tensor_tensor(sm(3), sm(9), sm(9), ALU.mult))
                        link(v.tensor_scalar(sm(3), sm(3), -2.0, 1.0, ALU.mult, ALU.add))
                        link(v.tensor_tensor(sm(0), sm(3), av[:, :], ALU.mult))
                    else:
                        v.tensor_copy(sm(1), av[:, :])
                        link(v.tensor_copy(sm(0), av[:, :]))
                    v.tensor_tensor(self_all[:, :, :], self_all[:, :, :],
                                    sm(0).unsqueeze(2).broadcast_to([P, NB, D]), ALU.mult)
                    link(v.tensor_tensor(conv_all[:, :, 0:D], conv_all[:, :, 0:D],
                                         sm(1).unsqueeze(2).broadcast_to([P, NB, D]), ALU.mult))
                    link(v.tensor_tensor(x_all[:, :, :], x_all[:, :, :], self_all[:, :, :], ALU.add))
                    link(v.tensor_tensor(x_all[:, :, :], x_all[:, :, :], conv_all[:, :, 0:D], ALU.add))
                barrier(dve, "dve")
                if l == 1:
                    bilinear()
                    barrier(dve, "dve")
                with dve.Fori(0, NB // U) as u:
                    for k in range(U):
                        v.bn_stats(stats[:, ds(u * U + k, 1), :], x_all[:, ds(u * U + k, 1), :])\
                            .then_inc(stats_sem, 1)
                dve.wait_ge(stats_sem, NB * (l + 1))
                me, qe, mo, qo = (stats[:, :, c] for c in (1, 2, 4, 5))
                link(v.tensor_tensor(sm(14), me, mo, ALU.add))
                link(v.tensor_scalar(sm(14), sm(14), 0.5, None, ALU.mult))
                link(v.tensor_tensor(sm(10), me, mo, ALU.subtract))
                link(v.scalar_tensor_tensor(sm(10), sm(10), 0.25, sm(10), ALU.mult, ALU.mult))
                link(v.tensor_tensor(sm(11), qe, qo, ALU.add))
                link(v.scalar_tensor_tensor(sm(11), sm(11), 1 / D, sm(10), ALU.mult, ALU.add))
                v.tensor_scalar(sm(11), sm(11), EPS, None, ALU.add).then_inc(r["sqrt_in"], 1)
                dve.wait_ge(r["sqrt_out"], l + 1)
                link(v.reciprocal(sm(13), sm(12)))
                if l < LAST_LAYER:
                    publish(l + 1)
                    barrier(dve, "dve")
            with dve.Fori(0, NB // U) as u:
                for k in range(U):
                    g = u * U + k
                    v.tensor_scalar(x_all[:, ds(g, 1), :], x_all[:, ds(g, 1), :], small[:, 14, ds(g, 1)],
                                    small[:, 13, ds(g, 1)], ALU.subtract, ALU.mult).then_inc(final, 1)



def _component_major(x):
    import numpy as np
    n = x.shape[0]
    return np.concatenate([x[:, :S], x[:, S:].reshape(n, V, 3).transpose(0, 2, 1).reshape(n, 3 * V)], axis=1)


def _layout(inputs):
    import numpy as np
    i = {k: np.asarray(a) for k, a in inputs.items()}
    f = np.float32

    def tiles(a, fill):
        a = a.reshape(E, -1)
        p = np.full((EA, a.shape[1]), fill, a.dtype)
        p[:E] = a
        return p.reshape(TA, P, -1).transpose(1, 0, 2).reshape(P, -1)

    def wide(a):
        p = np.zeros((a.shape[1], EA), f)
        p[:, :E] = a.T
        return p

    x = np.zeros((NB * P, D), f)
    x[:N] = _component_major(i["x"])
    a = np.zeros((NB * P,), f)
    a[:N] = i["node_vec1"][:, 0]
    o = {
        "x_in": x, "a_t": a.reshape(NB, P).T,
        "src_t": tiles(i["src"], PAD_SRC), "dst_t": tiles(i["dst"], PAD_DST),
        "attr4_t": tiles(i["edge_attr_4"], 0),
        "a16T": wide(i["edge_attr_16"]), "a8T": wide(i["edge_attr_8"]), "a10T": wide(i["edge_attr_10"]),
        "wu_ss": i["L1_gnn_Wu_ss"].reshape(S * S, S), "wu_vv": i["L1_gnn_Wu_vv"].reshape(V * V, S),
        "wu_sv": i["L1_gnn_Wu_sv"].reshape(S, V * V),
        "wu_vs": i["L1_gnn_Wu_vs"].transpose(1, 0, 2).reshape(S, V * V),
    }
    for k, w in i.items():
        if k.startswith("L") and "Wu_" not in k:
            o[k] = w
    return {k: np.ascontiguousarray(w) for k, w in o.items()}


def kernel(**inputs):
    import numpy as _np
    import concourse.bacc as _bacc
    from concourse import mybir as _mybir
    from concourse.bass_utils import run_bass_kernel_spmd as _run

    nc = _bacc.Bacc("TRN2", target_bir_lowering=False, num_devices=1)
    arrays, args = {}, {}
    for name, a in _layout(inputs).items():
        arrays[f"in_{name}"] = a
        args[name] = nc.dram_tensor(f"in_{name}", a.shape, _mybir.dt.from_np(a.dtype), kind="ExternalInput").ap()
    out = nc.dram_tensor("out_x", (NB * P, D), _mybir.dt.float32, kind="ExternalOutput").ap()
    gnn_kernel(nc, args, out)
    y = _run(nc, [arrays], core_ids=[0]).results[0]["out_x"][:N]
    vec = y[:, S:].reshape(N, 3, V).transpose(0, 2, 1).reshape(N, 3 * V)
    return _np.concatenate([y[:, :S], vec], axis=1)
```

```python
from contextlib import ExitStack
import math

import concourse.bass as bass
from concourse import mybir

F32 = mybir.dt.float32
BF16 = mybir.dt.bfloat16
I32 = mybir.dt.int32
ALU = mybir.AluOpType
ACT = mybir.ActivationFunctionType
AX = mybir.AxisListType
ds = bass.ds

P = 128
N = 3125
NB = 25
E = 103125
T = 816
TA = 832
EA = TA * P
BT = 4
R = 4
S, V, D = 64, 32, 160
EPS = 1e-5
PAD_DST = NB * P + P - 1
PAD_SRC = NB * P - 1
TWO_PI = (6.28125, 2029 / 2.0 ** 20, 2 * math.pi - 6.28125 - 2029 / 2.0 ** 20)
ROUND = 1.5 * 2.0 ** 23
U = 5
WX = 224
NREC = T * P + BT * P
AW = 608
CW = 162
GSS, GVV = 8, 2
NG = GSS + GVV
LAYERS = 4

R96, R32, R3 = 1 / math.sqrt(96.0), 1 / math.sqrt(32.0), 1 / math.sqrt(3.0)

FC = {
    0: dict(attr="a16T", k=16, h=64, c1=1 / 4.0, c2=1 / 8.0, act=ACT.Silu, cm=R96),
    2: dict(attr="a8T", k=8, h=64, c1=1 / math.sqrt(8.0), c2=1 / 8.0, act=ACT.Silu, cm=R96 / 4.0),
    3: dict(attr="a10T", k=10, h=100, c1=1 / math.sqrt(10.0), c2=math.sqrt(2.0) / 10.0, act=ACT.Relu,
            cm=R96 / 4.0 * 0.5),
}
W_FC = {0: ("L0_gnn_Wfc1", "L0_gnn_Wfc2"), 2: ("L2_gnn_fc_w1", "L2_gnn_fc_w2"), 3: ("L3_gnn_W_fc1", "L3_gnn_W_fc2")}
W_LIN = {0: ("L0_gnn_Wl1_0", "L0_gnn_Wl1_1"), 2: ("L2_gnn_lin1_w0", "L2_gnn_lin1_w1"),
         3: ("L3_gnn_W_l1_0", "L3_gnn_W_l1_1")}
W_SELF = {0: ("L0_gnn_Wsc0", "L0_gnn_Wsc1"), 1: ("L1_gnn_Lu_s", "L1_gnn_Lu_v"),
          2: ("L2_gnn_sc_w0", "L2_gnn_sc_w1"), 3: ("L3_gnn_W_si0", "L3_gnn_W_si1")}

CONV_ROWS = [("P0", h, 0) for h in range(2)] + [("P1", h, i) for i in range(3) for h in range(2)] \
    + [("P2", m, 0) for m in range(3)] + [("P3", m, 0) for m in range(3)]
CNT_COL = 32 * len(CONV_ROWS)
MW = CNT_COL + 4
WW = S + V
TP_PARTS = [(0, D, 0, 0), (0, D, 1, 160), (32, 96, 2, 320), (0, 96, 3, 416), (128, 96, 4, 0)]


def msg_rows():
    order = [("v", 1), ("s", 0), ("s", 1), ("v", 0), ("v", 2)]
    rows = []
    for kind, m in order:
        rows.append(("Lm_s", m, 0, S, 1 / 8) if kind == "s" else ("Lm_v", 0, S + V * m, V, R32))
    for kind, m in order:
        rows.append(("Wm_ss", m, 0, S, 1 / 8) if kind == "s" else ("Wm_vs", 0, S + V * m, V, R32))
    for i, part in ((0, "ssv"), (1, "vss"), (2, "vss")):
        half = 0
        for kind in part:
            if kind == "s":
                rows.append(("Wm_sv", half, S + V * i, V, 1 / 8))
                half += 1
            else:
                rows.append(("Wm_vv", 0, 0, S, R3 * R32))
    return rows


def gnn_kernel(nc, A, out):
    ctx = ExitStack()
    with ctx:
        def sb(name, shape, dt=F32):
            return ctx.enter_context(nc.sbuf_tensor(name, shape, dt))

        def sem(name):
            return ctx.enter_context(nc.semaphore(name))

        def scratch(name, shape, dt=F32):
            return nc.dram_tensor(name, shape, dt, kind="Internal").ap()

        table = {l: scratch(f"table{l}", (NB * P, D)) for l in (0, 2, 3)}
        table[1] = scratch("table1", ((NB + 1) * P, WX))
        agg_dram = {l: scratch(f"agg{l}", (NB * P, AW)) for l in range(4)}
        rec_dram = scratch("records", (NREC, 8))

        ident = sb("ident", [P, P])
        lower = sb("lower", [P, P])
        ones = sb("ones", [P, P])
        zeros_bf = sb("zeros_bf", [P, 512], BF16)
        iota = sb("iota", [P, P])
        blk_id = sb("blk_id", [P, NB])
        tile_id = sb("tile_id", [P, 7])
        node_id = sb("node_id", [P, P])
        av = sb("av", [P, NB])
        meta = sb("meta", [P, TA, 5])
        srci = sb("srci", [P, TA], I32)
        x_all = sb("x_all", [P, NB, D])
        self_all = sb("self_all", [P, NB, D])
        conv_all = sb("conv_all", [P, NB, CW])
        ebuf = sb("ebuf", [P, 5248])
        agg_in = sb("agg_in", [P, U, AW])
        aggT = sb("aggT", [P, U, 5 * P])
        gathered = sb("gathered", [P, R, BT, WX])
        idx_slot = sb("idx_slot", [P, R * BT], I32)
        meta_slot = sb("meta_slot", [P, BT, 5])
        dst_slot = sb("dst_slot", [P, BT])
        sh_slot = sb("sh_slot", [P, BT, 4])
        rec_slot = sb("rec_slot", [P, R * BT, 8])
        attrT = sb("attrT", [P, BT * P])
        hidT = sb("hidT", [P, BT * P])
        agg_stage = sb("agg_stage", [P, AW])
        xs = sb("xs", [P, U, D])
        xsT = sb("xsT", [P, U, 2 * P])
        row_out = sb("row_out", [P, U, WX])
        small = sb("small", [P, 16, NB])
        stats = sb("stats", [P, NB, 6])
        tab_i = {l: sb(f"tab_{l}", [1, 3, NB], I32) for l in ("dst", "src")}

        o0 = 0
        sel = ebuf[:, o0:o0 + BT * 5 * P].rearrange("p (j k n) -> p j k n", j=BT, k=5)
        msg = ebuf[:, o0:o0 + BT * MW].rearrange("p (j c) -> p j c", j=BT)
        o1 = o0 + BT * MW
        wsh = ebuf[:, o1:o1 + BT * 4 * WW].rearrange("p (j k c) -> p j k c", j=BT, k=4)
        o2 = o1 + BT * 4 * WW
        hot = ebuf[:, o2:o2 + BT * P].rearrange("p (j n) -> p j n", j=BT)
        zs = ebuf[:, 0:4 * 1024].rearrange("p (k c) -> p k c", k=4)
        zT = ebuf[:, 4 * 1024:5 * 1024].rearrange("p (h c) -> p h c", h=2)
        zv = aggT[:, :, :].rearrange("p k c -> p (k c)")[:, 0:3 * 1024].rearrange("p (i c) -> p i c", i=3)
        tt = agg_in[:, :, :].rearrange("p k c -> p (k c)")[:, 0:2048]
        sort_v = ebuf[:, 0:5 * T].rearrange("p (c t) -> p c t", c=5)
        blk_i = ebuf[:, 5 * T:6 * T].bitcast(I32)

        pack = {l: 2 if f["h"] <= P // 2 else 1 for l, f in FC.items()}
        hrows = {l: pack[l] * f["h"] for l, f in FC.items()}
        hcols = {l: BT * P // pack[l] for l in FC}
        w1 = {l: sb(f"w1_{l}", [P, hrows[l]]) for l in FC}
        w2 = {l: sb(f"w2_{l}", [P, pack[l], 2 * WW]) for l in FC}
        wconv = {l: sb(f"wconv_{l}", [P, 4, 161]) for l in FC}
        wmsg = sb("wmsg", [P, 5, D])
        wa = {l: sb(f"wa_{l}", [P, 2, P]) for l in range(4)}
        wb = {l: sb(f"wb_{l}", [V, 2, V]) for l in range(4)}
        wu_ss = sb("wu_ss", [P, GSS * 4, S])
        wu_vv = sb("wu_vv", [P, 8, S])
        wu_sv = sb("wu_sv", [S, V * V])
        wu_vs = sb("wu_vs", [S, V * V])
        upd = sb("upd", [P, 2, D])
        row_scale = {l: sb(f"row_scale{l}", [P, 5]) for l in range(4)}
        wa_scale = sb("wa_scale", [P, 1])
        blk128 = sb("blk128", [P, NB])
        tile_mm = sb("tile_mm", [P, 2, 7])
        tile_lim = sb("tile_lim", [P, 2, 7])
        hit = sb("hit", [P, 2, NB, 7])
        rng = sb("rng", [P, 2 * NB])
        rng_max = sb("rng_max", [2 * NB, 1])
        trow = sb("trow", [1, 4, NB])
        tri = sb("tri", [1, NB], I32)
        zrow = sb("zrow", [P, T])
        scat_rec = sb("scat_rec", [P, 2, 8, 8])
        scat_idx = sb("scat_idx", [P, 2, 8], I32)

        banks = [ctx.enter_context(nc.psum_tensor(f"bank{i}", [P, 512], F32)) for i in range(8)]
        ps_hid, ps_w, ps_agg, ps_agg2 = banks[0], banks[1:3], banks[3], banks[4]

        bar = sem("bar")
        w_zero, loads, w_in, w_scaled = sem("w_zero"), sem("loads"), sem("w_in"), sem("w_scaled")
        consts = sem("consts")
        go = sem("go")
        vch = sem("vch")
        pch = sem("pch")
        out_done = sem("out_done")

        bars = {}

        def barrier(eng, name):
            k = bars.get(name, 0) + 1
            bars[name] = k
            eng.drain().then_inc(bar, 1)
            eng.wait_ge(bar, 5 * k)

        chain = [0]

        def link(ins):
            chain[0] += 1
            ins.then_inc(vch, 1)
            nc.vector.wait_ge(vch, chain[0])

        block = ctx.enter_context(nc.Block())

        w_loads = []
        for l, f in FC.items():
            w_loads += [(w1[l][h * f["k"]:(h + 1) * f["k"], h * f["h"]:(h + 1) * f["h"]], A[W_FC[l][0]])
                        for h in range(pack[l])]
            for c0, src0, n in ((0, 0, S), (S, 2 * S, V), (WW, S, S), (WW + S, 2 * S + V, V)):
                w_loads += [(w2[l][h * f["h"]:(h + 1) * f["h"], h, c0:c0 + n], A[W_FC[l][1]][:, src0:src0 + n])
                            for h in range(pack[l])]
            w_loads += [(wa[l][0:S, 0, 0:S], A[W_LIN[l][0]]), (wb[l][:, 0, :], A[W_LIN[l][1]])]
            w_loads += [(wa[l][S + V * m:S + V * m + V, 0, S + V * m:S + V * m + V], A[W_LIN[l][1]]) for m in (0, 1)]
            for r, (what, h, i) in enumerate(CONV_ROWS):
                q, c = 32 * (r % 4), r // 4
                dst = wconv[l][q:q + 32, c, :]
                if l == 0:
                    ws, wv, wg = A["L0_gnn_Wl2_s"], A["L0_gnn_Wl2_v"], A["L0_gnn_Wa"]
                    ws, wv = [ws[0:32], ws[32:64], ws[64:96]], [wv[0:32], wv[32:64], wv[64:96]]
                elif l == 2:
                    ws, wv, wg = A["L2_gnn_lin2_w0"], A["L2_gnn_lin2_w1"], A["L2_gnn_lin3_w"]
                    ws, wv = [ws[0:32], ws[32:64], ws[64:96]], [wv[0:32], wv[32:64], wv[64:96]]
                else:
                    ws = [A["L3_gnn_W_l2_00"][0:32], A["L3_gnn_W_l2_00"][32:64], A["L3_gnn_W_l2_10"]]
                    wv = [A["L3_gnn_W_l2_01"][0:32], A["L3_gnn_W_l2_01"][32:64], A["L3_gnn_W_l2_11"]]
                    wg = None
                if what in ("P0", "P3"):
                    part = h if what == "P0" else 2
                    w_loads.append((dst[:, 0:S], ws[part]))
                    if wg is not None:
                        w_loads.append((dst[:, D:D + 1], wg[32 * part:32 * part + 32, :]))
                else:
                    part, m = (h, i) if what == "P1" else (2, h)
                    w_loads.append((dst[:, S + V * m:S + V * m + V], wv[part]))
        for l, (w0, w1n) in W_SELF.items():
            w_loads += [(wa[l][0:S, 1, 0:S], A[w0]), (wb[l][:, 1, :], A[w1n])]
            w_loads += [(wa[l][S + V * m:S + V * m + V, 1, S + V * m:S + V * m + V], A[w1n]) for m in (0, 1)]
        for r, (name, h, c0, cn, _) in enumerate(msg_rows()):
            w_loads.append((wmsg[32 * (r % 4):32 * (r % 4) + 32, r // 4, c0:c0 + cn],
                            A["L1_gnn_" + name][32 * h:32 * h + 32, :]))
        w_loads += [(wu_ss[:, :, :], A["wu_ss"].rearrange("(c p) w -> p c w", p=P)),
                    (wu_vv[:, :, :], A["wu_vv"].rearrange("(c p) w -> p c w", p=P)),
                    (wu_sv[:, :], A["wu_sv"]), (wu_vs[:, :], A["wu_vs"])]
        half = len(w_loads) // 2

        both = ("meta_ready", "idx_in")
        sems = {}
        asem = {n: sem(n) for n in ("agg_closed", "agg_out", "agg_stored", "node_ids")}
        for l in range(4):
            names = both + (() if l == 1 else ("attr_in", "hid_ps", "sh_ready"))
            sems[l] = {n: sem(f"{n}_{l}") for n in names}
            for n, k in (("got", BT), ("prod_ready", BT), ("sel_done", BT)) + \
                    ((("hot_ready", BT), ("act_sel", BT)) if l == 1 else
                     (("wsh_ready", BT), ("w_ready", BT // 2), ("hid_ready", 3 - pack[l]))):
                sems[l][n] = [sem(f"{n}{j}_{l}") for j in range(k)]
        nsem = {n: sem("n_" + n) for n in ("aT_ps", "aT", "conv_ps", "conv", "func_in", "func_out")}
        nsem["in"] = [sem(f"n_in{k}") for k in range(U)]
        psem = {n: sem("p_" + n) for n in ("xs", "xT_ps", "xT", "out_ps", "row", "back")}
        psem["stored"] = [sem(f"p_stored{k}") for k in range(U)]
        bsem = {n: sem("b_" + n) for n in ("ax", "axT_ps", "axT", "y_ps", "y_used", "z_s", "z_v", "zT_ps", "zT",
                                           "z_mm", "done")}
        ssem = {n: sem("s_" + n) for n in ("cnt", "off", "range_ps", "range_in", "dstf")}
        srt, final = sem("srt"), sem("final")
        sc_slot = [sem(f"sc_slot{h}") for h in range(2)]
        sc_done = [[sems[2 * h + j // BT]["got"][j % BT] for j in range(8)] for h in range(2)]
        GOT0 = 16 * (T // 16)
        stats_sem = sem("stats_sem")
        bil_own = sem("bil_own")
        rec_fill = sem("rec_fill")

        def table_reg(eng, tab, row, b, hi):
            return eng.value_load(tab[0:1, row, ds(b, 1)], min_val=0, max_val=hi)

        def bounded(v, hi):
            return nc.s_assert_within(v, 0, hi, skip_runtime_bounds_check_because=
                                      "a body starts before its block's end, or at an empty block's start")

        def rounds(eng, n, body):
            body(0, True)
            with eng.Fori(1, n) as u:
                body(u, False)

        credits = []
        for l in range(4):
            q = sems[l]
            credits += [(c, R) for c in q["prod_ready"] + q["sel_done"]]
            if l != 1:
                credits += [(q["meta_ready"], R - 1), (q["hid_ps"], R - 2), (q["sh_ready"], R - 1)]
                credits += [(c, R) for c in q["wsh_ready"]] + [(c, R - 1) for c in q["w_ready"] + q["hid_ready"]]
            else:
                credits += [(q["meta_ready"], R)] + [(c, R) for c in q["act_sel"] + q["hot_ready"]]
        credits += [(asem["agg_out"], 1)]
        credits += [(nsem[n], U) for n in ("aT", "conv", "conv_ps")]
        credits += [(psem[n], U) for n in ("xT_ps", "xT", "out_ps", "row", "back")]
        credits += [(bsem[n], 1) for n in ("done", "y_used", "axT_ps", "y_ps")]
        credits += [(bsem["zT_ps"], NG), (bsem["zT"], 2), (bsem["z_mm"], 2)]

        def pair_end(k):
            return min(k // 2 * 2 + 2, U)

        def conv_end(k, l):
            return 3 if k < 3 and l != 1 else U

        def table_of(l):
            return tab_i["src"] if l == 1 else tab_i["dst"]

        MAXB = NB * (TA // BT)

        def chunks(l):
            return [128, 128, 128, 128, 96] if l == 1 else [128, 128, 128, 64]

        @block.sync
        def _(sp):
            sp.dma_start(srci[:, :], A["src_t"]).then_inc(loads, 16)
            sp.dma_start(av[:, :], A["a_t"]).then_inc(loads, 16)
            sp.dma_start(ebuf[:, 0:TA].bitcast(I32), A["dst_t"]).then_inc(loads, 16)
            sp.dma_start(ebuf[:, TA:5 * TA], A["attr4_t"]).then_inc(loads, 16)
            sp.dma_start(x_all[:, :, :], A["x_in"].rearrange("(b p) d -> p b d", p=P)).then_inc(w_in, 16)
            sp.wait_ge(w_zero, 1)
            for dst, src in w_loads[:half]:
                sp.dma_start(dst, src).then_inc(w_in, 16)
            for l in range(4):
                sp.dma_start(idx_slot[:, 0:BT], A["src_t"][:, 0:BT]).then_inc(sems[l]["idx_in"], 16)
                sp.wait_ge(sems[l]["idx_in"], 16)
            barrier(sp, "sp")

            def publish(l):
                with sp.Fori(0, NB // U) as u:
                    for k in range(U):
                        sp.wait_ge(psem["row"], NB * l + u * U + k + 1 + U)
                        w = WX if l == 1 else D
                        sp.dma_start(table[l][ds((u * U + k) * P, P), :], row_out[:, k, 0:w])\
                            .then_inc(psem["stored"][k], 16)
                for k in range(U):
                    sp.wait_ge(psem["stored"][k], 16 * (NB // U) * (l + 1))

            publish(0)
            barrier(sp, "sp")
            for l in range(LAYERS):
                q = sems[l]
                tab = table_of(l)

                def indices(g, tile):
                    for j in range(BT):
                        sp.wait_ge(q["got"][j], g * 16 + (GOT0 + 16 - 16 * R))
                    sp.sem_inc(go, 1)
                    if l == 1:
                        sp.wait_ge(q["meta_ready"], g + 1)
                        sp.sem_inc(go, 1)
                    sp.wait_ge(q["idx_in"], g * 16 + 16)
                    sp.sem_inc(go, 1)
                    if l == 1:
                        sp.dma_start(rec_slot[:, ds(g % R * BT, BT), :],
                                     rec_dram[ds(tile, BT * P), :].rearrange("(p j) c -> p j c", j=BT))\
                            .then_inc(q["idx_in"], 16)
                    else:
                        sp.dma_start(idx_slot[:, ds(g % R * BT, BT)], A["src_t"][:, ds(tile, BT)])\
                            .then_inc(q["idx_in"], 16)

                def attributes(first):
                    k, n = FC[l]["k"], hcols[l]
                    for h in range(pack[l]):
                        sp.dma_start(attrT[h * k:(h + 1) * k, 0:n], A[FC[l]["attr"]][:, ds(first + h * n, n)])\
                            .then_inc(q["attr_in"], 16)

                with sp.Fori(0, NB) as b:
                    n = table_reg(sp, tab, 0, b, MAXB)
                    base = table_reg(sp, tab, 1, b, MAXB)
                    start = table_reg(sp, tab, 2, b, NREC)
                    with sp.Fori(0, n) as i:
                        if l == 1:
                            indices(base + i, bounded(start + i * (BT * P), T * P))
                        else:
                            sp.wait_ge(q["hid_ps"], base + i + R - 2)
                            attributes(bounded((start + i * BT) * P, (T - 1) * P))
                            indices(base + i, bounded(start + i * BT, T - 1))
                total = table_reg(sp, tab, 1, NB - 1, MAXB) + table_reg(sp, tab, 0, NB - 1, MAXB)
                if l != 1:
                    sp.wait_ge(q["hid_ps"], total + R - 2)
                    attributes(0)
                for r in range(R - 1):
                    indices(total + r, 0)
                sp.wait_ge(q["idx_in"], (total + R) * 16)
                sp.sem_inc(go, 1)
                barrier(sp, "sp")
                w = {0: CNT_COL + 1, 1: AW, 2: CNT_COL, 3: CNT_COL}[l]
                with sp.Fori(0, NB // U) as u:
                    for k in range(U):
                        sp.wait_ge(nsem["conv"], NB * l + u * U + k + 1)
                        sp.dma_start(agg_in[:, k, 0:w], agg_dram[l][ds((u * U + k) * P, P), 0:w])\
                            .then_inc(nsem["in"][k], 16)
                barrier(sp, "sp")
                if l == 1:
                    barrier(sp, "sp")
                if l < LAYERS - 1:
                    publish(l + 1)
                    barrier(sp, "sp")
            sp.wait_ge(final, NB)
            sp.dma_start(out.rearrange("(b p) d -> p b d", p=P), x_all[:, :, :]).then_inc(out_done, 16)
            sp.wait_ge(out_done, 16)

        @block.gpsimd
        def _(pool):
            def held():
                pool.sem_inc(go, 1)

            pool.memset(ident[:, :], 0.0).then_inc(pch, 1)
            pool.memset(lower[:, :], 1.0).then_inc(pch, 1)
            pool.memset(ones[:, :], 1.0).then_inc(consts, 1)
            pool.memset(zeros_bf[:, :], 0.0).then_inc(consts, 1)
            pool.iota(iota[:, :], [[1, P]], base=0, channel_multiplier=0,
                      allow_small_or_imprecise_dtypes=True).then_inc(consts, 1)
            pool.iota(blk_id[:, :], [[1, NB]], base=0, channel_multiplier=0,
                      allow_small_or_imprecise_dtypes=True).then_inc(consts, 1)
            pool.iota(tile_id[:, :], [[P, 7]], base=0, channel_multiplier=1,
                      allow_small_or_imprecise_dtypes=True).then_inc(consts, 1)
            pool.wait_ge(pch, 2)
            pool.affine_select(out=ident[:, :], in_=ident[:, :], compare_op=ALU.not_equal, fill=1.0, base=0,
                               pattern=[[-1, P]], channel_multiplier=1).then_inc(consts, 1)
            pool.affine_select(out=lower[:, :], in_=lower[:, :], compare_op=ALU.is_gt, fill=0.0, base=0,
                               pattern=[[1, P]], channel_multiplier=-1).then_inc(consts, 1)
            pool.memset(agg_stage[:, :], 0.0).then_inc(pch, 1)
            pool.wait_ge(pch, 3)
            pool.memset(agg_stage[:, 0:8 * BT].rearrange("p (j c) -> p j c", c=8)[:, :, 1:2], -1.0).then_inc(pch, 1)
            pool.wait_ge(pch, 4)
            pool.dma_start(rec_dram[T * P:NREC, :].rearrange("(p j) c -> p (j c)", j=BT),
                           agg_stage[:, 0:8 * BT]).then_inc(rec_fill, 16)
            pool.dma_start(table[1][NB * P:(NB + 1) * P, :], agg_stage[:, 64:64 + WX]).then_inc(rec_fill, 16)
            pool.wait_ge(rec_fill, 32)
            barrier(pool, "pool")
            with pool.Fori(0, T // 16) as i:
                for h in range(2):
                    pool.wait_ge(sc_slot[h], i + 1)
                    held()
                    for j in range(8):
                        pool.indirect_dma_start(
                            rec_dram[:, :], bass.IndirectOffsetOnAxis(ap=scat_idx[:, h, j:j + 1], axis=0),
                            scat_rec[:, h, j, :], None).then_inc(sc_done[h][j], 16)
            for h in range(2):
                for j in range(8):
                    pool.wait_ge(sc_done[h][j], 16 * (T // 16))
            barrier(pool, "pool")
            for l in range(LAYERS):
                q = sems[l]
                tab = table_of(l)
                w = WX if l == 1 else D
                total = table_reg(pool, tab, 1, NB - 1, MAXB) + table_reg(pool, tab, 0, NB - 1, MAXB)
                laps = (total + R - 1) // R
                with pool.Fori(0, laps) as i:
                    for h in range(R):
                        g = i * R + h
                        pool.wait_ge(q["idx_in"], g * 16 + 32)
                        held()
                        for j in range(BT):
                            pool.wait_ge(q["got"][j], g * 16 + GOT0)
                            if j == 0:
                                held()
                            pool.wait_ge(q["sel_done" if l == 1 else "prod_ready"][j], g + 1)
                            held()
                            s0 = h * BT + j
                            idx = rec_slot[:, s0, 0:1].bitcast(I32) if l == 1 else idx_slot[:, s0:s0 + 1]
                            pool.indirect_dma_start(
                                gathered[:, h, j, 0:w], None, table[l][:, :],
                                bass.IndirectOffsetOnAxis(ap=idx, axis=0)).then_inc(q["got"][j], 16)
                for j in range(BT):
                    pool.wait_ge(q["got"][j], laps * (16 * R) + GOT0)
                held()
                barrier(pool, "pool")
                barrier(pool, "pool")
                if l == 1:
                    z = bsem
                    with pool.Fori(0, NB) as b:
                        pool.wait_ge(z["zT_ps"], b * NG + NG)
                        held()
                        for i in range(3):
                            xv = x_all[:, ds(b, 1), S + V * i:S + V * i + V].rearrange("p o u -> p (o u)")
                            mv = conv_all[:, ds(b, 1), S + V * i:S + V * i + V].rearrange("p o u -> p (o u)")
                            pool.tensor_tensor(zv[:, i, :].rearrange("p (u v) -> p u v", v=V),
                                               xv.unsqueeze(2).broadcast_to([P, V, V]),
                                               mv.unsqueeze(1).broadcast_to([P, V, V]), ALU.mult)\
                                .then_inc(z["z_v"], 1)
                        for i in range(2):
                            pool.wait_ge(z["z_v"], b * 5 + 3 + i)
                            held()
                            pool.tensor_tensor(zv[:, 0, :], zv[:, 0, :], zv[:, 1 + i, :], ALU.add)\
                                .then_inc(z["z_v"], 1)
                    barrier(pool, "pool")
                if l < LAYERS - 1:
                    barrier(pool, "pool")

        @block.scalar
        def _(act):
            act.wait_ge(w_zero, 1)
            for dst, src in w_loads[half:]:
                act.dma_start(dst, src).then_inc(w_in, 16)
            barrier(act, "act")
            act.wait_ge(w_in, 16 * (1 + len(w_loads)))

            def scale(w, by):
                return nc.scalar.activation(w, w, ACT.Copy, scale=by)

            for l in range(4):
                scale(wa[l][:, :, :], wa_scale[:, 0:1])
                scale(wb[l][:, 0 if l != 1 else 1:2, :], R32)
            for l, f in FC.items():
                scale(w1[l][:, :], f["c1"])
                scale(w2[l][:, :, :], f["c2"])
                for c in range(4):
                    scale(wconv[l][:, c, :], row_scale[l][:, c:c + 1])
            for c in range(5):
                scale(wmsg[:, c, :], row_scale[1][:, c:c + 1])
            scale(wu_ss[:, :, :], 1 / 64)
            scale(wu_vv[:, :, :], R3 / 32)
            scale(wu_sv[:, :], 1 / math.sqrt(2048.0))
            scale(wu_vs[:, :], 1 / math.sqrt(2048.0)).then_inc(w_scaled, 1)

            def publish(l):
                q = psem

                def body(u, first):
                    for k in range(U):
                        g = u * U + k
                        tp = banks[5 + k // 2][:, 256 * (k % 2):256 * (k % 2) + 256]
                        act.wait_ge(q["xT_ps"], NB * l + u * U + pair_end(k) + U)
                        act.wait_ge(q["out_ps"], NB * l + g + 1)
                        nc.scalar.activation(xsT[:, k, 0:P], tp[:, 0:P], ACT.Copy)
                        nc.scalar.activation(xsT[0:V, k, P:2 * P], tp[0:V, P:2 * P], ACT.Copy).then_inc(q["xT"], 1)
                    for k in range(U):
                        if l > 0:
                            nc.scalar.activation(x_all[:, ds(u * U + k, 1), :], xs[:, k:k + 1, :], ACT.Copy)\
                                .then_inc(q["back"], 1)

                rounds(act, NB // U, body)

            publish(0)
            barrier(act, "act")
            for l in range(LAYERS):
                q = sems[l]
                tab = table_of(l)

                def hidden(g, h):
                    act.wait_ge(q["hid_ps"], g + R)
                    for half in ((0, 1) if pack[l] == 2 else (h,)):
                        act.wait_ge(q["w_ready"][half], g + R)
                    hidden_out(h)

                def hidden_out(h):
                    r, n = hrows[l], 2 * P
                    nc.scalar.activation(hidT[0:r, n * h:n * h + n], ps_hid[0:r, n * h:n * h + n], FC[l]["act"])\
                        .then_inc(q["hid_ready"][h], 1)

                if l != 1:
                    act.wait_ge(q["hid_ps"], R - 1)
                    for h in range(3 - pack[l]):
                        hidden_out(h)
                if l == 0:
                    act.dma_start(agg_dram[l][0:P, 0:NB], av[:, :]).then_inc(asem["agg_stored"], 16)
                with act.Fori(0, NB) as b:
                    n = table_reg(act, tab, 0, b, MAXB)
                    base = table_reg(act, tab, 1, b, MAXB)
                    if l == 1:
                        with act.Fori(0, n) as i:
                            g = base + i
                            for j in range(BT):
                                act.wait_ge(q["hot_ready"][j], g + R + 1)
                                for k, c in ((3, 1), (4, 2)):
                                    last = nc.scalar.activation(sel[:, j, k, :], sel[:, j, 0, :], ACT.Copy,
                                                                scale=meta_slot[:, j, c + 1:c + 2])
                                last.then_inc(q["act_sel"][j], 1)
                    else:
                        start = table_reg(act, tab, 2, b, NREC)
                        with act.Fori(0, n) as i:
                            g = base + i
                            act.wait_ge(q["wsh_ready"][BT - 1], g + R)
                            act.sem_inc(go, 1)
                            nc.scalar.activation(sh_slot[:, :, :], meta[:, ds(bounded(start + i * BT, T - 1), BT), 0:4],
                                                 ACT.Copy).then_inc(q["sh_ready"], 1)
                            act.wait_ge(q["sh_ready"], g + R)
                            for j in range(BT):
                                if j % 2 == 0:
                                    act.wait_ge(q["w_ready"][j // 2], g + R)
                                act.wait_ge(q["prod_ready"][j], g + R)
                                w = ps_w[j // 2][:, 2 * WW * (j % 2):2 * WW * (j % 2) + 2 * WW]
                                for k in range(4):
                                    c0 = WW if k else 0
                                    last = nc.scalar.activation(wsh[:, j, k, :], w[:, c0:c0 + WW], ACT.Copy,
                                                                scale=sh_slot[:, j, k:k + 1])
                                last.then_inc(q["wsh_ready"][j], 1)
                                if 2 <= j < 5 - pack[l]:
                                    hidden(g, j - 2)
                    act.wait_ge(asem["agg_closed"], NB * l + b + 1)
                    act.wait_ge(asem["agg_stored"], b * 16 + (16 * NB * l + 16))
                    if l == 1:
                        nc.scalar.activation(agg_stage[:, 0:512], ps_agg[:, 0:512], ACT.Copy)
                        nc.scalar.activation(agg_stage[:, 512:AW], ps_agg2[:, 0:96], ACT.Copy)\
                            .then_inc(asem["agg_out"], 1)
                        w = AW
                    else:
                        w = CNT_COL + 1 if l == 0 else CNT_COL
                        nc.scalar.activation(agg_stage[:, 0:w], ps_agg[:, 0:w], ACT.Copy).then_inc(asem["agg_out"], 1)
                    act.wait_ge(asem["agg_out"], NB * l + b + 2)
                    act.dma_start(agg_dram[l][ds(b * P, P), 0:w], agg_stage[:, 0:w]).then_inc(asem["agg_stored"], 16)
                act.wait_ge(asem["agg_stored"], 16 * NB * (l + 1) + 16)
                barrier(act, "act")
                r = nsem
                with act.Fori(0, NB // U) as u:
                    for k in range(U):
                        act.wait_ge(r["aT_ps"], NB * l + u * U + (U if l == 1 else k + 1))
                        act.wait_ge(r["conv_ps"], NB * l + u * U + k + 1)
                        last = chunks(l)[3]
                        nc.scalar.activation(aggT[:, k, 0:384], banks[k][:, 0:384], ACT.Copy)
                        ins = nc.scalar.activation(aggT[0:last, k, 384:512], banks[k][0:last, 384:512], ACT.Copy)
                        if l == 1:
                            bk, c = (7, P * k) if k < 4 else (6, 352)
                            ins = nc.scalar.activation(aggT[0:96, k, 512:640], banks[bk][0:96, c:c + P], ACT.Copy)
                        ins.then_inc(r["aT"], 1)
                if l == 2:
                    act.wait_ge(r["func_in"], l + 1)
                    nc.scalar.activation(small[:, 8:10, :], small[:, 6:8, :], ACT.Sin).then_inc(r["func_out"], 1)
                barrier(act, "act")
                if l == 1:
                    z = bsem
                    with act.Fori(0, NB) as b:
                        act.wait_ge(z["axT_ps"], b + 1)
                        act.sem_inc(go, 1)
                        nc.scalar.activation(xs[:, 0:1, 0:P], conv_all[:, ds(b, 1), 0:P], ACT.Copy)
                        nc.scalar.activation(xs[:, 1:2, 0:P], x_all[:, ds(b, 1), 0:P], ACT.Copy).then_inc(z["ax"], 1)
                        act.wait_ge(z["axT_ps"], b + 2)
                        act.wait_ge(z["y_ps"], b + 1)
                        nc.scalar.activation(xsT[0:S, 0, :], banks[0][0:S, 0:2 * P], ACT.Copy).then_inc(z["axT"], 1)
                        for q in range(NG):
                            n = b * NG + q
                            act.wait_ge(z["zT_ps"], n + 1 + NG)
                            act.wait_ge(z["z_mm"], n + 1)
                            nc.scalar.activation(zT[:, q % 2, :], banks[1 + q % 2][:, :], ACT.Copy)\
                                .then_inc(z["zT"], 1)
                    barrier(act, "act")
                act.wait_ge(r["func_in"], l + 1 + (l >= 2))
                nc.scalar.activation(small[:, 12, :], small[:, 11, :], ACT.Sqrt).then_inc(r["func_out"], 1)
                if l < LAYERS - 1:
                    publish(l + 1)
                    barrier(act, "act")

        @block.tensor
        def _(pe):
            mm, tr = nc.tensor.matmul, nc.tensor.transpose
            pe.wait_ge(consts, 7)
            pe.wait_ge(ssem["dstf"], 1)
            for c in range(7):
                w = min(P, T - P * c)
                last = tr(banks[1 + c // 4][0:w, P * (c % 4):P * (c % 4) + P], sort_v[:, 4, P * c:P * c + w], ident[:, :])
            last.then_inc(ssem["range_ps"], 1)
            pe.wait_ge(ssem["range_in"], 1)
            tr(banks[3][0:2 * NB, 0:P], rng[:, :], ident[:, :]).then_inc(ssem["range_ps"], 1)
            pe.wait_ge(ssem["range_in"], 2)
            tr(banks[4][0:1, 0:2 * NB], rng_max[:, 0:1], ident[0:2 * NB, 0:2 * NB]).then_inc(ssem["range_ps"], 1)
            pe.wait_ge(ssem["cnt"], 1)
            mm(banks[0][:, 0:NB], lower[:, :], small[:, 0, :], start=True, stop=True)
            mm(banks[0][:, NB:2 * NB], ones[:, :], small[:, 0, :], start=True, stop=True).then_inc(ssem["off"], 1)
            barrier(pe, "pe")
            pe.wait_ge(w_scaled, 1)

            def publish(l):
                q = psem
                with pe.Fori(0, NB // U) as u:
                    for k in range(U):
                        g = u * U + k
                        tp = banks[5 + k // 2][:, 256 * (k % 2):256 * (k % 2) + 256]
                        pe.wait_ge(q["xs"], NB * l + g + 1)
                        pe.wait_ge(q["xT"], NB * l + u * U + pair_end(k))
                        tr(tp[:, 0:P], xs[:, k, 0:P], ident[:, :])
                        tr(tp[0:V, P:2 * P], xs[:, k, P:D], ident[:, :]).then_inc(q["xT_ps"], 1)
                    for k in range(U):
                        g = u * U + k
                        pe.wait_ge(q["xT"], NB * l + g + 1 + U)
                        pe.wait_ge(q["row"], NB * l + g + 1)
                        o = banks[k][:, 0:2 * D].rearrange("p (j c) -> p j c", j=2)
                        j0 = 1 if l == 1 else 0
                        mm(o[:, j0:2, 0:P], xsT[:, k, 0:P], wa[l][:, j0:2, :], start=True, stop=True)
                        mm(o[:, j0:2, P:D], xsT[0:V, k, P:2 * P], wb[l][:, j0:2, :], start=True, stop=True)\
                            .then_inc(q["out_ps"], 1)

            publish(0)
            barrier(pe, "pe")
            for l in range(LAYERS):
                q = sems[l]
                tab = table_of(l)
                wagg = 512 if l == 1 else (CNT_COL + 1 if l == 0 else CNT_COL)

                def hidden(g):
                    pe.wait_ge(q["attr_in"], (g + 1) * (16 * pack[l]))
                    for h in range(3 - pack[l]):
                        pe.wait_ge(q["hid_ready"][h], g + R - 1)
                    mm(ps_hid[0:hrows[l], 0:hcols[l]], w1[l][:, :], attrT[:, 0:hcols[l]], start=True, stop=True)\
                        .then_inc(q["hid_ps"], 1)

                def weights(g, j0):
                    pe.wait_ge(q["hid_ready"][0 if pack[l] == 2 else j0 // 2], g + R)
                    pe.wait_ge(q["wsh_ready"][j0 + 1], g + R)
                    for j in (j0, j0 + 1):
                        last = mm(ps_w[j0 // 2][:, 2 * WW * (j % 2):2 * WW * (j % 2) + 2 * WW],
                           hidT[:, P * j % hcols[l]:P * j % hcols[l] + P], w2[l][:, P * j // hcols[l], :],
                           start=True, stop=True)
                    last.then_inc(q["w_ready"][j0 // 2], 1)

                def aggregate(g, *tiles):
                    for j in tiles:
                        pe.wait_ge(q["prod_ready"][j], g + R + 1)
                        mm(ps_agg[:, 0:wagg], hot[:, j, :], msg[:, j, 0:wagg], start=False, stop=False)\
                            .then_inc(q["sel_done"][j], 1)

                if l != 1:
                    pe.wait_ge(q["attr_in"], 16 * pack[l])
                    mm(ps_hid[0:hrows[l], 0:hcols[l]], w1[l][:, :], attrT[:, 0:hcols[l]], start=True, stop=True)\
                        .then_inc(q["hid_ps"], 1)
                    weights(0, 0)
                with pe.Fori(0, NB) as b:
                    n = table_reg(pe, tab, 0, b, MAXB)
                    base = table_reg(pe, tab, 1, b, MAXB)
                    pe.wait_ge(asem["agg_out"], NB * l + b + 1)
                    mm(ps_agg[:, 0:wagg], zeros_bf[:, 0:P], zeros_bf[:, 0:wagg], start=True, stop=False)
                    if l == 1:
                        mm(ps_agg2[:, 0:96], zeros_bf[:, 0:P], zeros_bf[:, 0:96], start=True, stop=False)
                    with pe.Fori(0, n) as i:
                        g = base + i
                        if l != 1:
                            weights(g, 2)
                            hidden(g + 1)
                            aggregate(g, 0, 1)
                            weights(g + 1, 0)
                            aggregate(g, 2, 3)
                        else:
                            for j in range(BT):
                                pe.wait_ge(q["prod_ready"][j], g + R + 1)
                                pe.wait_ge(q["act_sel"][j], g + R + 1)
                                pe.wait_ge(q["got"][j], g * 16 + (GOT0 + 16))
                                for s0, w, k, c0 in TP_PARTS:
                                    dst = ps_agg2 if k == 4 else ps_agg
                                    last = mm(dst[:, c0:c0 + w], sel[:, j, k, :],
                                              gathered[:, ds(g % R, 1), j, s0:s0 + w].rearrange("p o c -> p (o c)"),
                                              start=False, stop=False)
                                last.then_inc(q["sel_done"][j], 1)
                    if l == 1:
                        mm(ps_agg2[:, 0:96], zeros_bf[:, 0:P], zeros_bf[:, 0:96], start=False, stop=True)
                    mm(ps_agg[:, 0:wagg], zeros_bf[:, 0:P], zeros_bf[:, 0:wagg], start=False, stop=True)\
                        .then_inc(asem["agg_closed"], 1)
                barrier(pe, "pe")
                r = nsem
                ch = chunks(l)
                with pe.Fori(0, NB // U) as u:
                    for k in range(U):
                        g = u * U + k
                        pe.wait_ge(r["in"][k], 16 * (NB // U) * l + u * 16 + 16)
                        pe.wait_ge(r["aT"], NB * l + u * U + (U if l == 1 else k + 1))
                        if l == 1:
                            pe.wait_ge(r["conv"], NB * l + u * U + U)
                        for c, rows in enumerate(ch):
                            bk, c0 = (k, P * c) if c < 4 else ((7, P * k) if k < 4 else (6, 352))
                            last = tr(banks[bk][0:rows, c0:c0 + P], agg_in[:, k, P * c:P * c + rows], ident[:, :])
                        last.then_inc(r["aT_ps"], 1)
                    for k in range(U):
                        g = u * U + k
                        w = D if l == 1 else 161
                        wt = wmsg if l == 1 else wconv[l]
                        pe.wait_ge(r["aT"], NB * l + u * U + (U if l == 1 else k + 1) + U)
                        pe.wait_ge(r["conv"], NB * l + u * U + conv_end(k, l))
                        o = banks[5 + k // 3][:, 161 * (k % 3):161 * (k % 3) + w] if k < 3 else \
                            banks[6][:, 161 * (k - 3):161 * (k - 3) + w]
                        for c, rows in enumerate(ch):
                            last = mm(o, aggT[0:rows, k, P * c:P * c + P], wt[0:rows, c, 0:w],
                                      start=(c == 0), stop=(c == len(ch) - 1))
                        last.then_inc(r["conv_ps"], 1)
                barrier(pe, "pe")
                if l == 1:
                    z = bsem

                    def transposed(b, q):
                        if q < GSS:
                            src = zs[:, q // 2, :]
                            if q % 2 == 0:
                                pe.wait_ge(z["z_s"], b * 4 + q // 2 + 1)
                        else:
                            src = zv[:, 0, :]
                            if q % 2 == 0:
                                pe.wait_ge(z["z_v"], b * 5 + 5)
                        pe.wait_ge(z["zT"], b * NG + q + 1)
                        for c in range(4):
                            c0 = 512 * (q % 2) + P * c
                            last = tr(banks[1 + q % 2][:, P * c:P * c + P], src[:, c0:c0 + P], ident[:, :])
                        last.then_inc(z["zT_ps"], 1)

                    with pe.Fori(0, NB) as b:
                        pe.wait_ge(z["ax"], b + 1)
                        for h in range(2):
                            last = tr(banks[0][:, P * h:P * h + P], xs[:, h, 0:P], ident[:, :])
                        last.then_inc(z["axT_ps"], 1)
                        pe.wait_ge(z["axT"], b + 1)
                        pe.wait_ge(z["y_used"], b + 1)
                        for c in range(4):
                            h, wt = (1, wu_sv) if c < 2 else (0, wu_vs)
                            last = mm(banks[4 + c][:, :], xsT[0:S, 0, P * h:P * h + P],
                                      wt[:, 512 * (c % 2):512 * (c % 2) + 512], start=True, stop=True)
                        last.then_inc(z["y_ps"], 1)
                        transposed(b, 0)
                        for q in range(NG):
                            if q + 1 < NG:
                                transposed(b, q + 1)
                            pe.wait_ge(z["zT"], b * NG + q + 1 + 2)
                            if q == 0:
                                pe.wait_ge(z["done"], b + 1)
                            for c in range(4):
                                wt = wu_ss[:, 4 * q + c, :] if q < GSS else wu_vv[:, 4 * (q % 2) + c, :]
                                last = mm(banks[3][:, 0:S], zT[:, q % 2, P * c:P * c + P], wt,
                                          start=(q == 0 and c == 0), stop=(q == NG - 1 and c == 3))
                            last.then_inc(z["z_mm"], 1)
                    barrier(pe, "pe")
                if l < LAYERS - 1:
                    publish(l + 1)
                    barrier(pe, "pe")

        @block.vector
        def _(dve):
            v = nc.vector
            for l in FC:
                v.memset(wconv[l][:, :, :], 0.0)
                v.memset(w1[l][:, :], 0.0)
                v.memset(w2[l][:, :, :], 0.0)
            v.memset(attrT[:, :], 0.0)
            v.memset(hidT[:, :], 0.0)
            for l in range(4):
                v.memset(wa[l][:, :, :], 0.0)
            v.memset(wmsg[:, :, :], 0.0).then_inc(w_zero, 1)
            for l in FC:
                for r, (what, _, _) in enumerate(CONV_ROWS):
                    q0 = 32 * (r % 4)
                    v.memset(row_scale[l][q0:q0 + 32, r // 4:r // 4 + 1], FC[l]["cm"] * (R3 if what == "P3" else 1.0))
                v.memset(row_scale[l][64:P, 3:4], 0.0)
            for r, (_, _, _, _, s) in enumerate(msg_rows()):
                q0 = 32 * (r % 4)
                last = v.memset(row_scale[1][q0:q0 + 32, r // 4:r // 4 + 1], s)
            v.memset(row_scale[1][96:P, 4:5], 0.0)
            v.memset(wa_scale[0:S, :], 1 / 8)
            link(v.memset(wa_scale[S:P, :], R32))
            dve.wait_ge(loads, 16 * 4)
            dve.wait_ge(consts, 7)
            v.tensor_scalar(blk128[:, :], blk_id[:, :], float(P), None, ALU.mult)
            link(v.memset(zrow[:, :], 0.0))
            for c, n in credits:
                dve.sem_inc(c, n)
            raw_dst = ebuf[:, 0:TA].bitcast(I32)
            link(v.tensor_copy(meta[:, :, 0:4], ebuf[:, TA:5 * TA].rearrange("p (t c) -> p t c", c=4)))
            link(v.tensor_copy(meta[:, :, 4:5], raw_dst.rearrange("p (t c) -> p t c", c=1)))
            link(v.tensor_scalar(blk_i[:, :], raw_dst[:, 0:T], 7, None, ALU.logical_shift_right))
            v.tensor_copy(sort_v[:, 4, :], blk_i[:, :]).then_inc(ssem["dstf"], 1)
            dve.wait_ge(ssem["dstf"], 1)
            link(v.tensor_scalar(blk_i[:, :], srci[:, 0:T], 7, None, ALU.logical_shift_right))
            blk, eq, cum, pos = (sort_v[:, c, :] for c in (0, 1, 2, 3))
            link(v.tensor_copy(blk, blk_i[:, :]))
            dve.wait_ge(ssem["range_ps"], 1)
            link(v.memset(tile_mm[:, :, :], 30.0))
            link(v.memset(tile_mm[:, 1, :], -1.0))
            for c in range(7):
                w = min(P, T - P * c)
                src = banks[1 + c // 4][0:w, P * (c % 4):P * (c % 4) + P]
                v.tensor_reduce(tile_mm[0:w, 0, c:c + 1], src, AX.X, ALU.min)
                link(v.tensor_reduce(tile_mm[0:w, 1, c:c + 1], src, AX.X, ALU.max))
            bb = blk_id[:, :].unsqueeze(2).broadcast_to([P, NB, 7])
            for r in range(2):
                src = tile_mm[:, r:r + 1, :].broadcast_to([P, NB, 7])
                link(v.tensor_tensor(hit[:, r, :, :], src, bb, (ALU.is_le, ALU.is_ge)[r]))
            link(v.tensor_tensor(hit[:, 0, :, :], hit[:, 0, :, :], hit[:, 1, :, :], ALU.mult))
            v.tensor_scalar(tile_lim[:, 0, :], tile_id[:, :], -1.0, float(T), ALU.mult, ALU.add)
            link(v.tensor_scalar(tile_lim[:, 1, :], tile_id[:, :], 1.0, None, ALU.add))
            for r in (1, 0):
                src = tile_lim[:, r:r + 1, :].broadcast_to([P, NB, 7])
                link(v.tensor_tensor(hit[:, 1, :, :], hit[:, 0, :, :], src, ALU.mult))
                link(v.tensor_reduce(rng[:, NB * r:NB * r + NB], hit[:, 1, :, :], AX.X, ALU.max))
            v.tensor_copy(rng[:, 0:1], rng[:, 0:1]).then_inc(ssem["range_in"], 1)
            dve.wait_ge(ssem["range_ps"], 2)
            v.tensor_reduce(rng_max[:, 0:1], banks[3][0:2 * NB, 0:P], AX.X, ALU.max).then_inc(ssem["range_in"], 1)
            dve.wait_ge(ssem["range_ps"], 3)
            link(v.tensor_copy(trow[0:1, 0:2, :], banks[4][0:1, 0:2 * NB].rearrange("p (r b) -> p r b", r=2)))
            link(v.tensor_scalar(trow[0:1, 2, :], trow[0:1, 0, :], -1.0, float(T), ALU.mult, ALU.add))
            link(v.tensor_scalar(trow[0:1, 2, :], trow[0:1, 2, :], float(T - BT), None, ALU.min))
            link(v.tensor_tensor(trow[0:1, 3, :], trow[0:1, 1, :], trow[0:1, 2, :], ALU.subtract))

            def finish_table(tab, shift):
                link(v.tensor_scalar(trow[0:1, 3, :], trow[0:1, 3, :], float(2 ** shift - 1), 1.0 * 2 ** shift,
                                     ALU.add, ALU.max))
                link(v.tensor_copy(tri[0:1, :], trow[0:1, 3, :]))
                link(v.tensor_scalar(tab[0:1, 0, :], tri[0:1, :], shift, None, ALU.logical_shift_right))
                link(v.tensor_copy(trow[0:1, 3, :], tab[0:1, 0, :]))
                link(v.tensor_tensor_scan(trow[0:1, 1, :], trow[0:1, 3, :], zrow[0:1, 0:NB], 0.0, ALU.add, ALU.add))
                link(v.tensor_tensor(trow[0:1, 1, :], trow[0:1, 1, :], trow[0:1, 3, :], ALU.subtract))
                link(v.tensor_copy(tab[0:1, 1, :], trow[0:1, 1, :]))
                link(v.tensor_copy(tab[0:1, 2, :], trow[0:1, 2, :]))

            finish_table(tab_i["dst"], 2)
            link(v.memset(pos, 0.0))
            with dve.Fori(0, NB) as b:
                c0 = small[:, 0, ds(b, 1)]
                v.tensor_scalar(eq, blk, blk_id[:, ds(b, 1)], None, ALU.is_equal).then_inc(srt, 1)
                dve.wait_ge(srt, b * 5 + 1)
                v.tensor_tensor_scan(cum, eq, zrow[:, :], 0.0, ALU.add, ALU.add).then_inc(srt, 1)
                dve.wait_ge(srt, b * 5 + 2)
                v.tensor_scalar(c0, cum[:, T - 1:T], 1.0, None, ALU.mult).then_inc(srt, 1)
                dve.wait_ge(srt, b * 5 + 3)
                v.tensor_tensor(cum, cum, eq, ALU.mult).then_inc(srt, 1)
                dve.wait_ge(srt, b * 5 + 4)
                v.tensor_tensor(pos, pos, cum, ALU.add).then_inc(srt, 1)
                dve.wait_ge(srt, b * 5 + 5)
            v.tensor_copy(small[:, 1, :], small[:, 0, :]).then_inc(ssem["cnt"], 1)
            dve.wait_ge(ssem["off"], 1)
            link(v.tensor_copy(small[:, 2, :], banks[0][:, NB:2 * NB]))
            link(v.tensor_tensor_scan(small[:, 3, :], small[:, 2, :], zrow[:, 0:NB], 0.0, ALU.add, ALU.add))
            link(v.tensor_tensor(small[:, 3, :], small[:, 3, :], small[:, 2, :], ALU.subtract))
            link(v.tensor_tensor(small[:, 4, :], small[:, 3, :], banks[0][:, 0:NB], ALU.add))
            link(v.tensor_scalar(small[:, 4, :], small[:, 4, :], -1.0, None, ALU.add))
            link(v.tensor_copy(trow[0:1, 2, :], small[0:1, 3, :]))
            link(v.tensor_copy(trow[0:1, 3, :], small[0:1, 2, :]))
            finish_table(tab_i["src"], 9)
            with dve.Fori(0, NB) as b:
                v.tensor_scalar(eq, blk, blk_id[:, ds(b, 1)], small[:, 4, ds(b, 1)], ALU.is_equal, ALU.mult)\
                    .then_inc(srt, 1)
                dve.wait_ge(srt, b * 2 + (5 * NB + 1))
                v.tensor_tensor(pos, pos, eq, ALU.add).then_inc(srt, 1)
                dve.wait_ge(srt, b * 2 + (5 * NB + 2))
            barrier(dve, "dve")
            link(v.memset(scat_rec[:, :, :, :], 0.0))

            def fill(i, first):
                for h in range(2):
                    if not first:
                        for j in range(8):
                            dve.wait_ge(sc_done[h][j], i * 16)
                    t0 = i * 16 + 8 * h
                    v.tensor_scalar(scat_rec[:, h, :, 2:6], meta[:, ds(t0, 8), 0:4], 1.0, None, ALU.mult)
                    v.tensor_scalar(scat_rec[:, h, :, 0:1].bitcast(I32), meta[:, ds(t0, 8), 4:5], 1.0, None, ALU.mult)
                    v.tensor_scalar(scat_rec[:, h, :, 1], srci[:, ds(t0, 8)], 1.0, None, ALU.mult)
                    v.tensor_scalar(scat_idx[:, h, :], pos[:, ds(t0, 8)], 1.0, None, ALU.mult).then_inc(sc_slot[h], 1)

            def publish(l, between=None):
                q = psem

                def body(u, first):
                    for k in range(U):
                        g = u * U + k
                        dve.wait_ge(q["xT_ps"], NB * l + g + 1)
                        if l == 0:
                            ins = v.tensor_scalar(xs[:, k:k + 1, :], x_all[:, ds(g, 1), :], 1.0, None, ALU.mult)
                        else:
                            dve.wait_ge(q["back"], NB * (l - 1) + g + 1)
                            if l == 1:
                                dve.wait_ge(q["row"], NB * l + g + 1)
                            ins = v.tensor_scalar(xs[:, k:k + 1, :], x_all[:, ds(g, 1), :], small[:, 14, ds(g, 1)],
                                                  small[:, 13, ds(g, 1)], ALU.subtract, ALU.mult)
                        ins.then_inc(q["xs"], 1)
                    for k in range(U):
                        g = u * U + k
                        dve.wait_ge(q["out_ps"], NB * l + g + 1 + U)
                        if not first:
                            dve.wait_ge(q["stored"][k], 16 * (NB // U) * l + u * 16)
                        if l == 1:
                            dve.wait_ge(q["xs"], NB * l + g + 1)
                            row = row_out[:, k, :]
                            v.tensor_scalar(row[:, 32:96], xs[:, k, 0:S], 1.0, None, ALU.mult)
                            v.tensor_scalar(row[:, 160:224], xs[:, k, 0:S], 1.0, None, ALU.mult)
                            v.tensor_scalar(row[:, 0:32], xs[:, k, S + V:S + 2 * V], 1.0, None, ALU.mult)
                            v.tensor_scalar(row[:, 96:128], xs[:, k, S:S + V], 1.0, None, ALU.mult)
                            v.tensor_scalar(row[:, 128:160], xs[:, k, S + 2 * V:D], 1.0, None, ALU.mult)
                        else:
                            v.tensor_scalar(row_out[:, k, 0:D], banks[k][:, 0:D], av[:, ds(g, 1)], None, ALU.mult)
                        v.tensor_scalar(self_all[:, ds(g, 1), :], banks[k][:, D:2 * D].unsqueeze(1), 1.0, None,
                                        ALU.mult).then_inc(q["row"], 1)

                if between is None:
                    rounds(dve, NB // U, body)
                else:
                    rounds(dve, NB // U, lambda u, first: (between(u), body(u, first)))

            def select(l, j, g):
                dve.wait_ge(sems[l]["sel_done"][j], g + R)
                node = meta_slot[:, j, 0:1]
                v.tensor_scalar(sel[:, j, 0, :], node_id[:, :], node, None, ALU.is_equal)\
                    .then_inc(sems[l]["hot_ready"][j], 1)
                for k, c in ((1, 3), (2, 0)):
                    last = v.tensor_scalar(sel[:, j, k, :], node_id[:, :], node, meta_slot[:, j, c + 1:c + 2],
                                           ALU.is_equal, ALU.mult)
                return last

            def bilinear():
                z = bsem
                with dve.Fori(0, NB) as b:
                    def cols(t, c0, n):
                        return t[:, ds(b, 1), c0:c0 + n].rearrange("p o c -> p (o c)")

                    for p in range(4):
                        dve.wait_ge(z["zT_ps"], b * NG + 2 * p + 2)
                        v.tensor_tensor(zs[:, p, :].rearrange("p (u v) -> p u v", v=S),
                                        cols(x_all, 16 * p, 16).unsqueeze(2).broadcast_to([P, 16, S]),
                                        cols(conv_all, 0, S).unsqueeze(1).broadcast_to([P, 16, S]), ALU.mult)\
                            .then_inc(z["z_s"], 1)
                    dve.wait_ge(z["y_ps"], b + 2)
                    for i in range(3):
                        for c in range(4):
                            mul = cols(conv_all if c < 2 else x_all, S + V * i + 16 * (c % 2), 16)
                            last = v.tensor_tensor(
                                tt[:, 512 * c:512 * c + 512].rearrange("p (r w) -> p r w", w=V),
                                banks[4 + c][:, :].rearrange("p (r w) -> p r w", w=V),
                                mul.unsqueeze(2).broadcast_to([P, 16, V]), ALU.mult)
                        last.then_inc(z["y_used"] if i == 2 else bil_own, 1)
                        if i == 2:
                            dve.wait_ge(z["y_used"], b + 2)
                        else:
                            dve.wait_ge(bil_own, b * 7 + 2 * i + 1)
                        v.tensor_reduce(upd[:, 1, S + V * i:S + V * i + V],
                                        tt[:, :].rearrange("p (r w) -> p w r", w=V), AX.X, ALU.add)\
                            .then_inc(bil_own, 1)
                        dve.wait_ge(bil_own, b * 7 + (5 if i == 2 else 2 * i + 2))
                    v.scalar_tensor_tensor(upd[:, 0, :], cols(x_all, 0, D), 2.0, cols(self_all, 0, D), ALU.mult,
                                           ALU.add).then_inc(bil_own, 1)
                    dve.wait_ge(bil_own, b * 7 + 6)
                    dve.wait_ge(z["z_mm"], b * NG + NG + 2)
                    v.tensor_tensor(cols(x_all, S, 3 * V), upd[:, 0, S:D], upd[:, 1, S:D], ALU.add)\
                        .then_inc(bil_own, 1)
                    v.tensor_tensor(cols(x_all, 0, S), upd[:, 0, 0:S], banks[3][:, 0:S], ALU.add)\
                        .then_inc(z["done"], 1)
                    dve.wait_ge(z["done"], b + 2)

            per = (T // 16 - 1) // (NB // U)

            def fills(u):
                with dve.Fori(0, per) as r:
                    fill(u * per + r + 1, False)

            fill(0, True)
            dve.wait_ge(w_in, 16 * (1 + len(w_loads)))
            publish(0, fills)
            for i in range((NB // U) * per + 1, T // 16):
                fill(i, False)
            barrier(dve, "dve")
            for l in range(LAYERS):
                q = sems[l]
                tab = table_of(l)
                if l == 0:
                    link(v.memset(msg[:, :, CNT_COL:MW], 1.0))
                with dve.Fori(0, NB) as b:
                    n = table_reg(dve, tab, 0, b, MAXB)
                    base = table_reg(dve, tab, 1, b, MAXB)
                    start = table_reg(dve, tab, 2, b, NREC)
                    dve.wait_ge(q["prod_ready"][BT - 1], base + R)
                    v.tensor_scalar(node_id[:, :], iota[:, :], blk128[:, ds(b, 1)], None, ALU.add)\
                        .then_inc(asem["node_ids"], 1)
                    dve.wait_ge(asem["node_ids"], NB * l + b + 1)
                    dve.sem_inc(go, 1)
                    with dve.Fori(0, n) as i:
                        g = base + i
                        if l == 1:
                            dve.wait_ge(q["idx_in"], g * 16 + 32)
                            dve.wait_ge(q["act_sel"][BT - 1], g + R)
                            dve.wait_ge(q["prod_ready"][BT - 1], g + R)
                            v.tensor_scalar(meta_slot[:, :, :], rec_slot[:, ds(g % R * BT, BT), 1:6], 1.0, None,
                                            ALU.mult).then_inc(q["meta_ready"], 1)
                            dve.wait_ge(q["meta_ready"], g + R + 1)
                            for j in range(BT):
                                select(l, j, g).then_inc(q["prod_ready"][j], 1)
                        else:
                            dve.wait_ge(q["prod_ready"][BT - 1], g + R)
                            v.tensor_scalar(dst_slot[:, :].unsqueeze(2), meta[:, ds(bounded(start + i * BT, T - 1), BT), 4:5],
                                            1.0, None, ALU.mult).then_inc(q["meta_ready"], 1)
                            dve.wait_ge(q["meta_ready"], g + R)
                            for j in range(BT):
                                dve.wait_ge(q["sel_done"][j], g + R)
                                v.tensor_scalar(hot[:, j, :], node_id[:, :], dst_slot[:, j:j + 1], None, ALU.is_equal)
                                dve.wait_ge(q["got"][j], g * 16 + (GOT0 + 16))
                                dve.wait_ge(q["wsh_ready"][j], g + R + 1)
                                row = gathered[:, ds(g % R, 1), j, 0:D]
                                e0 = row[:, :, 0:S].broadcast_to([P, 4, S])
                                e1 = row[:, :, S:D].rearrange("p o (m c) -> p (o m) c", c=V)
                                out = msg[:, j, 0:CNT_COL]
                                v.tensor_tensor(out[:, 0:4 * S].rearrange("p (k c) -> p k c", c=S),
                                                wsh[:, j, :, 0:S], e0, ALU.mult)
                                v.tensor_tensor(out[:, 4 * S:4 * S + 96].rearrange("p (m c) -> p m c", c=V),
                                                wsh[:, j, 0:1, S:WW].broadcast_to([P, 3, V]), e1, ALU.mult)
                                v.tensor_tensor(out[:, 4 * S + 96:CNT_COL].rearrange("p (m c) -> p m c", c=V),
                                                wsh[:, j, 1:4, S:WW], e1, ALU.mult).then_inc(q["prod_ready"][j], 1)
                barrier(dve, "dve")
                r = nsem
                w = D if l == 1 else 161
                with dve.Fori(0, NB // U) as u:
                    for k in range(U):
                        g = u * U + k
                        dve.wait_ge(r["conv_ps"], NB * l + u * U + conv_end(k, l) + U)
                        o = banks[5][:, 161 * k:161 * k + w] if k < 3 else banks[6][:, 161 * (k - 3):161 * (k - 3) + w]
                        if l == 0:
                            v.tensor_scalar(conv_all[:, ds(g, 1), 161:162],
                                            agg_in[:, k:k + 1, CNT_COL:CNT_COL + 1], 1.0, None, ALU.mult)
                        v.tensor_scalar(conv_all[:, ds(g, 1), 0:w], o.unsqueeze(1), 1.0, None, ALU.mult)\
                            .then_inc(r["conv"], 1)
                sm = lambda c: small[:, c, :]
                if l != 1:
                    dve.wait_ge(r["conv"], NB * (l + 1) + U)
                    gate = conv_all[:, :, 160]
                    if l == 0:
                        link(v.tensor_scalar(sm(2), conv_all[:, :, 161], 1.0, None, ALU.max))
                        link(v.reciprocal(sm(3), sm(2)))
                        link(v.tensor_tensor(sm(3), sm(3), av[:, :], ALU.mult))
                        link(v.tensor_tensor(sm(4), sm(3), sm(3), ALU.mult))
                        link(v.tensor_tensor(sm(1), sm(4), gate, ALU.mult))
                        link(v.tensor_copy(sm(0), av[:, :]))
                    elif l == 2:
                        link(v.scalar_tensor_tensor(sm(2), gate, 0.1, av[:, :], ALU.mult, ALU.mult))
                        link(v.tensor_scalar(sm(3), sm(2), 1 / (2 * math.pi), ROUND, ALU.mult, ALU.add))
                        link(v.tensor_scalar(sm(3), sm(3), -ROUND, None, ALU.add))
                        for part in TWO_PI:
                            link(v.scalar_tensor_tensor(sm(2), sm(3), -part, sm(2), ALU.mult, ALU.add))
                        link(v.tensor_scalar(sm(6), sm(2), 3.1415925, -3.1415925, ALU.min, ALU.max))
                        v.tensor_scalar(sm(7), sm(6), 0.5, None, ALU.mult).then_inc(r["func_in"], 1)
                        dve.wait_ge(r["func_out"], l + 1)
                        link(v.tensor_tensor(sm(1), sm(8), av[:, :], ALU.mult))
                        link(v.tensor_tensor(sm(3), sm(9), sm(9), ALU.mult))
                        link(v.tensor_scalar(sm(3), sm(3), -2.0, 1.0, ALU.mult, ALU.add))
                        link(v.tensor_tensor(sm(0), sm(3), av[:, :], ALU.mult))
                    else:
                        v.tensor_copy(sm(1), av[:, :])
                        link(v.tensor_copy(sm(0), av[:, :]))
                    v.tensor_tensor(self_all[:, :, :], self_all[:, :, :],
                                    sm(0).unsqueeze(2).broadcast_to([P, NB, D]), ALU.mult)
                    link(v.tensor_tensor(conv_all[:, :, 0:D], conv_all[:, :, 0:D],
                                         sm(1).unsqueeze(2).broadcast_to([P, NB, D]), ALU.mult))
                    link(v.tensor_tensor(x_all[:, :, :], x_all[:, :, :], self_all[:, :, :], ALU.add))
                    link(v.tensor_tensor(x_all[:, :, :], x_all[:, :, :], conv_all[:, :, 0:D], ALU.add))
                barrier(dve, "dve")
                if l == 1:
                    bilinear()
                    barrier(dve, "dve")
                with dve.Fori(0, NB // U) as u:
                    for k in range(U):
                        v.bn_stats(stats[:, ds(u * U + k, 1), :], x_all[:, ds(u * U + k, 1), :])\
                            .then_inc(stats_sem, 1)
                dve.wait_ge(stats_sem, NB * (l + 1))
                me, qe, mo, qo = (stats[:, :, c] for c in (1, 2, 4, 5))
                link(v.tensor_tensor(sm(14), me, mo, ALU.add))
                link(v.tensor_scalar(sm(14), sm(14), 0.5, None, ALU.mult))
                link(v.tensor_tensor(sm(10), me, mo, ALU.subtract))
                link(v.scalar_tensor_tensor(sm(10), sm(10), 0.25, sm(10), ALU.mult, ALU.mult))
                link(v.tensor_tensor(sm(11), qe, qo, ALU.add))
                link(v.scalar_tensor_tensor(sm(11), sm(11), 1 / D, sm(10), ALU.mult, ALU.add))
                v.tensor_scalar(sm(11), sm(11), EPS, None, ALU.add).then_inc(r["func_in"], 1)
                dve.wait_ge(r["func_out"], l + 1 + (l >= 2))
                link(v.reciprocal(sm(13), sm(12)))
                if l < LAYERS - 1:
                    publish(l + 1)
                    barrier(dve, "dve")
            with dve.Fori(0, NB // U) as u:
                for k in range(U):
                    g = u * U + k
                    v.tensor_scalar(x_all[:, ds(g, 1), :], x_all[:, ds(g, 1), :], small[:, 14, ds(g, 1)],
                                    small[:, 13, ds(g, 1)], ALU.subtract, ALU.mult).then_inc(final, 1)



def _component_major(x):
    import numpy as np
    n = x.shape[0]
    return np.concatenate([x[:, :S], x[:, S:].reshape(n, V, 3).transpose(0, 2, 1).reshape(n, 3 * V)], axis=1)


def _layout(inputs):
    import numpy as np
    i = {k: np.asarray(a) for k, a in inputs.items()}
    f = np.float32

    def tiles(a, fill):
        a = a.reshape(E, -1)
        p = np.full((EA, a.shape[1]), fill, a.dtype)
        p[:E] = a
        return p.reshape(TA, P, -1).transpose(1, 0, 2).reshape(P, -1)

    def wide(a):
        p = np.zeros((a.shape[1], EA), f)
        p[:, :E] = a.T
        return p

    x = np.zeros((NB * P, D), f)
    x[:N] = _component_major(i["x"])
    a = np.zeros((NB * P,), f)
    a[:N] = i["node_vec1"][:, 0]
    o = {
        "x_in": x, "a_t": a.reshape(NB, P).T,
        "src_t": tiles(i["src"], PAD_SRC), "dst_t": tiles(i["dst"], PAD_DST),
        "attr4_t": tiles(i["edge_attr_4"], 0),
        "a16T": wide(i["edge_attr_16"]), "a8T": wide(i["edge_attr_8"]), "a10T": wide(i["edge_attr_10"]),
        "wu_ss": i["L1_gnn_Wu_ss"].reshape(S * S, S), "wu_vv": i["L1_gnn_Wu_vv"].reshape(V * V, S),
        "wu_sv": i["L1_gnn_Wu_sv"].reshape(S, V * V),
        "wu_vs": i["L1_gnn_Wu_vs"].transpose(1, 0, 2).reshape(S, V * V),
    }
    for k, w in i.items():
        if k.startswith("L") and "Wu_" not in k:
            o[k] = w
    return {k: np.ascontiguousarray(w) for k, w in o.items()}


def kernel(**inputs):
    import numpy as _np
    import concourse.bacc as _bacc
    from concourse import mybir as _mybir
    from concourse.bass_utils import run_bass_kernel_spmd as _run

    nc = _bacc.Bacc("TRN2", target_bir_lowering=False, num_devices=1)
    arrays, args = {}, {}
    for name, a in _layout(inputs).items():
        arrays[f"in_{name}"] = a
        args[name] = nc.dram_tensor(f"in_{name}", a.shape, _mybir.dt.from_np(a.dtype), kind="ExternalInput").ap()
    out = nc.dram_tensor("out_x", (NB * P, D), _mybir.dt.float32, kind="ExternalOutput").ap()
    gnn_kernel(nc, args, out)
    y = _run(nc, [arrays], core_ids=[0]).results[0]["out_x"][:N]
    vec = y[:, S:].reshape(N, 3, V).transpose(0, 2, 1).reshape(N, 3 * V)
    return _np.concatenate([y[:, :S], vec], axis=1)
```
